# Optimizing a Trainium2 kernel written in Bass

```python
import numpy as np
import jax
import jax.numpy as jnp

def _softmax(x, axis=-1):
    return jax.nn.softmax(x, axis=axis)

def _gelu(x):
    return jax.nn.gelu(x, approximate=True)

def _silu(x):
    return jax.nn.silu(x)

def _sigmoid(x):
    return jax.nn.sigmoid(x)

def _layernorm(x, axis=-1, eps=1e-05):
    m = jnp.mean(x, axis=axis, keepdims=True)
    v = jnp.var(x, axis=axis, keepdims=True)
    return (x - m) / jnp.sqrt(v + eps)

def _scatter_add(tgt, idx, src, axis=0):
    return tgt.at[idx].add(src)

def _segment_sum(src, seg, n):
    return jax.ops.segment_sum(src, seg, n)
kernel_name = 'mk_adaln_d1_jaxref_r8_c516b9'

def setup_inputs(seed: int=0):
    np.random.seed(seed)
    _w = jnp.asarray

    def _L0_attn_setup():
        import jax, jax.numpy as jnp
        import numpy as np
        D_MODEL = 256
        D_STATE = 128
        D_CONV = 4
        EXPAND = 2
        HEADDIM = 64
        NGROUPS = 1
        D_INNER = EXPAND * D_MODEL
        NHEADS = D_INNER // HEADDIM
        D_XBC = D_INNER + 2 * NGROUPS * D_STATE
        D_IN_PROJ = 2 * D_INNER + 2 * NGROUPS * D_STATE + NHEADS
        BLOCK_LEN = 64

        def _segsum(x):
            T = x.shape[-1]
            xc = jnp.cumsum(x, axis=-1)
            seg = xc[..., :, None] - xc[..., None, :]
            mask = jnp.tril(jnp.ones((T, T), dtype=bool))
            return jnp.where(mask, seg, -jnp.inf)

        def _ssd_scan(X, A, B, C, block_len):
            b, L, h, p = X.shape
            c = L // block_len
            X = X.reshape(b, c, block_len, h, p)
            A = A.reshape(b, c, block_len, h).transpose(0, 3, 1, 2)
            B = B.reshape(b, c, block_len, h, -1)
            C = C.reshape(b, c, block_len, h, -1)
            A_cumsum = jnp.cumsum(A, axis=-1)
            Lmat = jnp.exp(_segsum(A))
            Y_diag = jnp.einsum('bclhn,bcshn,bhcls,bcshp->bclhp', C, B, Lmat, X)
            decay_states = jnp.exp(A_cumsum[:, :, :, -1:] - A_cumsum)
            states = jnp.einsum('bclhn,bhcl,bclhp->bchpn', B, decay_states, X)
            init = jnp.zeros_like(states[:, :1])
            states = jnp.concatenate([init, states], axis=1)
            A_last = jnp.pad(A_cumsum[:, :, :, -1], ((0, 0), (0, 0), (1, 0)))
            decay_chunk = jnp.exp(_segsum(A_last))
            new_states = jnp.einsum('bhzc,bchpn->bzhpn', decay_chunk, states)
            states = new_states[:, 1:]
            state_decay_out = jnp.exp(A_cumsum)
            Y_off = jnp.einsum('bclhn,bchpn,bhcl->bclhp', C, states, state_decay_out)
            return (Y_diag + Y_off).reshape(b, L, h, p)

        def _forward(x, in_proj_w, conv_w, conv_b, A_log, D, dt_bias, norm_w, out_proj_w):
            Bsz, L, _ = x.shape
            proj = x @ in_proj_w.T
            z = proj[:, :, :D_INNER]
            xBC = proj[:, :, D_INNER:D_INNER + D_XBC]
            dt_raw = proj[:, :, D_INNER + D_XBC:]
            xBC_t = xBC.transpose(0, 2, 1)
            conv = jax.lax.conv_general_dilated(xBC_t, conv_w, window_strides=(1,), padding=[(D_CONV - 1, 0)], feature_group_count=D_XBC, dimension_numbers=('NCH', 'OIH', 'NCH'))
            conv = conv + conv_b[None, :, None]
            xBC = jax.nn.silu(conv).transpose(0, 2, 1)
            x_ssm = xBC[:, :, :D_INNER]
            B_param = xBC[:, :, D_INNER:D_INNER + NGROUPS * D_STATE]
            C_param = xBC[:, :, D_INNER + NGROUPS * D_STATE:]
            dt = jax.nn.softplus(dt_raw + dt_bias)
            A = -jnp.exp(A_log)
            x_heads = x_ssm.reshape(Bsz, L, NHEADS, HEADDIM)
            hpg = NHEADS // NGROUPS
            X = x_heads * dt[..., None]
            A_disc = dt * A[None, None, :]
            B_heads = jnp.repeat(B_param.reshape(Bsz, L, NGROUPS, D_STATE), hpg, axis=2)
            C_heads = jnp.repeat(C_param.reshape(Bsz, L, NGROUPS, D_STATE), hpg, axis=2)
            pad_len = (BLOCK_LEN - L % BLOCK_LEN) % BLOCK_LEN
            if pad_len > 0:
                X = jnp.pad(X, ((0, 0), (0, pad_len), (0, 0), (0, 0)))
                A_disc = jnp.pad(A_disc, ((0, 0), (0, pad_len), (0, 0)))
                B_heads = jnp.pad(B_heads, ((0, 0), (0, pad_len), (0, 0), (0, 0)))
                C_heads = jnp.pad(C_heads, ((0, 0), (0, pad_len), (0, 0), (0, 0)))
            Y = _ssd_scan(X, A_disc, B_heads, C_heads, BLOCK_LEN)[:, :L]
            Y = Y + x_heads * D[None, None, :, None]
            y = Y.reshape(Bsz, L, D_INNER)
            y = y * jax.nn.silu(z)
            rms = jnp.sqrt(jnp.mean(y * y, axis=-1, keepdims=True) + 1e-05)
            y = y / rms * norm_w
            return y @ out_proj_w.T
        key = jax.random.key(seed)
        ks = jax.random.split(key, 8)
        x = jax.random.normal(ks[0], (2, 256, D_MODEL), dtype=jnp.float32)
        in_proj_w = jax.random.normal(ks[1], (D_IN_PROJ, D_MODEL), dtype=jnp.float32) * 0.02
        conv_w = jax.random.normal(ks[2], (D_XBC, 1, D_CONV), dtype=jnp.float32) * 0.2
        conv_b = jnp.zeros((D_XBC,), dtype=jnp.float32)
        A_log = jnp.log(jnp.arange(1, NHEADS + 1, dtype=jnp.float32))
        D = jnp.ones((NHEADS,), dtype=jnp.float32)
        dt_bias = jax.random.normal(ks[3], (NHEADS,), dtype=jnp.float32) * 0.1
        norm_w = jnp.ones((D_INNER,), dtype=jnp.float32)
        out_proj_w = jax.random.normal(ks[4], (D_MODEL, D_INNER), dtype=jnp.float32) * 0.02
        return {'x': x, 'in_proj_w': in_proj_w, 'conv_w': conv_w, 'conv_b': conv_b, 'A_log': A_log, 'D': D, 'dt_bias': dt_bias, 'norm_w': norm_w, 'out_proj_w': out_proj_w}
    _L0_attn_in = _L0_attn_setup()

    def _L0_ffn_setup():
        import jax, jax.numpy as jnp
        import numpy as np
        B, S, D = (4, 256, 256)
        E = 8
        H = 352
        CAP_F = 1.0

        def _moe(x, Wg, W1, W3, W2, sw1, sw3, sw2):
            b, sl, d = x.shape
            T = b * sl
            C = int(CAP_F * T / E)
            xt = x.reshape(T, d)
            probs = jax.nn.softmax(xt @ Wg, axis=-1)
            eidx = jnp.argmax(probs, axis=-1)
            gate = jnp.take_along_axis(probs, eidx[:, None], 1)[:, 0]
            oh = jax.nn.one_hot(eidx, E, dtype=jnp.int32)
            pos = (jnp.cumsum(oh, axis=0) * oh).sum(-1) - 1
            keep = pos < C
            flat = jnp.where(keep, eidx * C + pos, E * C)
            xd = jnp.zeros((E * C, d), x.dtype).at[flat].set(xt, mode='drop')
            xd = xd.reshape(E, C, d)
            h = jax.nn.silu(jnp.einsum('ecd,edh->ech', xd, W1)) * jnp.einsum('ecd,edh->ech', xd, W3)
            oe = jnp.einsum('ech,ehd->ecd', h, W2).reshape(E * C, d)
            out = jnp.take(oe, jnp.minimum(flat, E * C - 1), axis=0)
            out = out * (gate * keep.astype(x.dtype))[:, None]
            shared = jax.nn.silu(xt @ sw1) * (xt @ sw3) @ sw2
            return (out + shared).reshape(b, sl, d)
        key = jax.random.key(seed)
        ks = jax.random.split(key, 8)
        s = lambda fan: 1.0 / np.sqrt(fan)
        return {'x': jax.random.normal(ks[0], (B, S, D), jnp.float32), 'Wg': jax.random.normal(ks[1], (D, E), jnp.float32) * s(D), 'W1': jax.random.normal(ks[2], (E, D, H), jnp.float32) * s(D), 'W3': jax.random.normal(ks[3], (E, D, H), jnp.float32) * s(D), 'W2': jax.random.normal(ks[4], (E, H, D), jnp.float32) * s(H), 'sw1': jax.random.normal(ks[5], (D, H), jnp.float32) * s(D), 'sw3': jax.random.normal(ks[6], (D, H), jnp.float32) * s(D), 'sw2': jax.random.normal(ks[7], (H, D), jnp.float32) * s(H)}
    _L0_ffn_in = _L0_ffn_setup()
    _L0_c = _w((lambda *s: np.random.randn(*s).astype(np.float32) * 0.05)(2, 256))
    _L0_wmod = _w((lambda *s: np.random.randn(*s).astype(np.float32) * 0.05)(256, 6 * 256) * 256 ** (-0.5))
    _d = {'L0_attn_x': _L0_attn_in['x'], 'L0_attn_in_proj_w': _L0_attn_in['in_proj_w'], 'L0_attn_conv_w': _L0_attn_in['conv_w'], 'L0_attn_conv_b': _L0_attn_in['conv_b'], 'L0_attn_A_log': _L0_attn_in['A_log'], 'L0_attn_D': _L0_attn_in['D'], 'L0_attn_dt_bias': _L0_attn_in['dt_bias'], 'L0_attn_norm_w': _L0_attn_in['norm_w'], 'L0_attn_out_proj_w': _L0_attn_in['out_proj_w'], 'L0_ffn_Wg': _L0_ffn_in['Wg'], 'L0_ffn_W1': _L0_ffn_in['W1'], 'L0_ffn_W3': _L0_ffn_in['W3'], 'L0_ffn_W2': _L0_ffn_in['W2'], 'L0_ffn_sw1': _L0_ffn_in['sw1'], 'L0_ffn_sw3': _L0_ffn_in['sw3'], 'L0_ffn_sw2': _L0_ffn_in['sw2'], 'L0_c': _L0_c, 'L0_wmod': _L0_wmod}
    _x0 = _d['L0_attn_x']
    _d['L0_attn_x'] = jax.random.normal(jax.random.fold_in(jax.random.key(seed), 1), (2, 512, 256), dtype=_x0.dtype)
    del _x0
    return _d

def reference(L0_attn_x, L0_attn_in_proj_w, L0_attn_conv_w, L0_attn_conv_b, L0_attn_A_log, L0_attn_D, L0_attn_dt_bias, L0_attn_norm_w, L0_attn_out_proj_w, L0_ffn_Wg, L0_ffn_W1, L0_ffn_W3, L0_ffn_W2, L0_ffn_sw1, L0_ffn_sw3, L0_ffn_sw2, L0_c, L0_wmod):

    def _L0_attn_ref(x, in_proj_w, conv_w, conv_b, A_log, D, dt_bias, norm_w, out_proj_w):
        import jax, jax.numpy as jnp
        import numpy as np
        D_MODEL = 256
        D_STATE = 128
        D_CONV = 4
        EXPAND = 2
        HEADDIM = 64
        NGROUPS = 1
        D_INNER = EXPAND * D_MODEL
        NHEADS = D_INNER // HEADDIM
        D_XBC = D_INNER + 2 * NGROUPS * D_STATE
        D_IN_PROJ = 2 * D_INNER + 2 * NGROUPS * D_STATE + NHEADS
        BLOCK_LEN = 64

        def _segsum(x):
            T = x.shape[-1]
            xc = jnp.cumsum(x, axis=-1)
            seg = xc[..., :, None] - xc[..., None, :]
            mask = jnp.tril(jnp.ones((T, T), dtype=bool))
            return jnp.where(mask, seg, -jnp.inf)

        def _ssd_scan(X, A, B, C, block_len):
            b, L, h, p = X.shape
            c = L // block_len
            X = X.reshape(b, c, block_len, h, p)
            A = A.reshape(b, c, block_len, h).transpose(0, 3, 1, 2)
            B = B.reshape(b, c, block_len, h, -1)
            C = C.reshape(b, c, block_len, h, -1)
            A_cumsum = jnp.cumsum(A, axis=-1)
            Lmat = jnp.exp(_segsum(A))
            Y_diag = jnp.einsum('bclhn,bcshn,bhcls,bcshp->bclhp', C, B, Lmat, X)
            decay_states = jnp.exp(A_cumsum[:, :, :, -1:] - A_cumsum)
            states = jnp.einsum('bclhn,bhcl,bclhp->bchpn', B, decay_states, X)
            init = jnp.zeros_like(states[:, :1])
            states = jnp.concatenate([init, states], axis=1)
            A_last = jnp.pad(A_cumsum[:, :, :, -1], ((0, 0), (0, 0), (1, 0)))
            decay_chunk = jnp.exp(_segsum(A_last))
            new_states = jnp.einsum('bhzc,bchpn->bzhpn', decay_chunk, states)
            states = new_states[:, 1:]
            state_decay_out = jnp.exp(A_cumsum)
            Y_off = jnp.einsum('bclhn,bchpn,bhcl->bclhp', C, states, state_decay_out)
            return (Y_diag + Y_off).reshape(b, L, h, p)

        def _forward(x, in_proj_w, conv_w, conv_b, A_log, D, dt_bias, norm_w, out_proj_w):
            Bsz, L, _ = x.shape
            proj = x @ in_proj_w.T
            z = proj[:, :, :D_INNER]
            xBC = proj[:, :, D_INNER:D_INNER + D_XBC]
            dt_raw = proj[:, :, D_INNER + D_XBC:]
            xBC_t = xBC.transpose(0, 2, 1)
            conv = jax.lax.conv_general_dilated(xBC_t, conv_w, window_strides=(1,), padding=[(D_CONV - 1, 0)], feature_group_count=D_XBC, dimension_numbers=('NCH', 'OIH', 'NCH'))
            conv = conv + conv_b[None, :, None]
            xBC = jax.nn.silu(conv).transpose(0, 2, 1)
            x_ssm = xBC[:, :, :D_INNER]
            B_param = xBC[:, :, D_INNER:D_INNER + NGROUPS * D_STATE]
            C_param = xBC[:, :, D_INNER + NGROUPS * D_STATE:]
            dt = jax.nn.softplus(dt_raw + dt_bias)
            A = -jnp.exp(A_log)
            x_heads = x_ssm.reshape(Bsz, L, NHEADS, HEADDIM)
            hpg = NHEADS // NGROUPS
            X = x_heads * dt[..., None]
            A_disc = dt * A[None, None, :]
            B_heads = jnp.repeat(B_param.reshape(Bsz, L, NGROUPS, D_STATE), hpg, axis=2)
            C_heads = jnp.repeat(C_param.reshape(Bsz, L, NGROUPS, D_STATE), hpg, axis=2)
            pad_len = (BLOCK_LEN - L % BLOCK_LEN) % BLOCK_LEN
            if pad_len > 0:
                X = jnp.pad(X, ((0, 0), (0, pad_len), (0, 0), (0, 0)))
                A_disc = jnp.pad(A_disc, ((0, 0), (0, pad_len), (0, 0)))
                B_heads = jnp.pad(B_heads, ((0, 0), (0, pad_len), (0, 0), (0, 0)))
                C_heads = jnp.pad(C_heads, ((0, 0), (0, pad_len), (0, 0), (0, 0)))
            Y = _ssd_scan(X, A_disc, B_heads, C_heads, BLOCK_LEN)[:, :L]
            Y = Y + x_heads * D[None, None, :, None]
            y = Y.reshape(Bsz, L, D_INNER)
            y = y * jax.nn.silu(z)
            rms = jnp.sqrt(jnp.mean(y * y, axis=-1, keepdims=True) + 1e-05)
            y = y / rms * norm_w
            return y @ out_proj_w.T
        return _forward(x, in_proj_w, conv_w, conv_b, A_log, D, dt_bias, norm_w, out_proj_w)

    def _L0_ffn_ref(x, Wg, W1, W3, W2, sw1, sw3, sw2):
        import jax, jax.numpy as jnp
        import numpy as np
        B, S, D = (4, 256, 256)
        E = 8
        H = 352
        CAP_F = 1.0

        def _moe(x, Wg, W1, W3, W2, sw1, sw3, sw2):
            b, sl, d = x.shape
            T = b * sl
            C = int(CAP_F * T / E)
            xt = x.reshape(T, d)
            probs = jax.nn.softmax(xt @ Wg, axis=-1)
            eidx = jnp.argmax(probs, axis=-1)
            gate = jnp.take_along_axis(probs, eidx[:, None], 1)[:, 0]
            oh = jax.nn.one_hot(eidx, E, dtype=jnp.int32)
            pos = (jnp.cumsum(oh, axis=0) * oh).sum(-1) - 1
            keep = pos < C
            flat = jnp.where(keep, eidx * C + pos, E * C)
            xd = jnp.zeros((E * C, d), x.dtype).at[flat].set(xt, mode='drop')
            xd = xd.reshape(E, C, d)
            h = jax.nn.silu(jnp.einsum('ecd,edh->ech', xd, W1)) * jnp.einsum('ecd,edh->ech', xd, W3)
            oe = jnp.einsum('ech,ehd->ecd', h, W2).reshape(E * C, d)
            out = jnp.take(oe, jnp.minimum(flat, E * C - 1), axis=0)
            out = out * (gate * keep.astype(x.dtype))[:, None]
            shared = jax.nn.silu(xt @ sw1) * (xt @ sw3) @ sw2
            return (out + shared).reshape(b, sl, d)
        return _moe(x, Wg, W1, W3, W2, sw1, sw3, sw2)
    x = L0_attn_x
    mod = (_silu(L0_c) @ L0_wmod).reshape(L0_c.shape[0], 6, 1, -1)
    sa, ca, ga, sb, cb, gb = (mod[:, 0], mod[:, 1], mod[:, 2], mod[:, 3], mod[:, 4], mod[:, 5])
    ga = (2 * (ga >= 0) - 1) * jnp.maximum(jnp.abs(ga), 0.25)
    gb = (2 * (gb >= 0) - 1) * jnp.maximum(jnp.abs(gb), 0.25)
    h = _layernorm(x, axis=-1) * (1 + ca) + sa
    x = x + ga * _L0_attn_ref(h, L0_attn_in_proj_w, L0_attn_conv_w, L0_attn_conv_b, L0_attn_A_log, L0_attn_D, L0_attn_dt_bias, L0_attn_norm_w, L0_attn_out_proj_w)
    h = _layernorm(x, axis=-1) * (1 + cb) + sb
    x = x + gb * _L0_ffn_ref(h, L0_ffn_Wg, L0_ffn_W1, L0_ffn_W3, L0_ffn_W2, L0_ffn_sw1, L0_ffn_sw3, L0_ffn_sw2)
    return x

_drawn_inputs = setup_inputs


def setup_inputs(seed=0):
    import zlib

    import numpy as np

    out = dict(_drawn_inputs(seed))
    spreads = {'L0_attn_conv_b': (0.0, 0.1), 'L0_attn_D': (1.0, 0.6), 'L0_attn_norm_w': (1.0, 0.6)}
    factors = {'L0_attn_A_log': 8.0, 'L0_attn_dt_bias': 8.0}
    for name, (base, spread) in spreads.items():
        noise = np.random.default_rng([zlib.crc32(name.encode()), seed]).standard_normal(out[name].shape)
        drawn = base * np.exp(spread * noise) if base else spread * noise
        out[name] = jnp.asarray(drawn.astype(out[name].dtype))
    for name, factor in factors.items():
        out[name] = (out[name] * factor).astype(out[name].dtype)
    return out
```

```python
from contextlib import ExitStack

import concourse.bass as bass
from concourse import mybir

P = 128
D = 256
KD = D // P
NB = 2
L = 512
NT = NB * L // P
TB = L // P
DI = 512
MD = DI // P
NH = 8
HD = DI // NH
NS = 128
TAPS = 4
MC = MD + 2
DPROJ = 2 * DI + 2 * NS + NH
NE = 8
EB = 4
CAP = NB * L // NE
HID = 352
JH = 3
HJ = [0, P, HID - P]
DUP = HJ[1] + P - HJ[2]
EPS = 1e-5

C_CW = 0
C_CB = C_CW + MC * TAPS
C_NW = C_CB + MC
C_D = C_NW + MD
C_AL = C_D + MD
C_DB = C_AL + NH
C_C = C_DB + NH
C_WG = C_C + KD * NB
NPACK = C_WG + KD * NE

SA, CA, GA, SB, CB, GB = range(6)


def build(nc, x, in_w, out_w, pack, wmod, w1, w3, w2, sw1, sw3, sw2, out):
    f32, bf16, i32 = mybir.dt.float32, mybir.dt.bfloat16, mybir.dt.int32
    ALU, ACT, AX = mybir.AluOpType, mybir.ActivationFunctionType, mybir.AxisListType

    mod_rows = nc.dram_tensor("mod_rows", (6 * NB * KD, P), f32, kind="Internal").ap()
    xd = nc.dram_tensor("xd", (NE * CAP + NB * L, D), f32, kind="Internal").ap()
    oe = nc.dram_tensor("oe", (NE * CAP, D), f32, kind="Internal").ap()

    with ExitStack() as ctx:
        def sb(name, shape, dt=f32):
            return ctx.enter_context(nc.sbuf_tensor(name, shape, dt))

        def sem(name):
            return ctx.enter_context(nc.semaphore(name))

        ident = sb("ident", [P, P])
        le = sb("le", [P, P])
        gt = sb("gt", [P, P])
        ones = sb("ones", [P, P])
        le_b = sb("le_b", [P, P], bf16)
        ones_b = sb("ones_b", [P, P], bf16)
        neg_half = sb("neg_half", [P, NH])
        euler = sb("euler", [P, NT * NH])
        rank = sb("rank", [P, TB, NE])
        slot0 = sb("slot0", [P, TB, NE])
        spill = sb("spill", [P, NT])
        zero = sb("zero", [P, D])
        pk = sb("pk", [P, NPACK])
        xs = sb("xs", [P, NT, D])
        wm = sb("wm", [P, KD, 6 * D])
        win = sb("win", [P, KD, DPROJ])
        wo = sb("wo", [P, MD, D])
        shw1 = sb("shw1", [P, KD, HID])
        shw3 = sb("shw3", [P, KD, HID])
        shw2 = sb("shw2", [P, JH, D])
        ew1 = sb("ew1", [P, EB, KD, HID])
        ew3 = sb("ew3", [P, EB, KD, HID])
        ew2 = sb("ew2", [P, EB, JH, D])
        sc = sb("sc", [P, KD * NB])
        mcol = sb("mcol", [P, 6 * NB * KD])
        msgn = sb("msgn", [P, 2, NB * KD])
        mabs = sb("mabs", [P, 2, NB * KD])
        mrow_sb = sb("mrow_sb", [6 * NB * KD, P])
        mrow = sb("mrow", [P, 4, NB, D])
        wog = sb("wog", [P, NB, MD, D])
        shw2g = sb("shw2g", [P, NB, JH, D])
        stats = sb("stats", [P, 6])
        stats2 = sb("stats2", [P, 6])
        mv = sb("mv", [P, NT, 2])
        ve = sb("ve", [P, NT])
        rstd = sb("rstd", [P, NT])
        mv2 = sb("mv2", [P, NT, 2])
        ve2 = sb("ve2", [P, NT])
        rstd2 = sb("rstd2", [P, NT])
        xn = sb("xn", [P, NT, D])
        h2 = xn
        cent = sb("cent", [P, D])
        hT = sb("hT", [P, KD, NB * L])
        acc = sb("acc", [P, 3, L])
        xcT = sb("xcT", [P, MC, NB * L])
        zs = sb("zs", [P, MD, NB * L])
        NDT = NT * NH
        v = sb("v", [P, NDT])
        nabs = sb("nabs", [P, NDT])
        en = sb("en", [P, NDT])
        zz = sb("zz", [P, NDT])
        z2 = sb("z2", [P, NDT])
        pp = sb("pp", [P, NDT])
        dt = sb("dt", [P, NT, NH])
        expa = sb("expa", [P, NH])
        a = sb("a", [P, NT, NH])
        dec = sb("dec", [P, NB, 3, TB, NH])
        wm_flat = wm[:, :, :].rearrange("p k n -> p (k n)")
        win_flat = win[:, :, :].rearrange("p k n -> p (k n)")
        al = sb("al", [P, 2, NH, P])
        lm = wm_flat[:, 0:2 * NH * P].rearrange("p (q h l) -> p q h l", q=2, h=NH)
        btok = sb("btok", [P, 2, NS])
        gm = sb("gm", [P, 2, P])
        xdt = wm_flat[:, 2 * NH * P:2 * NH * P + 2 * DI].rearrange("p (q n) -> p q n", q=2)
        xdd = win_flat[:, 0:2 * DI].rearrange("p (q n) -> p q n", q=2)
        st = sb("st", [P, 2, DI])
        stdec = sb("stdec", [P, DI])
        y = win_flat[:, 2 * DI:4 * DI].rearrange("p (q n) -> p q n", q=2)
        yoff = win_flat[:, 4 * DI:5 * DI]
        ydx = sb("ydx", [P, 2, MD, P])
        yg = sb("yg", [P, 2, MD, P])
        sq = sb("sq", [P, 2, MD, P])
        rv = sb("rv", [P, NT])
        rr = sb("rr", [P, NT])
        h2T = hT
        mx = sb("mx", [P, NT])
        sh = sb("sh", [P, NT, NE])
        cand = sb("cand", [P, NT, NE])
        best = sb("best", [P, NT])
        oh = sb("oh", [P, NT, NE], bf16)
        pre = sb("pre", [P, NT, NE], bf16)
        offs = sb("offs", [P, NT, NE])
        off = sb("off", [P, NT])
        cnts = sb("cnts", [P, NT, NE])
        cnt = sb("cnt", [P, NT])
        keep = sb("keep", [P, NT])
        flat = sb("flat", [P, NT])
        dlt = sb("dlt", [P, NT])
        dest = sb("dest", [P, NT], i32)
        src = sb("src", [P, NT], i32)
        ex = sb("ex", [P, NT, NE])
        es = sb("es", [P, NT])
        gate = sb("gate", [P, NT])
        sg = acc
        shact = wm_flat.rearrange("p (j n) -> p j n", j=JH)
        eact = sb("eact", [P, 2, JH, P])
        xg = zs[:, 0:2, :].rearrange("p m (e d) -> p (m e) d", d=D)
        xdT = sb("xdT", [P, 2, KD, P])
        oes = zs[:, 2:4, :].rearrange("p m (e d) -> p (m e) d", d=D)
        gath = xcT[:, 0:2, :].rearrange("p m (t d) -> p (m t) d", d=D)
        res = xcT[:, 2:4, :].rearrange("p m (t d) -> p (m t) d", d=D)

        seg_ps = ctx.enter_context(nc.psum_tensor("seg_ps", [P, 2, 512], f32))
        bank = [seg_ps[:, 0, :], seg_ps[:, 1, :]]
        for i in range(2, 8):
            bank.append(ctx.enter_context(nc.psum_tensor(f"bank{i}", [P, 512], f32))[:, :])
        XY, BG, YD, YOFF, ST, MISC = 2, 3, 4, 5, 6, 7
        proj_bank = [2, 3, 4, 5]
        mc_ps = bank[6][:, 0:24]
        mt_ps = bank[6][0:24, 128:256]
        dt_ps = bank[7][:, 0:NDT]
        out_ps = bank[MISC][:, 0:D]
        small_ps = bank[ST][:, 0:3 * TB * NH]
        ssq_ps = bank[MISC][:, 352:352 + NT]
        lg_ps = bank[MISC][:, 360:360 + NT * NE]
        pos_ps = bank[MISC][:, 424:424 + NT * NE]
        b_ps = bank[BG][:, 0:P]
        g_ps = bank[BG][:, P:2 * P]
        h2T_ps = bank[BG][:, 2 * P:4 * P]
        up_bank = [(0, 1), (5, 6)]
        down_bank = [3, 4]
        xdT_bank = [XY, MISC]
        sd_bank = [0, 1, 5, 6]

        s_pack, s_x = sem("pack_in"), [sem("x0_in"), sem("x1_in")]
        s_wma, s_wmb = sem("wmod_a_in"), sem("wmod_b_in")
        s_winx, s_winz = sem("winx_in"), sem("winz_in")
        s_wo, s_shw, s_sh2 = sem("wo_in"), sem("shared_up_in"), sem("shared_down_in")
        s_ew = [sem(f"expert{e}_in") for e in range(NE)]
        s_rowout, s_rowin = sem("mod_rows_out"), sem("mod_rows_in")
        s_zeroed, s_scat, s_xg = sem("xd_zeroed"), sem("scattered"), sem("slots_in")
        s_oeout, s_gath, s_out = sem("expert_out"), [sem(f"gathered{t}") for t in range(NT)], sem("stored")
        s_pc, s_const = sem("pool_chain"), sem("constants")
        s_rstd, s_expa, s_en = sem("rstd"), sem("exp_a"), sem("exp_neg")
        s_al, s_xdd, s_sdec, s_yg = sem("a_masked"), sem("x_decayed"), sem("state_decayed"), sem("y_gated")
        s_rr, s_rstd2, s_shg, s_pad = sem("rrms"), sem("rstd2"), sem("shared_gated"), sem("w2_pads")
        s_sc, s_hT, s_tap, s_xc, s_zs = sem("silu_c"), sem("hT"), sem("first_tap"), sem("conv_silu"), sem("z_silu")
        s_mrow, s_dec, s_l, s_btok = sem("mod_rows_sb"), sem("decays"), sem("decay_matrix"), sem("b_tokens")
        s_y0, s_st0, s_sq, s_h2T = sem("y_first"), sem("state_first"), sem("y_squared"), sem("h2T")
        s_sg, s_xdT, s_ex = sem("up_silu"), sem("slots_T"), sem("gate_exp")
        s_vc = sem("vector_chain")
        s_ve, s_xn, s_mcol, s_conv = sem("variance"), sem("x_normed"), sem("mod_cols"), sem("conv_done")
        s_nabs, s_dt, s_wog = sem("neg_abs"), sem("time_steps"), sem("wo_gated")
        s_m, s_xdt, s_gm = sem("m_matrix"), sem("x_dt"), sem("g_masked")
        s_yoffe, s_y, s_st = sem("yoff_scaled"), sem("y_rest"), sem("state_rest")
        s_ydx, s_rv, s_x1, s_ve2, s_h2 = sem("y_plus_dx"), sem("mean_square"), sem("x1"), sem("variance2"), sem("h2_rows")
        s_sh, s_oh, s_dest, s_gate = sem("logits_shifted"), sem("one_hot"), sem("slots"), sem("gates")
        s_act, s_oes, s_fin = sem("up_act"), sem("expert_rows"), sem("final_rows")
        p_mc, p_mt, p_hT, p_dt, p_proj = sem("p_mod_cols"), sem("p_mod_rows"), sem("p_hT"), sem("p_dt"), sem("p_proj")
        p_small, p_xtok, p_bg, p_seg = sem("p_small"), sem("p_x_tokens"), sem("p_b_g"), sem("p_seg")
        p_yd, p_yoff, p_st, p_yT, p_out = sem("p_y_diag"), sem("p_y_off"), sem("p_state"), sem("p_yT"), sem("p_out")
        p_h2T, p_lg, p_pos = sem("p_h2T"), sem("p_logits"), sem("p_positions")
        p_up, p_xdT, p_dn, p_sd = sem("p_up"), sem("p_slots_T"), sem("p_down"), sem("p_shared_down")

        block = ctx.enter_context(nc.Block())

        def tok(c):
            return slice(c * P, (c + 1) * P)

        def seq(b):
            return slice(b * L, (b + 1) * L)

        def yoffs_before(c):
            return c + 1 - c // TB - 1

        def states_before(c):
            return c + 1 - (c + 1) // TB

        def rest_before(c):
            return 2 * (c // TB) + min(max(c % TB, 0), 2)

        UPS = [("shared", b, j) for b in range(NB) for j in range(JH)] + [("expert", e, 0) for e in range(NE)]
        NSH = NB * JH

        @block.sync
        def _(sp):
            sp.dma_start(pk[:, :], pack).then_inc(s_pack, 16)
            xv = x.rearrange("b (t p) d -> p (b t) d", p=P)
            wmv = wmod.rearrange("(k p) n -> p k n", p=P)
            wiv = in_w.rearrange("(k p) n -> p k n", p=P)
            sp.dma_start(xs[:, 0:TB, :], xv[:, 0:TB, :]).then_inc(s_x[0], 16)
            sp.dma_start(wm[:, :, 0:2 * D], wmv[:, :, 0:2 * D]).then_inc(s_wma, 16)
            sp.dma_start(win[:, :, DI:DPROJ], wiv[:, :, DI:DPROJ]).then_inc(s_winx, 16)
            sp.dma_start(xs[:, TB:NT, :], xv[:, TB:NT, :]).then_inc(s_x[1], 16)
            sp.dma_start(wm[:, :, 2 * D:6 * D], wmv[:, :, 2 * D:6 * D]).then_inc(s_wmb, 16)
            sp.dma_start(win[:, :, 0:DI], wiv[:, :, 0:DI]).then_inc(s_winz, 16)
            sp.dma_start(wo[:, :, :], out_w.rearrange("(m p) n -> p m n", p=P)).then_inc(s_wo, 16)
            sp.wait_ge(s_mrow, 1)
            sp.dma_start(mod_rows, mrow_sb[:, :]).then_inc(s_rowout, 16)
            sp.dma_start(shw1[:, :, :], sw1.rearrange("(k p) n -> p k n", p=P)).then_inc(s_shw, 16)
            sp.dma_start(shw3[:, :, :], sw3.rearrange("(k p) n -> p k n", p=P)).then_inc(s_shw, 16)
            sp.wait_ge(s_rowout, 16)
            sp.dma_start(mrow[:, :, :, :].rearrange("p a b d -> p (a b d)"),
                         mod_rows[GA * NB * KD:6 * NB * KD, :].rearrange("r n -> (r n)")
                         .partition_broadcast(P)).then_inc(s_rowin, 16)
            sp.dma_start(shw2[:, 0:2, :], sw2[0:2 * P, :].rearrange("(j p) n -> p j n", p=P)).then_inc(s_sh2, 16)
            sp.dma_start(shw2[DUP:P, 2, :], sw2[2 * P:HID, :]).then_inc(s_sh2, 16)
            sp.wait_ge(s_const, 1)
            for e in range(NE):
                sp.dma_start(xd[e * CAP:(e + 1) * CAP, :], zero[:, :]).then_inc(s_zeroed, 16)
            sp.wait_ge(s_pad, 1)
            def load_expert(e):
                q = e % EB
                if e >= EB:
                    sp.wait_ge(p_dn, e - EB + 1)
                sp.dma_start(ew1[:, q, :, :], w1[e].rearrange("(k p) n -> p k n", p=P)).then_inc(s_ew[e], 16)
                sp.dma_start(ew3[:, q, :, :], w3[e].rearrange("(k p) n -> p k n", p=P)).then_inc(s_ew[e], 16)
                sp.dma_start(ew2[:, q, 0:2, :], w2[e, 0:2 * P, :].rearrange("(j p) n -> p j n", p=P)).then_inc(s_ew[e], 16)
                sp.dma_start(ew2[DUP:P, q, 2, :], w2[e, 2 * P:HID, :]).then_inc(s_ew[e], 16)
            for e in range(EB):
                load_expert(e)
            sp.wait_ge(s_scat, 16 * NT)
            for q in range(2):
                sp.dma_start(xg[:, 4 * q:4 * q + 4, :],
                             xd[4 * q * CAP:(4 * q + 4) * CAP, :].rearrange("(e p) d -> p e d", p=P)).then_inc(s_xg, 16)
                sp.wait_ge(s_xg, 16 * (q + 1))
            for e in range(NE):
                if e + EB < NE:
                    load_expert(e + EB)
                sp.wait_ge(s_oes, e + 1)
                sp.dma_start(oe[e * CAP:(e + 1) * CAP, :], oes[:, e, :]).then_inc(s_oeout, 16)
            ov = out.rearrange("b (t p) d -> (b t) p d", p=P)
            for t in range(NT):
                sp.wait_ge(s_fin, t + 1)
                sp.dma_start(ov[t], res[:, t, :]).then_inc(s_out, 16)
            sp.wait_ge(s_out, 16 * NT)

        @block.gpsimd
        def _(pool):
            chained = [0]

            def then_wait(ins):
                chained[0] += 1
                ins.then_inc(s_pc, 1)
                pool.wait_ge(s_pc, chained[0])

            pool.memset(zero[:, :], 0.0)
            pool.memset(neg_half[:, :], -0.5)
            pool.memset(euler[:, :], 2.718281828459045)
            pool.memset(ones_b[:, :], 1.0)
            pool.memset(ones[:, :], 1.0)
            then_wait(pool.memset(ident[:, :], 0.0))
            pool.affine_select(out=ident[:, :], in_=ident[:, :], compare_op=ALU.not_equal, fill=1.0,
                               base=0, pattern=[[-1, P]], channel_multiplier=1)
            pool.affine_select(out=le[:, :], in_=ones[:, :], compare_op=ALU.is_ge, fill=0.0,
                               base=0, pattern=[[1, P]], channel_multiplier=-1)
            pool.affine_select(out=le_b[:, :], in_=ones[:, :], compare_op=ALU.is_ge, fill=0.0,
                               base=0, pattern=[[1, P]], channel_multiplier=-1)
            pool.affine_select(out=gt[:, :], in_=ones[:, :], compare_op=ALU.is_gt, fill=0.0,
                               base=0, pattern=[[-1, P]], channel_multiplier=1)
            pool.iota(rank[:, :, :], pattern=[[0, TB], [-1, NE]], base=NE, channel_multiplier=0,
                      allow_small_or_imprecise_dtypes=True)
            pool.iota(slot0[:, :, :], pattern=[[0, TB], [CAP, NE]], base=-1, channel_multiplier=0,
                      allow_small_or_imprecise_dtypes=True)
            pool.iota(spill[:, :], pattern=[[P, NT]], base=NE * CAP, channel_multiplier=1,
                      allow_small_or_imprecise_dtypes=True).then_inc(s_const, 1)

            for b in range(NB):
                pool.wait_ge(s_ve, b + 1)
                bt = slice(b * TB, (b + 1) * TB)
                pool.tensor_tensor(rstd[:, bt], ve[:, bt], neg_half[:, 0:TB], ALU.pow).then_inc(s_rstd, 1)
            pool.wait_ge(s_pack, 16)
            pool.tensor_tensor(expa[:, :], euler[:, 0:NH], pk[:, C_AL:C_AL + NH], ALU.pow).then_inc(s_expa, 1)
            pool.wait_ge(s_nabs, 1)
            pool.tensor_tensor(en[:, :], euler[:, :], nabs[:, :], ALU.pow).then_inc(s_en, 1)
            pool.memset(shw2[0:DUP, 2, :], 0.0)
            pool.memset(ew2[0:DUP, :, 2, :], 0.0).then_inc(s_pad, 1)

            def masked_a(c):
                if c >= 2:
                    pool.wait_ge(p_seg, c - 1)
                pool.tensor_tensor(al[:, c % 2, :, :], le[:, :].unsqueeze(1).to_broadcast([P, NH, P]),
                                   a[:, c, :].unsqueeze(2).to_broadcast([P, NH, P]), ALU.mult).then_inc(s_al, 1)

            def rest_decay(c):
                pool.wait_ge(s_xdt, c + 1)
                pool.wait_ge(s_dec, c // TB + 1)
                if c >= 2:
                    pool.wait_ge(p_st, states_before(c - 2))
                pool.tensor_tensor(xdd[:, c % 2, :].rearrange("p (h d) -> p h d", h=NH),
                                   xdt[:, c % 2, :].rearrange("p (h d) -> p h d", h=NH),
                                   dec[:, c // TB, 1, c % TB, :].unsqueeze(2).to_broadcast([P, NH, HD]),
                                   ALU.mult).then_inc(s_xdd, 1)

            def decayed_state(c):
                if c % TB == 1:
                    pool.wait_ge(s_st0, c // TB + 1)
                else:
                    pool.wait_ge(s_st, rest_before(c - 1))
                if rest_before(c) > 1:
                    pool.wait_ge(s_st, rest_before(c) - 1)
                pool.tensor_tensor(stdec[:, :].rearrange("p (h d) -> p h d", h=NH),
                                   st[:, (c - 1) % 2, :].rearrange("p (h d) -> p h d", h=NH),
                                   dec[:, c // TB, 2, c % TB, :].unsqueeze(2).to_broadcast([P, NH, HD]),
                                   ALU.mult).then_inc(s_sdec, 1)

            def gated(c):
                pool.wait_ge(s_ydx, c + 1)
                pool.wait_ge(s_zs, MD * (c // TB + 1))
                if c >= 2:
                    pool.wait_ge(p_out, c - 1)
                pool.tensor_tensor(yg[:, c % 2, :, :], ydx[:, c % 2, :, :], zs[:, :, tok(c)], ALU.mult).then_inc(s_yg, 1)

            pool.wait_ge(s_dt, 1)
            pool.wait_ge(s_expa, 1)
            masked_a(0)
            masked_a(1)
            pool.wait_ge(s_rowin, 16)
            pool.wait_ge(s_sh2, 32)
            pool.wait_ge(s_pad, 1)
            for b in range(NB):
                pool.tensor_tensor(shw2g[:, b, :, :], shw2[:, :, :],
                                   mrow[:, GB - GA, b, :].unsqueeze(1).to_broadcast([P, JH, D]),
                                   ALU.mult).then_inc(s_shg, 1)
            rest_decay(0)

            def rrms(c):
                pool.wait_ge(s_rv, c + 1)
                pool.tensor_tensor(rr[:, c:c + 1], rv[:, c:c + 1], neg_half[:, 0:1], ALU.pow).then_inc(s_rr, 1)

            def norm2(c):
                pool.wait_ge(s_ve2, c + 1)
                pool.tensor_tensor(rstd2[:, c:c + 1], ve2[:, c:c + 1], neg_half[:, 0:1], ALU.pow).then_inc(s_rstd2, 1)

            def scatter(b):
                pool.wait_ge(s_dest, b + 1)
                pool.wait_ge(s_zeroed, 16 * NE)
                for t in range(b * TB, (b + 1) * TB):
                    pool.indirect_dma_start(out=xd, out_offset=bass.IndirectOffsetOnAxis(ap=dest[:, t:t + 1], axis=0),
                                            in_=h2[:, t, :], in_offset=None).then_inc(s_scat, 16)

            for c in range(NT + 3):
                if c + 1 < NT and (c + 1) % TB != TB - 1:
                    rest_decay(c + 1)
                if c < NT and c % TB in (1, 2):
                    decayed_state(c)
                if 0 <= c - 2 < NT:
                    rrms(c - 2)
                    norm2(c - 2)
                if c + 2 < NT:
                    masked_a(c + 2)
                if 0 <= c - 1 < NT:
                    gated(c - 1)
                if c == NT + 1:
                    scatter(0)
            scatter(1)
            pool.wait_ge(s_oeout, 16 * NE)
            for t in range(NT):
                pool.indirect_dma_start(out=gath[:, t, :], out_offset=None, in_=oe,
                                        in_offset=bass.IndirectOffsetOnAxis(ap=src[:, t:t + 1], axis=0)).then_inc(s_gath[t], 16)

        @block.scalar
        def _(act):
            act.wait_ge(s_pack, 16)
            act.activation(sc[:, :], pk[:, C_C:C_C + KD * NB], ACT.Silu).then_inc(s_sc, 1)
            act.wait_ge(s_mcol, 1)

            def hT_out(b):
                for k in range(KD):
                    act.wait_ge(p_hT, KD * b + k + 1)
                    act.activation(hT[:, k, seq(b)], bank[k], ACT.Identity,
                                   bias=mcol[:, (SA * NB + b) * KD + k:(SA * NB + b) * KD + k + 1],
                                   scale=mcol[:, (CA * NB + b) * KD + k:(CA * NB + b) * KD + k + 1]).then_inc(s_hT, 1)

            def first_tap(b, m):
                n, i = b * (MC + MD) + m, b * MC + m
                act.wait_ge(p_proj, n + 1)
                if i >= 3:
                    act.wait_ge(s_xc, i - 2)
                act.activation(acc[:, i % 3, :], bank[proj_bank[n % 4]], ACT.Identity,
                               bias=pk[:, C_CB + m:C_CB + m + 1],
                               scale=pk[:, C_CW + m * TAPS + TAPS - 1:C_CW + m * TAPS + TAPS]).then_inc(s_tap, 1)

            def conv_silu(b, m):
                i = b * MC + m
                act.wait_ge(s_conv, i + 1)
                act.activation(xcT[:, m, seq(b)], acc[:, i % 3, :], ACT.Silu).then_inc(s_xc, 1)

            def z_silu(b, m):
                n = b * (MC + MD) + MC + m
                act.wait_ge(p_proj, n + 1)
                act.activation(zs[:, m, seq(b)], bank[proj_bank[n % 4]], ACT.Silu).then_inc(s_zs, 1)

            hT_out(0)
            for b in range(NB):
                first_tap(b, 0)
                first_tap(b, 1)
                if b == 0:
                    hT_out(1)
                for m in range(2, MC):
                    conv_silu(b, m - 2)
                    first_tap(b, m)
                if b == 0:
                    act.wait_ge(p_mt, 1)
                    act.activation(mrow_sb[:, :], mt_ps, ACT.Copy).then_inc(s_mrow, 1)
                conv_silu(b, MC - 2)
                z_silu(b, 0)
                conv_silu(b, MC - 1)
                for m in range(1, MD):
                    z_silu(b, m)

            def decays(b):
                act.wait_ge(p_small, b + 1)
                act.activation(dec[:, b, :, :, :].rearrange("p q t h -> p (q t h)"), small_ps, ACT.Exp).then_inc(s_dec, 1)

            def decay_matrix(c):
                act.wait_ge(p_seg, c + 1)
                if c >= 2:
                    act.wait_ge(p_yd, c - 1)
                act.activation(lm[:, c % 2, :, :].rearrange("p h l -> p (h l)"),
                               seg_ps[:, :, :].rearrange("p g n -> p (g n)"), ACT.Exp).then_inc(s_l, 1)

            def b_tokens(c):
                act.wait_ge(p_bg, c + 1)
                if c >= 2:
                    act.wait_ge(p_st, states_before(c - 2))
                act.activation(btok[:, c % 2, :], b_ps, ACT.Copy).then_inc(s_btok, 1)

            decays(0)
            b_tokens(0)
            decay_matrix(0)
            for c in range(NT + 4):
                if c < NT and c % TB == 0:
                    act.wait_ge(p_yd, c + 1)
                    if c >= 2:
                        act.wait_ge(p_yT, c - 1)
                    act.activation(y[:, c % 2, :], bank[YD], ACT.Copy).then_inc(s_y0, 1)
                    act.wait_ge(p_st, states_before(c))
                    act.activation(st[:, c % 2, :], bank[ST], ACT.Copy).then_inc(s_st0, 1)
                if c + 1 < NT:
                    if (c + 1) % TB == 0:
                        decays((c + 1) // TB)
                    b_tokens(c + 1)
                    decay_matrix(c + 1)
                if 0 <= c - 1 < NT:
                    act.wait_ge(s_yg, c)
                    if c - 1 >= 2:
                        act.wait_ge(p_out, c - 2)
                    act.activation(sq[:, (c - 1) % 2, :, :].rearrange("p m n -> p (m n)"),
                                   yg[:, (c - 1) % 2, :, :].rearrange("p m n -> p (m n)"), ACT.Square).then_inc(s_sq, 1)
                if 0 <= c - 3 < NT:
                    t = c - 3
                    act.wait_ge(p_h2T, t + 1)
                    act.activation(h2T[:, :, tok(t)], h2T_ps.rearrange("p (k n) -> p k n", k=KD), ACT.Copy).then_inc(s_h2T, 1)

            def up_silu(u):
                kind, e, j = UPS[u]
                act.wait_ge(p_up, u + 1)
                if u >= 2:
                    act.wait_ge(s_act, u - 1)
                n = L if kind == "shared" else JH * P
                act.activation(sg[:, u % 2, 0:n], bank[up_bank[u % 2][0]][:, 0:n], ACT.Silu).then_inc(s_sg, 1)

            def slots_T(e):
                act.wait_ge(p_xdT, e + 1)
                if e >= 2:
                    act.wait_ge(p_up, NSH + e - 1)
                act.activation(xdT[:, e % 2, :, :].rearrange("p k n -> p (k n)"),
                               bank[xdT_bank[e % 2]][:, 0:KD * P], ACT.Copy).then_inc(s_xdT, 1)

            for u in range(NSH):
                up_silu(u)
            slots_T(0)
            for e in range(NE):
                if e + 1 < NE:
                    slots_T(e + 1)
                up_silu(NSH + e)
            act.wait_ge(s_sh, NB)
            act.activation(ex[:, :, :].rearrange("p t e -> p (t e)"), sh[:, :, :].rearrange("p t e -> p (t e)"),
                           ACT.Exp).then_inc(s_ex, 1)

        @block.vector
        def _(dve):
            vec = nc.vector
            chained = [0]

            def then_wait(ins):
                chained[0] += 1
                ins.then_inc(s_vc, 1)
                dve.wait_ge(s_vc, chained[0])

            def norm1(b):
                dve.wait_ge(s_x[b], 16)
                for t in range(b * TB, (b + 1) * TB):
                    then_wait(vec.bn_stats(stats[:, :], xs[:, t, :]))
                    then_wait(vec.bn_aggr(mv[:, t, :], stats[:, :]))
                bt = slice(b * TB, (b + 1) * TB)
                vec.tensor_scalar(ve[:, bt], mv[:, bt, 1], EPS, None, ALU.add).then_inc(s_ve, 1)
                dve.wait_ge(s_rstd, b + 1)
                for t in range(b * TB, (b + 1) * TB):
                    vec.tensor_scalar(xn[:, t, :], xs[:, t, :], mv[:, t, 0:1], rstd[:, t:t + 1],
                                      ALU.subtract, ALU.mult).then_inc(s_xn, 1)

            norm1(0)
            for half in range(2):
                dve.wait_ge(p_mc, half + 1)
                n = 2 if half == 0 else 4
                q0 = 0 if half == 0 else 2
                then_wait(vec.tensor_copy(
                    mcol[:, q0 * 4:(q0 + n) * 4].rearrange("p (q b k) -> p q b k", b=NB, k=KD),
                    mc_ps[:, q0 * 4:(q0 + n) * 4].rearrange("p (q k b) -> p q b k", b=NB, k=KD)))
                if half == 0:
                    vec.tensor_scalar(mcol[:, CA * 4:CA * 4 + 4], mcol[:, CA * 4:CA * 4 + 4], 1.0, None,
                                      ALU.add).then_inc(s_mcol, 1)
                    norm1(1)
                else:
                    gates = mcol[:, :].rearrange("p (u r c) -> p u r c", u=2, r=3)[:, :, 2, :]
                    vec.tensor_scalar(mcol[:, CB * 4:CB * 4 + 4], mcol[:, CB * 4:CB * 4 + 4], 1.0, None, ALU.add)
                    then_wait(vec.tensor_scalar(msgn[:, :, :], gates, 0.0, 2.0, ALU.is_ge, ALU.mult))
                    vec.tensor_scalar(msgn[:, :, :], msgn[:, :, :], -1.0, None, ALU.add)
                    then_wait(vec.scalar_tensor_tensor(mabs[:, :, :], gates, -1.0, gates, ALU.mult, ALU.max))
                    vec.scalar_tensor_tensor(gates, mabs[:, :, :], 0.25, msgn[:, :, :],
                                             ALU.max, ALU.mult).then_inc(s_mcol, 1)

            def conv(b, m):
                n, i = b * (MC + MD) + m, b * MC + m
                dve.wait_ge(s_tap, i + 1)
                ps = bank[proj_bank[n % 4]]
                for s in range(1, TAPS):
                    w = C_CW + m * TAPS + TAPS - 1 - s
                    ins = vec.scalar_tensor_tensor(acc[:, i % 3, s:L], ps[:, 0:L - s], pk[:, w:w + 1],
                                                   acc[:, i % 3, s:L], ALU.mult, ALU.add)
                    if s < TAPS - 1:
                        then_wait(ins)
                ins.then_inc(s_conv, 1)

            for m in range(MC):
                conv(0, m)

            dve.wait_ge(p_dt, 1)
            then_wait(vec.tensor_tensor(v[:, :].rearrange("p (t h) -> p t h", h=NH),
                                        dt_ps.rearrange("p (t h) -> p t h", h=NH),
                                        pk[:, C_DB:C_DB + NH].unsqueeze(1).to_broadcast([P, NT, NH]), ALU.add))
            vec.scalar_tensor_tensor(nabs[:, :], v[:, :], -1.0, v[:, :], ALU.mult, ALU.min).then_inc(s_nabs, 1)
            dve.wait_ge(s_en, 1)
            then_wait(vec.tensor_scalar(zz[:, :], en[:, :], 2.0, None, ALU.add))
            then_wait(vec.reciprocal(zz[:, :], zz[:, :]))
            then_wait(vec.tensor_tensor(zz[:, :], zz[:, :], en[:, :], ALU.mult))
            then_wait(vec.tensor_tensor(z2[:, :], zz[:, :], zz[:, :], ALU.mult))
            then_wait(vec.tensor_scalar(pp[:, :], z2[:, :], 1.0 / 17, None, ALU.mult))
            for k in (15, 13, 11, 9, 7, 5, 3):
                then_wait(vec.scalar_tensor_tensor(pp[:, :], pp[:, :], 1.0 / k, z2[:, :], ALU.add, ALU.mult))
            then_wait(vec.scalar_tensor_tensor(pp[:, :], pp[:, :], 1.0, zz[:, :], ALU.add, ALU.mult))
            then_wait(vec.tensor_scalar(v[:, :], v[:, :], 0.0, None, ALU.max))
            dtf = dt[:, :, :].rearrange("p t h -> p (t h)")
            then_wait(vec.scalar_tensor_tensor(dtf, pp[:, :], 2.0, v[:, :], ALU.mult, ALU.add))
            dve.wait_ge(s_expa, 1)
            vec.scalar_tensor_tensor(a[:, :, :], dt[:, :, :], -1.0, expa[:, :].unsqueeze(1).to_broadcast([P, NT, NH]),
                                     ALU.mult, ALU.mult).then_inc(s_dt, 1)

            for m in range(MC):
                conv(1, m)

            dve.wait_ge(s_rowin, 16)
            dve.wait_ge(s_wo, 16)
            for b in range(NB):
                for m in range(MD):
                    vec.scalar_tensor_tensor(wog[:, b, m, :], wo[:, m, :], pk[:, C_NW + m:C_NW + m + 1],
                                             mrow[:, 0, b, :], ALU.mult, ALU.mult).then_inc(s_wog, 1)

            def x_dt(c):
                dve.wait_ge(p_xtok, c + 1)
                if c >= 2:
                    dve.wait_ge(p_yd, c - 1)
                    dve.wait_ge(s_xdd, states_before(c - 2))
                vec.tensor_tensor(xdt[:, c % 2, :].rearrange("p (h d) -> p h d", h=NH),
                                  bank[XY].rearrange("p (h d) -> p h d", h=NH),
                                  dt[:, c, :].unsqueeze(2).to_broadcast([P, NH, HD]), ALU.mult).then_inc(s_xdt, 1)

            def g_masked(c):
                dve.wait_ge(s_btok, c + 1)
                vec.tensor_tensor(gm[:, c % 2, :], g_ps, le[:, :], ALU.mult).then_inc(s_gm, 1)

            def m_matrix(c):
                dve.wait_ge(s_l, c + 1)
                dve.wait_ge(s_gm, c + 1)
                vec.tensor_tensor(lm[:, c % 2, :, :], lm[:, c % 2, :, :],
                                  gm[:, c % 2, :].unsqueeze(1).to_broadcast([P, NH, P]), ALU.mult).then_inc(s_m, 1)

            def y_rest(c):
                dve.wait_ge(p_yoff, yoffs_before(c))
                dve.wait_ge(s_dec, c // TB + 1)
                vec.tensor_tensor(yoff.rearrange("p (h d) -> p h d", h=NH),
                                  bank[YOFF].rearrange("p (h d) -> p h d", h=NH),
                                  dec[:, c // TB, 0, c % TB, :].unsqueeze(2).to_broadcast([P, NH, HD]),
                                  ALU.mult).then_inc(s_yoffe, 1)
                dve.wait_ge(s_yoffe, yoffs_before(c))
                dve.wait_ge(p_yd, c + 1)
                if c >= 2:
                    dve.wait_ge(p_yT, c - 1)
                vec.tensor_tensor(y[:, c % 2, :], yoff, bank[YD], ALU.add).then_inc(s_y, 1)

            def state_rest(c):
                dve.wait_ge(s_sdec, rest_before(c))
                dve.wait_ge(p_st, states_before(c))
                vec.tensor_tensor(st[:, c % 2, :], stdec[:, :], bank[ST], ALU.add).then_inc(s_st, 1)

            def y_plus_dx(c):
                dve.wait_ge(p_yT, c + 1)
                if c >= 2:
                    dve.wait_ge(s_yg, c - 1)
                for m in range(MD):
                    ins = vec.scalar_tensor_tensor(ydx[:, c % 2, m, :], xcT[:, m, tok(c)], pk[:, C_D + m:C_D + m + 1],
                                                   bank[XY][:, m * P:(m + 1) * P], ALU.mult, ALU.add)
                ins.then_inc(s_ydx, 1)

            def mean_square(t):
                dve.wait_ge(p_out, t + 1)
                vec.tensor_scalar(rv[:, t:t + 1], ssq_ps[:, t:t + 1], 1.0 / DI, EPS, ALU.mult, ALU.add).then_inc(s_rv, 1)

            def norm2(t):
                b = t // TB
                dve.wait_ge(s_rr, t + 1)
                vec.scalar_tensor_tensor(xs[:, t, :], out_ps, rr[:, t:t + 1], xs[:, t, :],
                                         ALU.mult, ALU.add).then_inc(s_x1, 1)
                dve.wait_ge(s_x1, t + 1)
                then_wait(vec.bn_stats(stats2[:, :], xs[:, t, :]))
                then_wait(vec.bn_aggr(mv2[:, t, :], stats2[:, :]))
                vec.tensor_scalar(ve2[:, t:t + 1], mv2[:, t, 1:2], EPS, None, ALU.add).then_inc(s_ve2, 1)
                then_wait(vec.scalar_tensor_tensor(cent[:, :], xs[:, t, :], mv2[:, t, 0:1], mrow[:, CB - GA, b, :],
                                                   ALU.subtract, ALU.mult))
                dve.wait_ge(s_rstd2, t + 1)
                vec.scalar_tensor_tensor(h2[:, t, :], cent[:, :], rstd2[:, t:t + 1], mrow[:, SB - GA, b, :],
                                         ALU.mult, ALU.add).then_inc(s_h2, 1)

            def route(b):
                ts, n = slice(b * TB, (b + 1) * TB), [P, TB, NE]
                lg = lg_ps.rearrange("p (t e) -> p t e", e=NE)[:, ts, :]
                dve.wait_ge(p_lg, (b + 1) * TB)
                then_wait(vec.tensor_reduce(mx[:, ts], lg, AX.X, ALU.max))
                ins = vec.tensor_tensor(sh[:, ts, :], lg, mx[:, ts].unsqueeze(2).to_broadcast(n), ALU.subtract)
                ins.then_inc(s_sh, 1)
                dve.wait_ge(s_sh, b + 1)
                then_wait(vec.scalar_tensor_tensor(cand[:, ts, :], sh[:, ts, :], 0.0, rank[:, :, :], ALU.is_ge, ALU.mult))
                then_wait(vec.tensor_reduce(best[:, ts], cand[:, ts, :], AX.X, ALU.max))
                then_wait(vec.tensor_tensor(oh[:, ts, :], cand[:, ts, :], best[:, ts].unsqueeze(2).to_broadcast(n), ALU.is_equal))
                for t in range(b * TB, (b + 1) * TB):
                    if t == 0:
                        ins = vec.memset(pre[:, 0, :], 0.0)
                    else:
                        ins = vec.tensor_tensor(pre[:, t, :], pre[:, t - 1, :], oh[:, t - 1, :], ALU.add)
                    if t % TB < TB - 1:
                        then_wait(ins)
                ins.then_inc(s_oh, 1)
                then_wait(vec.tensor_tensor(offs[:, ts, :], oh[:, ts, :], slot0[:, :, :], ALU.mult))
                then_wait(vec.tensor_reduce(off[:, ts], offs[:, ts, :], AX.X, ALU.add))

            def slots(b):
                ts = slice(b * TB, (b + 1) * TB)
                dve.wait_ge(p_pos, b + 1)
                then_wait(vec.tensor_tensor(cnts[:, ts, :], pos_ps.rearrange("p (t e) -> p t e", e=NE)[:, ts, :],
                                            oh[:, ts, :], ALU.mult))
                then_wait(vec.tensor_reduce(cnt[:, ts], cnts[:, ts, :], AX.X, ALU.add))
                vec.tensor_scalar(keep[:, ts], cnt[:, ts], float(CAP), None, ALU.is_le)
                then_wait(vec.tensor_tensor(flat[:, ts], cnt[:, ts], off[:, ts], ALU.add))
                then_wait(vec.tensor_tensor(dlt[:, ts], flat[:, ts], spill[:, ts], ALU.subtract))
                then_wait(vec.tensor_tensor(dlt[:, ts], dlt[:, ts], keep[:, ts], ALU.mult))
                vec.tensor_tensor(src[:, ts], flat[:, ts], keep[:, ts], ALU.mult)
                vec.tensor_tensor(dest[:, ts], dlt[:, ts], spill[:, ts], ALU.add).then_inc(s_dest, 1)

            x_dt(0)
            g_masked(0)
            dve.wait_ge(s_const, 1)
            for c in range(NT + 3):
                if c == NT:
                    route(0)
                if c == NT + 1:
                    slots(0)
                if c < NT:
                    m_matrix(c)
                if c + 1 < NT:
                    x_dt(c + 1)
                    g_masked(c + 1)
                if 0 <= c - 2 < NT:
                    mean_square(c - 2)
                if c < NT and c % TB:
                    y_rest(c)
                    if c % TB < TB - 1:
                        state_rest(c)
                if 0 <= c - 2 < NT:
                    norm2(c - 2)
                if 0 <= c - 1 < NT:
                    y_plus_dx(c - 1)

            def up_act(u):
                kind, e, j = UPS[u]
                dve.wait_ge(s_sg, u + 1)
                g, w = bank[up_bank[u % 2][1]], sg[:, u % 2, :]
                if kind == "shared":
                    vec.tensor_tensor(shact[:, j, seq(e)], w, g, ALU.mult).then_inc(s_act, 1)
                else:
                    if e >= 2:
                        dve.wait_ge(p_dn, e - 1)
                    vec.tensor_tensor(eact[:, e % 2, :, :].rearrange("p j n -> p (j n)"), w[:, 0:JH * P],
                                      g[:, 0:JH * P], ALU.mult).then_inc(s_act, 1)

            route(1)
            slots(1)
            for u in range(NSH):
                up_act(u)
            for e in range(NE + 1):
                if e < NE:
                    up_act(NSH + e)
                if e >= 1:
                    dve.wait_ge(p_dn, e)
                    vec.tensor_copy(oes[:, e - 1, :], bank[down_bank[(e - 1) % 2]][:, 0:D]).then_inc(s_oes, 1)
            dve.wait_ge(s_ex, 1)
            then_wait(vec.tensor_reduce(es[:, :], ex[:, :, :], AX.X, ALU.add))
            then_wait(vec.reciprocal(gate[:, :], es[:, :]))
            then_wait(vec.tensor_tensor(gate[:, :], gate[:, :], keep[:, :], ALU.mult))
            for t in range(NT):
                dve.wait_ge(s_gath[t], 16)
                then_wait(vec.scalar_tensor_tensor(res[:, t, :], gath[:, t, :], gate[:, t:t + 1],
                                                   mrow[:, GB - GA, t // TB, :], ALU.mult, ALU.mult))
                then_wait(vec.tensor_tensor(res[:, t, :], res[:, t, :], xs[:, t, :], ALU.add))
                dve.wait_ge(p_sd, t + 1)
                vec.tensor_tensor(res[:, t, :], res[:, t, :], bank[sd_bank[t % 4]][:, 0:D], ALU.add).then_inc(s_fin, 1)

        @block.tensor
        def _(pe):
            mm = pe.matmul
            pe.wait_ge(s_sc, 1)

            def mod_cols(lo, hi):
                for j in range(lo, hi):
                    for k in range(KD):
                        ins = mm(mc_ps[:, j * NB:(j + 1) * NB], wm[:, k, j * P:(j + 1) * P], sc[:, k * NB:(k + 1) * NB],
                                 start=(k == 0), stop=(k == KD - 1))
                ins.then_inc(p_mc, 1)

            def transposed_x(b):
                pe.wait_ge(s_xn, TB * (b + 1))
                for k in range(KD):
                    if b:
                        pe.wait_ge(s_hT, k + 1)
                    for i in range(TB):
                        ins = pe.transpose(bank[k][:, i * P:(i + 1) * P], xn[:, b * TB + i, k * P:(k + 1) * P], ident[:, :])
                    ins.then_inc(p_hT, 1)

            def project(b, q):
                n = b * (MC + MD) + q
                col = DI + q * P if q < MC else (q - MC) * P
                if n >= 4:
                    b4, q4 = divmod(n - 4, MC + MD)
                    if q4 < MC:
                        pe.wait_ge(s_conv, b4 * MC + q4 + 1)
                    else:
                        pe.wait_ge(s_zs, b4 * MD + q4 - MC + 1)
                for k in range(KD):
                    ins = mm(bank[proj_bank[n % 4]], win[:, k, col:col + P], hT[:, k, seq(b)],
                             start=(k == 0), stop=(k == KD - 1))
                ins.then_inc(p_proj, 1)

            pe.wait_ge(s_wma, 16)
            mod_cols(0, 2 * KD)
            pe.wait_ge(s_const, 1)
            transposed_x(0)
            pe.wait_ge(s_hT, KD)
            pe.wait_ge(s_winx, 16)
            project(0, 0)
            project(0, 1)
            transposed_x(1)
            project(0, 2)
            pe.wait_ge(s_wmb, 16)
            pe.wait_ge(s_mcol, 1)
            mod_cols(2 * KD, 6 * KD)
            project(0, 3)
            pe.wait_ge(s_mcol, 2)
            pe.transpose(mt_ps, mcol[:, :], ident[:, :]).then_inc(p_mt, 1)
            project(0, 4)
            pe.wait_ge(s_hT, NB * KD)
            for t in range(NT):
                for k in range(KD):
                    ins = mm(dt_ps[:, t * NH:(t + 1) * NH], hT[:, k, tok(t)], win[:, k, DPROJ - NH:DPROJ],
                             start=(k == 0), stop=(k == KD - 1))
            ins.then_inc(p_dt, 1)
            project(0, 5)
            pe.wait_ge(s_winz, 16)
            for q in range(MC, MC + MD):
                project(0, q)
            for q in range(MC + MD):
                project(1, q)

            def small(b):
                if b == 0:
                    pe.wait_ge(s_dt, 1)
                    pe.wait_ge(s_mrow, 1)
                else:
                    pe.wait_ge(s_st, rest_before(TB - 1))
                n = TB * NH
                rhs = a[:, b * TB:(b + 1) * TB, :].rearrange("p t h -> p (t h)")
                for q, lhs in enumerate((le, gt, ones)):
                    ins = mm(small_ps[:, q * n:(q + 1) * n], lhs[:, :], rhs, start=True, stop=True)
                ins.then_inc(p_small, 1)

            def prep(c):
                b = c // TB
                pe.wait_ge(s_xc, MC * (b + 1))
                if c == 0:
                    pe.wait_ge(s_conv, NB * MC)
                    pe.wait_ge(s_zs, NB * MD)
                if c >= 1:
                    pe.wait_ge(s_xdt, c)
                if c >= 3:
                    pe.wait_ge(s_ydx, c - 2)
                for m in range(MD):
                    ins = pe.transpose(bank[XY][:, m * P:(m + 1) * P], xcT[:, m, tok(c)], ident[:, :])
                ins.then_inc(p_xtok, 1)
                if c >= 1:
                    pe.wait_ge(s_gm, c)
                if c >= 5:
                    pe.wait_ge(s_h2T, c - 4)
                pe.transpose(b_ps, xcT[:, MD, tok(c)], ident[:, :])
                mm(g_ps, xcT[:, MD, tok(c)], xcT[:, MD + 1, tok(c)], start=True, stop=True).then_inc(p_bg, 1)
                pe.wait_ge(s_al, c + 1)
                if c >= 1:
                    pe.wait_ge(s_l, c)
                for g in range(2):
                    ins = mm(seg_ps[:, g, :], gt[:, :],
                             al[:, c % 2, g * NH // 2:(g + 1) * NH // 2, :].rearrange("p h l -> p (h l)"),
                             start=True, stop=True)
                ins.then_inc(p_seg, 1)

            def scan(c):
                b, i = divmod(c, TB)
                pe.wait_ge(s_xdt, c + 1)
                if c >= 1:
                    if (c - 1) % TB == 0:
                        pe.wait_ge(s_y0, (c - 1) // TB + 1)
                    else:
                        pe.wait_ge(s_y, yoffs_before(c - 1))
                if i > 0:
                    if i == 1:
                        pe.wait_ge(s_st0, c // TB + 1)
                    else:
                        pe.wait_ge(s_st, rest_before(c - 1))
                    mm(bank[YOFF], xcT[:, MD + 1, tok(c)], st[:, (c - 1) % 2, :], start=True, stop=True).then_inc(p_yoff, 1)
                if i < TB - 1:
                    pe.wait_ge(s_dec, b + 1)
                    if i > 1:
                        pe.wait_ge(s_st, rest_before(c - 1))
                    elif i == 1:
                        pe.wait_ge(s_st0, b + 1)
                    pe.wait_ge(s_btok, c + 1)
                    pe.wait_ge(s_xdd, states_before(c))
                    mm(bank[ST], btok[:, c % 2, :], xdd[:, c % 2, :], start=True, stop=True).then_inc(p_st, 1)
                pe.wait_ge(s_m, c + 1)
                for h in range(NH):
                    ins = mm(bank[YD][:, h * HD:(h + 1) * HD], lm[:, c % 2, h, :], xdt[:, c % 2, h * HD:(h + 1) * HD],
                             start=True, stop=True)
                ins.then_inc(p_yd, 1)

            def y_transposed(c):
                if c % TB == 0:
                    pe.wait_ge(s_y0, c // TB + 1)
                else:
                    pe.wait_ge(s_y, yoffs_before(c))
                pe.wait_ge(s_xdt, min(c + 3, NT))
                if c >= 1:
                    pe.wait_ge(s_ydx, c)
                for m in range(MD):
                    ins = pe.transpose(bank[XY][:, m * P:(m + 1) * P], y[:, c % 2, m * P:(m + 1) * P], ident[:, :])
                ins.then_inc(p_yT, 1)

            def out_project(c):
                b = c // TB
                if c == 0:
                    pe.wait_ge(s_wog, NB * MD)
                else:
                    pe.wait_ge(s_x1, c)
                pe.wait_ge(s_yg, c + 1)
                for m in range(MD):
                    mm(out_ps, yg[:, c % 2, m, :], wog[:, b, m, :], start=(m == 0), stop=(m == MD - 1))
                pe.wait_ge(s_sq, c + 1)
                for m in range(MD):
                    ins = mm(ssq_ps[:, c:c + 1], sq[:, c % 2, m, :], ones[:, 0:1], start=(m == 0), stop=(m == MD - 1))
                ins.then_inc(p_out, 1)

            def h2_transposed(t):
                pe.wait_ge(s_h2, t + 1)
                pe.wait_ge(s_gm, min(t + 5, NT))
                if t >= 1:
                    pe.wait_ge(s_h2T, t)
                for k in range(KD):
                    ins = pe.transpose(h2T_ps[:, k * P:(k + 1) * P], h2[:, t, k * P:(k + 1) * P], ident[:, :])
                ins.then_inc(p_h2T, 1)

            def logits(t):
                pe.wait_ge(s_h2T, t + 1)
                pe.wait_ge(s_x1, min(t + 2, NT))
                if t == TB:
                    pe.wait_ge(s_oh, 1)
                elif t == TB + 1:
                    pe.wait_ge(s_dest, 1)
                for k in range(KD):
                    ins = mm(lg_ps[:, t * NE:(t + 1) * NE], h2T[:, k, tok(t)], pk[:, C_WG + k * NE:C_WG + (k + 1) * NE],
                             start=(k == 0), stop=(k == KD - 1))
                ins.then_inc(p_lg, 1)

            def positions(b):
                pe.wait_ge(s_oh, b + 1)
                pe.wait_ge(s_x1, NT - 1 + b)
                n = TB * NE
                ps = pos_ps[:, b * n:(b + 1) * n]
                ts = slice(b * TB, (b + 1) * TB)
                mm(ps, le_b[:, :], oh[:, ts, :].rearrange("p t e -> p (t e)"), start=True, stop=False)
                mm(ps, ones_b[:, :], pre[:, ts, :].rearrange("p t e -> p (t e)"), start=False, stop=True).then_inc(p_pos, 1)

            def up_shared(u):
                _, b, j = UPS[u]
                if u == 0:
                    pe.wait_ge(s_shw, 32)
                    pe.wait_ge(s_l, NT)
                if u == 1:
                    pe.wait_ge(s_y, yoffs_before(NT - 1))
                if u >= 2:
                    pe.wait_ge(s_act, u - 1)
                pe.wait_ge(s_h2T, TB * (b + 1))
                for q, w in enumerate((shw1, shw3)):
                    for k in range(KD):
                        ins = mm(bank[up_bank[u % 2][q]], w[:, k, HJ[j]:HJ[j] + P], h2T[:, k, seq(b)],
                                 start=(k == 0), stop=(k == KD - 1))
                ins.then_inc(p_up, 1)

            def slots_transposed(e):
                pe.wait_ge(s_xg, 16 * (e // 4 + 1))
                if e == 1:
                    pe.wait_ge(s_dest, NB)
                if e >= 2:
                    pe.wait_ge(s_xdT, e - 1)
                for k in range(KD):
                    ins = pe.transpose(bank[xdT_bank[e % 2]][:, k * P:(k + 1) * P],
                                       xg[:, e, k * P:(k + 1) * P], ident[:, :])
                ins.then_inc(p_xdT, 1)

            def up_expert(e):
                u = NSH + e
                pe.wait_ge(s_ew[e], 64)
                pe.wait_ge(s_xdT, e + 1)
                pe.wait_ge(s_act, u - 1)
                for q, w in enumerate((ew1, ew3)):
                    for j in range(JH):
                        for k in range(KD):
                            ins = mm(bank[up_bank[u % 2][q]][:, j * P:(j + 1) * P], w[:, e % EB, k, HJ[j]:HJ[j] + P],
                                     xdT[:, e % 2, k, :], start=(k == 0), stop=(k == KD - 1))
                ins.then_inc(p_up, 1)

            def down_expert(e):
                pe.wait_ge(s_act, NSH + e + 1)
                pe.wait_ge(s_pad, 1)
                if e >= 2:
                    pe.wait_ge(s_oes, e - 1)
                for j in range(JH):
                    ins = mm(bank[down_bank[e % 2]][:, 0:D], eact[:, e % 2, j, :], ew2[:, e % EB, j, :],
                             start=(j == 0), stop=(j == JH - 1))
                ins.then_inc(p_dn, 1)

            def down_shared(t):
                pe.wait_ge(s_shg, NB)
                pe.wait_ge(s_act, len(UPS))
                if t >= 4:
                    pe.wait_ge(s_fin, t - 3)
                for j in range(JH):
                    ins = mm(bank[sd_bank[t % 4]][:, 0:D], shact[:, j, tok(t)], shw2g[:, t // TB, j, :],
                             start=(j == 0), stop=(j == JH - 1))
                ins.then_inc(p_sd, 1)

            small(0)
            prep(0)
            for c in range(NT + 4):
                if c + 1 < NT:
                    if (c + 1) % TB == 0:
                        small((c + 1) // TB)
                    prep(c + 1)
                if c < NT:
                    scan(c)
                if 0 <= c - 1 < NT:
                    y_transposed(c - 1)
                if c == NT + 1:
                    positions(0)
                if 0 <= c - 4 < NT:
                    logits(c - 4)
                if 0 <= c - 2 < NT:
                    out_project(c - 2)
                if 0 <= c - 3 < NT:
                    h2_transposed(c - 3)
            positions(1)
            for u in range(NSH):
                up_shared(u)
            slots_transposed(0)
            for e in range(NE + 1):
                if e + 1 < NE:
                    slots_transposed(e + 1)
                if e < NE:
                    up_expert(e)
                if e >= 1:
                    down_expert(e - 1)
            for t in range(NT):
                down_shared(t)


def kernel(L0_attn_x, L0_attn_in_proj_w, L0_attn_conv_w, L0_attn_conv_b, L0_attn_A_log, L0_attn_D,
           L0_attn_dt_bias, L0_attn_norm_w, L0_attn_out_proj_w, L0_ffn_Wg, L0_ffn_W1, L0_ffn_W3,
           L0_ffn_W2, L0_ffn_sw1, L0_ffn_sw3, L0_ffn_sw2, L0_c, L0_wmod):
    import numpy as np
    import concourse.bacc as bacc
    from concourse.bass_utils import run_bass_kernel_spmd

    def blocks(m):
        m = np.asarray(m)
        m = m.reshape(-1, P, int(np.prod(m.shape[1:])) if m.ndim > 1 else 1)
        return m.transpose(1, 0, 2).reshape(P, -1)

    pack = np.concatenate([
        blocks(L0_attn_conv_w), blocks(L0_attn_conv_b), blocks(L0_attn_norm_w),
        blocks(np.repeat(np.asarray(L0_attn_D), HD)),
        np.broadcast_to(np.asarray(L0_attn_A_log), (P, NH)), np.broadcast_to(np.asarray(L0_attn_dt_bias), (P, NH)),
        blocks(np.asarray(L0_c).T), blocks(L0_ffn_Wg)], axis=1)
    ins = {
        "x": L0_attn_x, "in_w": np.asarray(L0_attn_in_proj_w).T, "out_w": np.asarray(L0_attn_out_proj_w).T,
        "pack": pack, "wmod": L0_wmod, "w1": L0_ffn_W1, "w3": L0_ffn_W3, "w2": L0_ffn_W2,
        "sw1": L0_ffn_sw1, "sw3": L0_ffn_sw3, "sw2": L0_ffn_sw2,
    }
    nc = bacc.Bacc("TRN2", target_bir_lowering=False, num_devices=1)
    arrays, aps = {}, {}
    for name, value in ins.items():
        value = np.ascontiguousarray(value)
        arrays[f"in_{name}"] = value
        aps[name] = nc.dram_tensor(f"in_{name}", value.shape, mybir.dt.from_np(value.dtype), kind="ExternalInput").ap()
    aps["out"] = nc.dram_tensor("out_x", (NB, L, D), mybir.dt.float32, kind="ExternalOutput").ap()
    build(nc, **aps)
    return run_bass_kernel_spmd(nc, [arrays], core_ids=[0]).results[0]["out_x"]
```

```python
from contextlib import ExitStack

import concourse.bass as bass
from concourse import mybir

P = 128
D = 256
KD = D // P
NB = 2
L = 512
NT = NB * L // P
TB = L // P
DI = 512
MD = DI // P
NH = 8
HD = DI // NH
NS = 128
Q = 64
NQ = P // Q
TAPS = 4
MC = MD + 2
DPROJ = 2 * DI + 2 * NS + NH
NE = 8
EB = 4
CAP = NB * L // NE
HID = 352
JH = 3
HJ = [0, P, HID - P]
DUP = HJ[1] + P - HJ[2]
EPS = 1e-5

C_CW = 0
C_CB = C_CW + MC * TAPS
C_NW = C_CB + MC
C_D = C_NW + MD
C_AL = C_D + MD
C_DB = C_AL + NH
C_C = C_DB + NH
C_WG = C_C + KD * NB
NPACK = C_WG + KD * NE

SA, CA, GA, SB, CB, GB = range(6)


def build(nc, x, in_w, out_w, pack, wmod, w1, w3, w2, sw1, sw3, sw2, out):
    f32, bf16, i32 = mybir.dt.float32, mybir.dt.bfloat16, mybir.dt.int32
    ALU, ACT, AX = mybir.AluOpType, mybir.ActivationFunctionType, mybir.AxisListType

    mod_rows = nc.dram_tensor("mod_rows", (NB, 4, D), f32, kind="Internal").ap()
    xd = nc.dram_tensor("xd", (NE * CAP + NB * L, D), f32, kind="Internal").ap()
    oe = nc.dram_tensor("oe", (NE * CAP, D), f32, kind="Internal").ap()

    with ExitStack() as ctx:
        def sb(name, shape, dt=f32):
            return ctx.enter_context(nc.sbuf_tensor(name, shape, dt))

        def sem(name):
            return ctx.enter_context(nc.semaphore(name))

        ident = sb("ident", [P, P])
        ones = sb("ones", [P, P])
        le = sb("le", [P, Q])
        le2 = sb("le2", [P, P])
        gt2 = sb("gt2", [P, P])
        half = sb("half", [P, NQ, P])
        le_b = sb("le_b", [P, P], bf16)
        ones_b = sb("ones_b", [P, P], bf16)
        neg_half = sb("neg_half", [P, NH])
        euler = sb("euler", [P, NT * NH])
        rank = sb("rank", [P, TB, NE])
        slot0 = sb("slot0", [P, TB, NE])
        spill = sb("spill", [P, NT])
        zero = sb("zero", [P, D])
        pk = sb("pk", [P, NPACK])
        xs = sb("xs", [P, NT, D])
        wm = sb("wm", [P, KD, 6 * D])
        win = sb("win", [P, KD, DPROJ])
        wo = sb("wo", [P, MD, D])
        shw1 = sb("shw1", [P, KD, HID])
        shw3 = sb("shw3", [P, KD, HID])
        shw2 = sb("shw2", [P, JH, D])
        ew1 = sb("ew1", [P, EB, KD, HID])
        ew3 = sb("ew3", [P, EB, KD, HID])
        ew2 = sb("ew2", [P, EB, JH, D])
        sc = sb("sc", [P, KD * NB])
        mcol = sb("mcol", [P, 2 * NB * KD])
        mrow = sb("mrow", [P, NB, 4, D])
        wog = sb("wog", [P, NB, MD, D])
        shw2g = sb("shw2g", [P, NB, JH, D])
        stats = sb("stats", [P, NT, 6])
        stats2 = sb("stats2", [P, 6])
        mv = sb("mv", [P, NT, 2])
        ve = sb("ve", [P, NT])
        rstd = sb("rstd", [P, NT])
        mv2 = sb("mv2", [P, NT, 2])
        ve2 = sb("ve2", [P, NT])
        rstd2 = sb("rstd2", [P, NT])
        xn = sb("xn", [P, NT, D])
        h2 = xn
        cent = sb("cent", [P, D])
        hT = sb("hT", [P, KD, NB * L])
        acc = sb("acc", [P, 3, L])
        xcT = sb("xcT", [P, MC, NB * L])
        zs = sb("zs", [P, MD, NB * L])
        NDT = NT * NH
        v = sb("v", [P, NDT])
        nabs = sb("nabs", [P, NDT])
        en = sb("en", [P, NDT])
        zz = sb("zz", [P, NDT])
        z2 = sb("z2", [P, NDT])
        pp = sb("pp", [P, NDT])
        dt = sb("dt", [P, NT, NH])
        expa = sb("expa", [P, NH])
        a = sb("a", [P, NT, NH])
        dec = sb("dec", [P, NB, 2 + NQ, TB, NH])
        wm_flat = wm[:, :, :].rearrange("p k n -> p (k n)")
        win_flat = win[:, :, :].rearrange("p k n -> p (k n)")
        al = sb("al", [P, 2, NH, Q])
        btok = sb("btok", [P, 2, NS])
        gm = sb("gm", [P, 2, Q])
        lm = wm_flat[:, 0:2 * NH * Q].rearrange("p (r h l) -> p r h l", r=2, h=NH)
        xdt = wm_flat[:, 2 * DI:4 * DI].rearrange("p (r n) -> p r n", r=2)
        stdec = wm_flat[:, 4 * DI:6 * DI].rearrange("p (q n) -> p q n", q=NQ)
        xdd = win_flat[:, 0:2 * DI].rearrange("p (r n) -> p r n", r=2)
        y = win_flat[:, 2 * DI:4 * DI].rearrange("p (r n) -> p r n", r=2)
        yoff = win_flat[:, 4 * DI:5 * DI]
        st = sb("st", [P, 2, NQ, DI])
        ydx = sb("ydx", [P, 2, MD, P])
        yg = sb("yg", [P, 2, MD, P])
        sq = sb("sq", [P, 2, MD, P])
        sqs = sb("sqs", [P, 2, P])
        mrow_sb = ydx[0:NB, :, :, :].rearrange("b r m n -> b (r m n)").rearrange("b (q d) -> b q d", d=D)
        gside, gtest = (m[0:NB, :, :, :].rearrange("b r m n -> b (r m n)")
                        .rearrange("b (u s d) -> b u s d", u=2, s=2) for m in (yg, sq))
        rv = sb("rv", [P, NT])
        rr = sb("rr", [P, NT])
        h2T = hT
        mx = sb("mx", [P, NT])
        sh = sb("sh", [P, NT, NE])
        cand = sb("cand", [P, NT, NE])
        best = sb("best", [P, NT])
        oh = sb("oh", [P, NT, NE], bf16)
        pre = sb("pre", [P, NT, NE], bf16)
        offs = sb("offs", [P, NT, NE])
        off = sb("off", [P, NT])
        cnts = sb("cnts", [P, NT, NE])
        cnt = sb("cnt", [P, NT])
        keep = sb("keep", [P, NT])
        flat = sb("flat", [P, NT])
        dlt = sb("dlt", [P, NT])
        dest = sb("dest", [P, NT], i32)
        src = sb("src", [P, NT], i32)
        ex = sb("ex", [P, NT, NE])
        es = sb("es", [P, NT])
        gate = sb("gate", [P, NT])
        sg = acc
        shact = wm_flat.rearrange("p (j n) -> p j n", j=JH)
        eact = sb("eact", [P, 2, JH, P])
        xg = zs[:, 0:2, :].rearrange("p m (e d) -> p (m e) d", d=D)
        xdT = sb("xdT", [P, 2, KD, P])
        oes = zs[:, 2:4, :].rearrange("p m (e d) -> p (m e) d", d=D)
        gath = xcT[:, 0:2, :].rearrange("p m (t d) -> p (m t) d", d=D)
        res = xcT[:, 2:4, :].rearrange("p m (t d) -> p (m t) d", d=D)

        bank = [ctx.enter_context(nc.psum_tensor(f"bank{i}", [P, 512], f32))[:, :] for i in range(8)]
        SEG, ST, X, BG, YD, YOFF, YT, MISC = range(8)
        proj_bank = [2, 3, 4, 5]
        mc_ps = bank[6][:, 0:2 * NB * KD]
        dt_ps = bank[7][:, 0:NDT]
        out_ps = bank[MISC][:, 0:D]
        small_ps = bank[YT][:, 0:(2 + NQ) * TB * NH]
        ssq_ps = bank[MISC][:, 352:352 + NT]
        lg_ps = bank[BG][:, 4 * P - NT * NE:4 * P]
        pos_ps = bank[YD][:, 0:NT * NE]
        b_ps = bank[BG][:, 0:P]
        g_ps = bank[BG][:, P:P + Q]
        h2T_ps = bank[BG][:, P + Q:P + Q + D]
        up_bank = [(0, 1), (5, 6)]
        down_bank = [3, 4]
        xdT_bank = [X, MISC]
        sd_bank = [0, 1, 5, 6]

        s_pack, s_x = sem("pack_in"), [sem(f"x{t}_in") for t in range(NT)]
        s_wma, s_wmb = sem("wmod_a_in"), sem("wmod_b_in")
        s_winx, s_winz = sem("winx_in"), sem("winz_in")
        s_wo, s_shw, s_sh2 = sem("wo_in"), sem("shared_up_in"), sem("shared_down_in")
        s_ew = [sem(f"expert{e}_in") for e in range(NE)]
        s_rowout, s_rowin = sem("mod_rows_out"), sem("mod_rows_in")
        s_zeroed, s_scat, s_xg = sem("xd_zeroed"), sem("scattered"), [sem(f"slots{q}_in") for q in range(NE // 2)]
        s_oeout, s_gath, s_out = sem("expert_out"), [sem(f"gathered{t}") for t in range(NT)], sem("stored")
        s_pc, s_const = sem("pool_chain"), sem("constants")
        s_mrow, s_rstd, s_expa, s_en = sem("mod_rows_sb"), sem("rstd"), sem("exp_a"), sem("exp_neg")
        s_al, s_xdd, s_sdec, s_yg = sem("a_masked"), sem("x_decayed"), sem("state_decayed"), sem("y_gated")
        s_rr, s_rstd2, s_shg, s_pad = sem("rrms"), sem("rstd2"), sem("shared_gated"), sem("w2_pads")
        s_sc, s_hT, s_tap, s_xc, s_zs = sem("silu_c"), sem("hT"), sem("first_tap"), sem("conv_silu"), sem("z_silu")
        s_mraw, s_dec, s_l, s_btok = sem("mod_rows_raw"), sem("decays"), sem("decay_matrix"), sem("b_tokens")
        s_sq, s_h2T = sem("y_squared"), sem("h2T")
        s_sg, s_xdT, s_ex = sem("up_silu"), sem("slots_T"), sem("gate_exp")
        s_vc = sem("vector_chain")
        s_ve, s_xn, s_mcol, s_conv = sem("variance"), sem("x_normed"), sem("mod_cols"), sem("conv_done")
        s_nabs, s_dt, s_wog = sem("neg_abs"), sem("time_steps"), sem("wo_gated")
        s_m, s_xdt, s_gm = sem("m_matrix"), sem("x_dt"), sem("g_masked")
        s_yoffe, s_y, s_st = sem("yoff_scaled"), sem("y_sum"), sem("states")
        s_sqs, s_cent = sem("squares_summed"), sem("x_centred")
        s_ydx, s_rv, s_x1, s_ve2, s_h2 = sem("y_plus_dx"), sem("mean_square"), sem("x1"), sem("variance2"), sem("h2_rows")
        s_sh, s_oh, s_dest, s_gate = sem("logits_shifted"), sem("one_hot"), sem("slots"), sem("gates")
        s_pre = sem("shared_added")
        s_act, s_oes, s_fin = sem("up_act"), sem("expert_rows"), sem("final_rows")
        p_mc, p_mt, p_hT, p_dt, p_proj = sem("p_mod_cols"), sem("p_mod_rows"), sem("p_hT"), sem("p_dt"), sem("p_proj")
        p_small, p_xtok, p_bg, p_seg = sem("p_small"), sem("p_x_tokens"), sem("p_b_g"), sem("p_seg")
        p_yd, p_yoff, p_st, p_yT, p_ssq, p_out = sem("p_y_diag"), sem("p_y_off"), sem("p_state"), sem("p_yT"), sem("p_sum_squares"), sem("p_out")
        p_h2T, p_lg, p_pos = sem("p_h2T"), sem("p_logits"), sem("p_positions")
        p_up, p_xdT, p_dn, p_sd = sem("p_up"), sem("p_slots_T"), sem("p_down"), sem("p_shared_down")

        block = ctx.enter_context(nc.Block())

        def tok(c):
            return slice(c * P, (c + 1) * P)

        def seq(b):
            return slice(b * L, (b + 1) * L)

        def decays_before(c, q):
            return NQ * c + q + 1 - (c // TB + 1)

        PROJ = [0, 1, MC, 2, 3, MC + 1, 4, 5, MC + 2, MC + 3]
        NPROJ = MC + MD

        def place(b, q):
            return b * NPROJ + PROJ.index(q)

        UPS = [("shared", b, j) for b in range(NB) for j in range(JH)] + [("expert", e, 0) for e in range(NE)]
        NSH = NB * JH

        @block.sync
        def _(sp):
            sp.dma_start(pk[:, :], pack).then_inc(s_pack, 16)
            xv = x.rearrange("b (t p) d -> p (b t) d", p=P)
            wmv = wmod.rearrange("(k p) n -> p k n", p=P)
            wiv = in_w.rearrange("(k p) n -> p k n", p=P)
            sp.dma_start(wm[:, :, 0:2 * D], wmv[:, :, 0:2 * D]).then_inc(s_wma, 16)
            for t in range(TB):
                sp.dma_start(xs[:, t, :], xv[:, t, :]).then_inc(s_x[t], 16)
            sp.dma_start(win[:, :, DI:DPROJ], wiv[:, :, DI:DPROJ]).then_inc(s_winx, 16)
            for t in range(TB, NT):
                sp.dma_start(xs[:, t, :], xv[:, t, :]).then_inc(s_x[t], 16)
            sp.dma_start(wm[:, :, 2 * D:6 * D], wmv[:, :, 2 * D:6 * D]).then_inc(s_wmb, 16)
            sp.dma_start(win[:, :, 0:DI], wiv[:, :, 0:DI]).then_inc(s_winz, 16)
            sp.dma_start(wo[:, :, :], out_w.rearrange("(m p) n -> p m n", p=P)).then_inc(s_wo, 16)
            sp.wait_ge(s_mrow, 1)
            sp.dma_start(mod_rows, mrow_sb[:, :, :]).then_inc(s_rowout, 16)
            sp.dma_start(shw1[:, :, :], sw1.rearrange("(k p) n -> p k n", p=P)).then_inc(s_shw, 16)
            sp.dma_start(shw3[:, :, :], sw3.rearrange("(k p) n -> p k n", p=P)).then_inc(s_shw, 16)
            sp.wait_ge(s_rowout, 16)
            sp.dma_start(mrow[:, :, :, :].rearrange("p b a d -> p (b a d)"),
                         mod_rows.rearrange("b q d -> (b q d)").partition_broadcast(P)).then_inc(s_rowin, 16)
            sp.dma_start(shw2[:, 0:2, :], sw2[0:2 * P, :].rearrange("(j p) n -> p j n", p=P)).then_inc(s_sh2, 16)
            sp.dma_start(shw2[DUP:P, 2, :], sw2[2 * P:HID, :]).then_inc(s_sh2, 16)
            sp.wait_ge(s_const, 1)
            for e in range(NE):
                sp.dma_start(xd[e * CAP:(e + 1) * CAP, :], zero[:, :]).then_inc(s_zeroed, 16)
            sp.wait_ge(s_pad, 1)
            def load_expert(e):
                q = e % EB
                if e >= EB:
                    sp.wait_ge(p_dn, e - EB + 1)
                sp.dma_start(ew1[:, q, :, :], w1[e].rearrange("(k p) n -> p k n", p=P)).then_inc(s_ew[e], 16)
                sp.dma_start(ew3[:, q, :, :], w3[e].rearrange("(k p) n -> p k n", p=P)).then_inc(s_ew[e], 16)
                sp.dma_start(ew2[:, q, 0:2, :], w2[e, 0:2 * P, :].rearrange("(j p) n -> p j n", p=P)).then_inc(s_ew[e], 16)
                sp.dma_start(ew2[DUP:P, q, 2, :], w2[e, 2 * P:HID, :]).then_inc(s_ew[e], 16)
            for e in range(EB):
                load_expert(e)
            sp.wait_ge(s_scat, 16 * NT)
            for q in range(NE // 2):
                sp.dma_start(xg[:, 2 * q:2 * q + 2, :],
                             xd[2 * q * CAP:(2 * q + 2) * CAP, :].rearrange("(e p) d -> p e d", p=P)).then_inc(s_xg[q], 16)
            for e in range(NE):
                if e + EB < NE:
                    load_expert(e + EB)
                sp.wait_ge(s_oes, e + 1)
                sp.dma_start(oe[e * CAP:(e + 1) * CAP, :], oes[:, e, :]).then_inc(s_oeout, 16)
            ov = out.rearrange("b (t p) d -> (b t) p d", p=P)
            for t in range(NT):
                sp.wait_ge(s_fin, t + 1)
                sp.dma_start(ov[t], res[:, t, :]).then_inc(s_out, 16)
            sp.wait_ge(s_out, 16 * NT)

        @block.gpsimd
        def _(pool):
            chained = [0]

            def then_wait(ins):
                chained[0] += 1
                ins.then_inc(s_pc, 1)
                pool.wait_ge(s_pc, chained[0])

            pool.memset(zero[:, :], 0.0)
            pool.memset(neg_half[:, :], -0.5)
            pool.memset(euler[:, :], 2.718281828459045)
            pool.memset(ones_b[:, :], 1.0)
            pool.memset(ones[:, :], 1.0)
            pool.memset(half[:, :, :], 1.0)
            then_wait(pool.memset(ident[:, :], 0.0))
            pool.affine_select(out=ident[:, :], in_=ident[:, :], compare_op=ALU.not_equal, fill=1.0,
                               base=0, pattern=[[-1, P]], channel_multiplier=1)
            pool.affine_select(out=le_b[:, :], in_=ones[:, :], compare_op=ALU.is_ge, fill=0.0,
                               base=0, pattern=[[1, P]], channel_multiplier=-1)
            le2v, gt2v = (m[:, :].rearrange("p (q l) -> p q l", q=NQ) for m in (le2, gt2))
            onev = ones[:, :].rearrange("p (q l) -> p q l", q=NQ)
            pool.affine_select(out=le2v, in_=onev, compare_op=ALU.is_ge, fill=0.0, base=0,
                               pattern=[[Q, NQ], [1, Q]], channel_multiplier=-1)
            pool.affine_select(out=gt2v, in_=onev, compare_op=ALU.is_gt, fill=0.0, base=0,
                               pattern=[[-Q, NQ], [-1, Q]], channel_multiplier=1)
            then_wait(pool.affine_select(out=half[:, :, :], in_=half[:, :, :], compare_op=ALU.is_ge, fill=0.0,
                                         base=0, pattern=[[-Q, NQ], [0, P]], channel_multiplier=1))
            pool.affine_select(out=gt2v, in_=gt2v, compare_op=ALU.is_ge, fill=0.0, base=Q - 1,
                               pattern=[[Q, NQ], [0, Q]], channel_multiplier=-1)
            pool.affine_select(out=half[:, :, :], in_=half[:, :, :], compare_op=ALU.is_ge, fill=0.0, base=Q - 1,
                               pattern=[[Q, NQ], [0, P]], channel_multiplier=-1)
            then_wait(pool.affine_select(out=le2v, in_=le2v, compare_op=ALU.is_ge, fill=0.0, base=0,
                                         pattern=[[-Q, NQ], [0, Q]], channel_multiplier=1))
            pool.tensor_tensor(le[:, :], le2[:, 0:Q], le2[:, Q:P], ALU.add)
            pool.iota(rank[:, :, :], pattern=[[0, TB], [-1, NE]], base=NE, channel_multiplier=0,
                      allow_small_or_imprecise_dtypes=True)
            pool.iota(slot0[:, :, :], pattern=[[0, TB], [CAP, NE]], base=-1, channel_multiplier=0,
                      allow_small_or_imprecise_dtypes=True)
            pool.iota(spill[:, :], pattern=[[P, NT]], base=NE * CAP, channel_multiplier=1,
                      allow_small_or_imprecise_dtypes=True).then_inc(s_const, 1)

            for b in range(NB):
                pool.wait_ge(s_ve, b + 1)
                bt = slice(b * TB, (b + 1) * TB)
                pool.tensor_tensor(rstd[:, bt], ve[:, bt], neg_half[:, 0:TB], ALU.pow).then_inc(s_rstd, 1)
            pool.wait_ge(s_pack, 16)
            pool.tensor_tensor(expa[:, :], euler[:, 0:NH], pk[:, C_AL:C_AL + NH], ALU.pow).then_inc(s_expa, 1)
            pool.wait_ge(s_nabs, 1)
            pool.tensor_tensor(en[:, :], euler[:, :], nabs[:, :], ALU.pow).then_inc(s_en, 1)
            pool.wait_ge(s_mraw, 2)
            gates = [mrow_sb[:, q - GA, :] for q in (GA, GB)]
            pool.tensor_scalar(mrow_sb[:, CB - GA, :], mrow_sb[:, CB - GA, :], 1.0, None, ALU.add)
            for u in range(2):
                pool.tensor_scalar(gside[:, u, 0, :], gates[u], 0.25, None, ALU.max)
                pool.tensor_scalar(gside[:, u, 1, :], gates[u], -0.25, None, ALU.min)
                pool.tensor_scalar(gtest[:, u, 0, :], gates[u], 0.0, None, ALU.is_ge)
                ins = pool.tensor_scalar(gtest[:, u, 1, :], gates[u], 0.0, None, ALU.is_lt)
            then_wait(ins)
            then_wait(pool.tensor_tensor(gside[:, :, :, :], gside[:, :, :, :], gtest[:, :, :, :], ALU.mult))
            for u in range(2):
                ins = pool.tensor_tensor(gates[u], gside[:, u, 0, :], gside[:, u, 1, :], ALU.add)
            ins.then_inc(s_mrow, 1)
            pool.memset(shw2[0:DUP, 2, :], 0.0)
            pool.memset(ew2[0:DUP, :, 2, :], 0.0).then_inc(s_pad, 1)

            def masked_a(c):
                if c >= 2:
                    pool.wait_ge(p_seg, c - 1)
                pool.tensor_tensor(al[:, c % 2, :, :], le[:, :].unsqueeze(1).to_broadcast([P, NH, Q]),
                                   a[:, c, :].unsqueeze(2).to_broadcast([P, NH, Q]), ALU.mult).then_inc(s_al, 1)

            def rest_decay(c):
                pool.wait_ge(s_xdt, c + 1)
                pool.wait_ge(s_dec, c // TB + 1)
                if c >= 2:
                    pool.wait_ge(p_st, NQ * (c - 1))
                pool.tensor_tensor(xdd[:, c % 2, :].rearrange("p (h d) -> p h d", h=NH),
                                   xdt[:, c % 2, :].rearrange("p (h d) -> p h d", h=NH),
                                   dec[:, c // TB, 1, c % TB, :].unsqueeze(2).to_broadcast([P, NH, HD]),
                                   ALU.mult).then_inc(s_xdd, 1)

            def decayed_state(c, q):
                if c % TB == 0 and q == 0:
                    return
                pool.wait_ge(s_st, NQ * c + q)
                before = st[:, c % 2, 0, :] if q else st[:, (c - 1) % 2, NQ - 1, :]
                pool.tensor_tensor(stdec[:, q, :].rearrange("p (h d) -> p h d", h=NH),
                                   before.rearrange("p (h d) -> p h d", h=NH),
                                   dec[:, c // TB, 2 + q, c % TB, :].unsqueeze(2).to_broadcast([P, NH, HD]),
                                   ALU.mult).then_inc(s_sdec, 1)

            def gated(c):
                pool.wait_ge(s_ydx, c + 1)
                pool.wait_ge(s_zs, MD * (c // TB + 1))
                if c >= 2:
                    pool.wait_ge(p_out, c - 1)
                pool.tensor_tensor(yg[:, c % 2, :, :], ydx[:, c % 2, :, :], zs[:, :, tok(c)], ALU.mult).then_inc(s_yg, 1)

            pool.wait_ge(s_dt, 1)
            masked_a(0)
            masked_a(1)

            def gated_shared_weights(b):
                pool.wait_ge(s_rowin, 16)
                pool.wait_ge(s_sh2, 32)
                pool.wait_ge(s_pad, 1)
                pool.tensor_tensor(shw2g[:, b, :, :], shw2[:, :, :],
                                   mrow[:, b, GB - GA, :].unsqueeze(1).to_broadcast([P, JH, D]),
                                   ALU.mult).then_inc(s_shg, 1)

            def rrms(c):
                pool.wait_ge(s_rv, c + 1)
                pool.tensor_tensor(rr[:, c:c + 1], rv[:, c:c + 1], neg_half[:, 0:1], ALU.pow).then_inc(s_rr, 1)

            def norm2(c):
                pool.wait_ge(s_ve2, c + 1)
                pool.tensor_tensor(rstd2[:, c:c + 1], ve2[:, c:c + 1], neg_half[:, 0:1], ALU.pow).then_inc(s_rstd2, 1)

            def scatter(b):
                pool.wait_ge(s_dest, b + 1)
                pool.wait_ge(s_zeroed, 16 * NE)
                for t in range(b * TB, (b + 1) * TB):
                    pool.indirect_dma_start(out=xd, out_offset=bass.IndirectOffsetOnAxis(ap=dest[:, t:t + 1], axis=0),
                                            in_=h2[:, t, :], in_offset=None).then_inc(s_scat, 16)

            rest_decay(0)
            rest_decay(1)
            for c in range(NT):
                decayed_state(c, 1)
                if c + 1 < NT:
                    if c == 0:
                        decayed_state(1, 0)
                        masked_a(2)
                    else:
                        if c + 2 < NT:
                            masked_a(c + 2)
                        decayed_state(c + 1, 0)
                        rest_decay(c + 1)
                if c >= 2:
                    rrms(c - 2)
                if c >= 1:
                    gated(c - 1)
                if c >= 2:
                    norm2(c - 2)
                if 2 <= c < 2 + NB:
                    gated_shared_weights(c - 2)
            rrms(NT - 2)
            gated(NT - 1)
            norm2(NT - 2)
            rrms(NT - 1)
            norm2(NT - 1)
            scatter(0)
            scatter(1)
            pool.wait_ge(s_oeout, 16 * NE)
            for t in range(NT):
                pool.indirect_dma_start(out=gath[:, t, :], out_offset=None, in_=oe,
                                        in_offset=bass.IndirectOffsetOnAxis(ap=src[:, t:t + 1], axis=0)).then_inc(s_gath[t], 16)

        @block.scalar
        def _(act):
            act.wait_ge(s_pack, 16)
            act.activation(sc[:, :], pk[:, C_C:C_C + KD * NB], ACT.Silu).then_inc(s_sc, 1)
            act.wait_ge(s_mcol, 1)

            def hT_out(b):
                act.wait_ge(p_hT, b + 1)
                for k in range(KD):
                    act.activation(hT[:, k, seq(b)], bank[k], ACT.Identity,
                                   bias=mcol[:, (SA * NB + b) * KD + k:(SA * NB + b) * KD + k + 1],
                                   scale=mcol[:, (CA * NB + b) * KD + k:(CA * NB + b) * KD + k + 1]).then_inc(s_hT, 1)

            def first_tap(b, m):
                n, i = place(b, m), b * MC + m
                act.wait_ge(p_proj, n + 1)
                if i >= 3:
                    act.wait_ge(s_xc, i - 2)
                act.activation(acc[:, i % 3, :], bank[proj_bank[n % 4]], ACT.Identity,
                               bias=pk[:, C_CB + m:C_CB + m + 1],
                               scale=pk[:, C_CW + m * TAPS + TAPS - 1:C_CW + m * TAPS + TAPS]).then_inc(s_tap, 1)

            def conv_silu(i):
                b, m = divmod(i, MC)
                act.wait_ge(s_conv, i + 1)
                act.activation(xcT[:, m, seq(b)], acc[:, i % 3, :], ACT.Silu).then_inc(s_xc, 1)

            def z_silu(b, m):
                n = place(b, MC + m)
                act.wait_ge(p_proj, n + 1)
                act.activation(zs[:, m, seq(b)], bank[proj_bank[n % 4]], ACT.Silu).then_inc(s_zs, 1)

            hT_out(0)
            for b in range(NB):
                for q in PROJ:
                    i = b * MC + q
                    if q >= MC:
                        z_silu(b, q - MC)
                        if b == NB - 1 and q == MC + MD - 2:
                            conv_silu(NB * MC - 2)
                        continue
                    if i >= 2:
                        conv_silu(i - 2)
                    first_tap(b, q)
                    if i == 1:
                        hT_out(1)
                    if i == 3:
                        act.wait_ge(p_mt, 1)
                        for k in range(2):
                            act.activation(mrow_sb[:, 2 * k:2 * k + 2, :].rearrange("b q d -> b (q d)"),
                                           bank[k][0:NB, :], ACT.Copy).then_inc(s_mraw, 1)
            conv_silu(NB * MC - 1)

            def decays(b):
                act.wait_ge(p_small, b + 1)
                act.activation(dec[:, b, :, :, :].rearrange("p q t h -> p (q t h)"), small_ps, ACT.Exp).then_inc(s_dec, 1)

            def decay_matrix(c):
                act.wait_ge(p_seg, c + 1)
                if c >= 2:
                    act.wait_ge(p_yd, c - 1)
                act.activation(lm[:, c % 2, :, :].rearrange("p h l -> p (h l)"),
                               bank[SEG], ACT.Exp).then_inc(s_l, 1)

            def b_tokens(c):
                act.wait_ge(p_bg, c + 1)
                if c >= 2:
                    act.wait_ge(p_st, NQ * (c - 1))
                act.activation(btok[:, c % 2, :], b_ps, ACT.Copy).then_inc(s_btok, 1)

            def heads_scaled(out, ps, scale):
                for h in range(NH):
                    cols = slice(h * HD, (h + 1) * HD)
                    ins = act.activation(out[:, cols], ps[:, cols], ACT.Copy, scale=scale[:, h:h + 1])
                return ins

            def y_off(c):
                act.wait_ge(p_yoff, c + 1)
                if c >= 1:
                    act.wait_ge(s_y, c)
                heads_scaled(yoff, bank[YOFF], dec[:, c // TB, 0, c % TB, :]).then_inc(s_yoffe, 1)

            def y_squared(c):
                act.wait_ge(s_yg, c + 1)
                if c >= 2:
                    act.wait_ge(s_sqs, c - 1)
                act.activation(sq[:, c % 2, :, :].rearrange("p m n -> p (m n)"),
                               yg[:, c % 2, :, :].rearrange("p m n -> p (m n)"), ACT.Square).then_inc(s_sq, 1)

            def h2T_out(t):
                act.wait_ge(p_h2T, t + 1)
                act.activation(h2T[:, :, tok(t)], h2T_ps.rearrange("p (k n) -> p k n", k=KD), ACT.Copy).then_inc(s_h2T, 1)

            def up_silu(u):
                kind, e, j = UPS[u]
                act.wait_ge(p_up, u + 1)
                if u >= 2:
                    act.wait_ge(s_act, u - 1)
                n = L if kind == "shared" else JH * P
                act.activation(sg[:, u % 2, 0:n], bank[up_bank[u % 2][0]][:, 0:n], ACT.Silu).then_inc(s_sg, 1)

            def slots_T(e):
                act.wait_ge(p_xdT, e + 1)
                if e >= 2:
                    act.wait_ge(p_up, NSH + e - 1)
                act.activation(xdT[:, e % 2, :, :].rearrange("p k n -> p (k n)"),
                               bank[xdT_bank[e % 2]][:, 0:KD * P], ACT.Copy).then_inc(s_xdT, 1)

            decays(0)
            b_tokens(0)
            decay_matrix(0)
            for c in range(NT):
                if c + 1 == TB:
                    decays(1)
                if c + 1 < NT:
                    b_tokens(c + 1)
                    decay_matrix(c + 1)
                if c >= 3:
                    h2T_out(c - 3)
                y_off(c)
                if c >= 1:
                    y_squared(c - 1)
            y_squared(NT - 1)
            up_silu(0)
            h2T_out(NT - 3)
            h2T_out(NT - 2)
            up_silu(1)
            h2T_out(NT - 1)
            for u in range(2, NSH):
                up_silu(u)
            slots_T(0)
            for e in range(NE):
                if e + 1 < NE:
                    slots_T(e + 1)
                up_silu(NSH + e)
            act.wait_ge(s_sh, NB)
            act.activation(ex[:, :, :].rearrange("p t e -> p (t e)"), sh[:, :, :].rearrange("p t e -> p (t e)"),
                           ACT.Exp).then_inc(s_ex, 1)

        @block.vector
        def _(dve):
            vec = nc.vector
            chained = [0]

            def then_wait(ins):
                chained[0] += 1
                ins.then_inc(s_vc, 1)
                dve.wait_ge(s_vc, chained[0])

            def norm1(b):
                for t in range(b * TB, (b + 1) * TB):
                    dve.wait_ge(s_x[t], 16)
                    ins = vec.bn_stats(stats[:, t, :], xs[:, t, :])
                then_wait(ins)
                for t in range(b * TB, (b + 1) * TB):
                    ins = vec.bn_aggr(mv[:, t, :], stats[:, t, :])
                then_wait(ins)
                bt = slice(b * TB, (b + 1) * TB)
                vec.tensor_scalar(ve[:, bt], mv[:, bt, 1], EPS, None, ALU.add).then_inc(s_ve, 1)
                dve.wait_ge(s_rstd, b + 1)
                for t in range(b * TB, (b + 1) * TB):
                    vec.tensor_scalar(xn[:, t, :], xs[:, t, :], mv[:, t, 0:1], rstd[:, t:t + 1],
                                      ALU.subtract, ALU.mult).then_inc(s_xn, 1)

            def conv(b, m):
                n, i = place(b, m), b * MC + m
                dve.wait_ge(s_tap, i + 1)
                ps = bank[proj_bank[n % 4]]
                for s in range(1, TAPS):
                    w = C_CW + m * TAPS + TAPS - 1 - s
                    ins = vec.scalar_tensor_tensor(acc[:, i % 3, s:L], ps[:, 0:L - s], pk[:, w:w + 1],
                                                   acc[:, i % 3, s:L], ALU.mult, ALU.add)
                    if s < TAPS - 1:
                        then_wait(ins)
                ins.then_inc(s_conv, 1)

            norm1(0)
            dve.wait_ge(p_mc, 1)
            then_wait(vec.tensor_copy(mcol[:, :].rearrange("p (q b k) -> p q b k", b=NB, k=KD),
                                      mc_ps.rearrange("p (q k b) -> p q b k", b=NB, k=KD)))
            vec.tensor_scalar(mcol[:, CA * 4:CA * 4 + 4], mcol[:, CA * 4:CA * 4 + 4], 1.0, None,
                              ALU.add).then_inc(s_mcol, 1)
            norm1(1)
            conv(0, 0)
            conv(0, 1)

            dve.wait_ge(p_dt, 1)
            then_wait(vec.tensor_tensor(v[:, :].rearrange("p (t h) -> p t h", h=NH),
                                        dt_ps.rearrange("p (t h) -> p t h", h=NH),
                                        pk[:, C_DB:C_DB + NH].unsqueeze(1).to_broadcast([P, NT, NH]), ALU.add))
            vec.scalar_tensor_tensor(nabs[:, :], v[:, :], -1.0, v[:, :], ALU.mult, ALU.min).then_inc(s_nabs, 1)
            conv(0, 2)
            conv(0, 3)
            conv(0, 4)
            dve.wait_ge(s_en, 1)
            then_wait(vec.tensor_scalar(zz[:, :], en[:, :], 2.0, None, ALU.add))
            then_wait(vec.reciprocal(zz[:, :], zz[:, :]))
            then_wait(vec.tensor_tensor(zz[:, :], zz[:, :], en[:, :], ALU.mult))
            then_wait(vec.tensor_tensor(z2[:, :], zz[:, :], zz[:, :], ALU.mult))
            then_wait(vec.tensor_scalar(pp[:, :], z2[:, :], 1.0 / 17, None, ALU.mult))
            conv(0, 5)
            for k in (15, 13, 11, 9, 7, 5, 3):
                then_wait(vec.scalar_tensor_tensor(pp[:, :], pp[:, :], 1.0 / k, z2[:, :], ALU.add, ALU.mult))
            then_wait(vec.scalar_tensor_tensor(pp[:, :], pp[:, :], 1.0, zz[:, :], ALU.add, ALU.mult))
            then_wait(vec.tensor_scalar(v[:, :], v[:, :], 0.0, None, ALU.max))
            dtf = dt[:, :, :].rearrange("p t h -> p (t h)")
            then_wait(vec.scalar_tensor_tensor(dtf, pp[:, :], 2.0, v[:, :], ALU.mult, ALU.add))
            dve.wait_ge(s_expa, 1)
            vec.scalar_tensor_tensor(a[:, :, :], dt[:, :, :], -1.0, expa[:, :].unsqueeze(1).to_broadcast([P, NT, NH]),
                                     ALU.mult, ALU.mult).then_inc(s_dt, 1)
            for m in range(MC):
                conv(1, m)

            def gated_out_weights(b):
                dve.wait_ge(s_rowin, 16)
                dve.wait_ge(s_wo, 16)
                for m in range(MD):
                    vec.scalar_tensor_tensor(wog[:, b, m, :], wo[:, m, :], pk[:, C_NW + m:C_NW + m + 1],
                                             mrow[:, b, 0, :], ALU.mult, ALU.mult).then_inc(s_wog, 1)

            def x_dt(c):
                dve.wait_ge(p_xtok, c + 1)
                if c >= 2:
                    dve.wait_ge(p_yd, c - 1)
                    dve.wait_ge(s_xdd, c - 1)
                vec.tensor_tensor(xdt[:, c % 2, :].rearrange("p (h d) -> p h d", h=NH),
                                  bank[X].rearrange("p (h d) -> p h d", h=NH),
                                  dt[:, c, :].unsqueeze(2).to_broadcast([P, NH, HD]), ALU.mult).then_inc(s_xdt, 1)

            def g_masked(c):
                dve.wait_ge(s_btok, c + 1)
                vec.tensor_tensor(gm[:, c % 2, :], g_ps, le[:, :], ALU.mult).then_inc(s_gm, 1)

            def m_matrix(c):
                dve.wait_ge(s_l, c + 1)
                dve.wait_ge(s_gm, c + 1)
                vec.tensor_tensor(lm[:, c % 2, :, :], lm[:, c % 2, :, :],
                                  gm[:, c % 2, :].unsqueeze(1).to_broadcast([P, NH, Q]), ALU.mult).then_inc(s_m, 1)

            def y_sum(c):
                dve.wait_ge(s_yoffe, c + 1)
                dve.wait_ge(p_yd, c + 1)
                if c >= 2:
                    dve.wait_ge(p_yT, c - 1)
                vec.tensor_tensor(y[:, c % 2, :], yoff, bank[YD], ALU.add).then_inc(s_y, 1)

            def state(c, q):
                dve.wait_ge(p_st, NQ * c + q + 1)
                if c >= 2:
                    dve.wait_ge(p_yoff, c - 1)
                if c % TB == 0 and q == 0:
                    vec.tensor_copy(st[:, c % 2, q, :], bank[ST]).then_inc(s_st, 1)
                    return
                dve.wait_ge(s_sdec, decays_before(c, q))
                vec.tensor_tensor(st[:, c % 2, q, :], stdec[:, q, :], bank[ST], ALU.add).then_inc(s_st, 1)

            def y_plus_dx(c):
                dve.wait_ge(p_yT, c + 1)
                if c >= 2:
                    dve.wait_ge(s_yg, c - 1)
                for m in range(MD):
                    ins = vec.scalar_tensor_tensor(ydx[:, c % 2, m, :], xcT[:, m, tok(c)], pk[:, C_D + m:C_D + m + 1],
                                                   bank[YT][:, m * P:(m + 1) * P], ALU.mult, ALU.add)
                ins.then_inc(s_ydx, 1)

            def squares_summed(t):
                dve.wait_ge(s_sq, t + 1)
                if t >= 2:
                    dve.wait_ge(p_ssq, t - 1)
                vec.tensor_reduce(sqs[:, t % 2, :], sq[:, t % 2, :, :].rearrange("p m n -> p n m"),
                                  AX.X, ALU.add).then_inc(s_sqs, 1)

            def mean_square(t):
                dve.wait_ge(p_ssq, t + 1)
                vec.tensor_scalar(rv[:, t:t + 1], ssq_ps[:, t:t + 1], 1.0 / DI, EPS, ALU.mult, ALU.add).then_inc(s_rv, 1)

            def x1_stats(t):
                dve.wait_ge(s_rr, t + 1)
                vec.scalar_tensor_tensor(xs[:, t, :], out_ps, rr[:, t:t + 1], xs[:, t, :],
                                         ALU.mult, ALU.add).then_inc(s_x1, 1)
                dve.wait_ge(s_x1, t + 1)
                then_wait(vec.bn_stats(stats2[:, :], xs[:, t, :]))
                then_wait(vec.bn_aggr(mv2[:, t, :], stats2[:, :]))
                vec.tensor_scalar(ve2[:, t:t + 1], mv2[:, t, 1:2], EPS, None, ALU.add).then_inc(s_ve2, 1)
                vec.scalar_tensor_tensor(cent[:, :], xs[:, t, :], mv2[:, t, 0:1], mrow[:, t // TB, CB - GA, :],
                                         ALU.subtract, ALU.mult).then_inc(s_cent, 1)

            def h2_rows(t):
                dve.wait_ge(s_cent, t + 1)
                dve.wait_ge(s_rstd2, t + 1)
                vec.scalar_tensor_tensor(h2[:, t, :], cent[:, :], rstd2[:, t:t + 1], mrow[:, t // TB, SB - GA, :],
                                         ALU.mult, ALU.add).then_inc(s_h2, 1)

            def route(b):
                ts, n = slice(b * TB, (b + 1) * TB), [P, TB, NE]
                lg = lg_ps.rearrange("p (t e) -> p t e", e=NE)[:, ts, :]
                dve.wait_ge(p_lg, (b + 1) * TB)
                if b == 0:
                    dve.wait_ge(s_h2T, TB + 1)
                then_wait(vec.tensor_reduce(mx[:, ts], lg, AX.X, ALU.max))
                ins = vec.tensor_tensor(sh[:, ts, :], lg, mx[:, ts].unsqueeze(2).to_broadcast(n), ALU.subtract)
                ins.then_inc(s_sh, 1)
                dve.wait_ge(s_sh, b + 1)
                then_wait(vec.scalar_tensor_tensor(cand[:, ts, :], sh[:, ts, :], 0.0, rank[:, :, :], ALU.is_ge, ALU.mult))
                then_wait(vec.tensor_reduce(best[:, ts], cand[:, ts, :], AX.X, ALU.max))
                then_wait(vec.tensor_tensor(oh[:, ts, :], cand[:, ts, :], best[:, ts].unsqueeze(2).to_broadcast(n), ALU.is_equal))
                for t in range(b * TB, (b + 1) * TB):
                    if t == 0:
                        ins = vec.memset(pre[:, 0, :], 0.0)
                    else:
                        ins = vec.tensor_tensor(pre[:, t, :], pre[:, t - 1, :], oh[:, t - 1, :], ALU.add)
                    if t % TB < TB - 1:
                        then_wait(ins)
                ins.then_inc(s_oh, 1)
                then_wait(vec.tensor_tensor(offs[:, ts, :], oh[:, ts, :], slot0[:, :, :], ALU.mult))
                then_wait(vec.tensor_reduce(off[:, ts], offs[:, ts, :], AX.X, ALU.add))

            def slots(b):
                ts = slice(b * TB, (b + 1) * TB)
                dve.wait_ge(p_pos, b + 1)
                then_wait(vec.tensor_tensor(cnts[:, ts, :], pos_ps.rearrange("p (t e) -> p t e", e=NE)[:, ts, :],
                                            oh[:, ts, :], ALU.mult))
                then_wait(vec.tensor_reduce(cnt[:, ts], cnts[:, ts, :], AX.X, ALU.add))
                vec.tensor_scalar(keep[:, ts], cnt[:, ts], float(CAP), None, ALU.is_le)
                then_wait(vec.tensor_tensor(flat[:, ts], cnt[:, ts], off[:, ts], ALU.add))
                then_wait(vec.tensor_tensor(dlt[:, ts], flat[:, ts], spill[:, ts], ALU.subtract))
                then_wait(vec.tensor_tensor(dlt[:, ts], dlt[:, ts], keep[:, ts], ALU.mult))
                vec.tensor_tensor(src[:, ts], flat[:, ts], keep[:, ts], ALU.mult)
                vec.tensor_tensor(dest[:, ts], dlt[:, ts], spill[:, ts], ALU.add).then_inc(s_dest, 1)

            dve.wait_ge(s_const, 1)
            x_dt(0)
            g_masked(0)
            x_dt(1)
            g_masked(1)
            state(0, 0)
            for c in range(NT):
                m_matrix(c)
                state(c, 1)
                if 0 < c < NT - 1:
                    x_dt(c + 1)
                    g_masked(c + 1)
                if c < NB:
                    gated_out_weights(c)
                if c >= 2:
                    squares_summed(c - 2)
                if c >= 1:
                    y_plus_dx(c - 1)
                if c >= 2:
                    mean_square(c - 2)
                    x1_stats(c - 2)
                if c + 1 < NT:
                    state(c + 1, 0)
                if c >= 2:
                    h2_rows(c - 2)
                y_sum(c)

            def up_act(u):
                kind, e, j = UPS[u]
                dve.wait_ge(s_sg, u + 1)
                g, w = bank[up_bank[u % 2][1]], sg[:, u % 2, :]
                if kind == "shared":
                    vec.tensor_tensor(shact[:, j, seq(e)], w, g, ALU.mult).then_inc(s_act, 1)
                else:
                    if e >= 2:
                        dve.wait_ge(p_dn, e - 1)
                    vec.tensor_tensor(eact[:, e % 2, :, :].rearrange("p j n -> p (j n)"), w[:, 0:JH * P],
                                      g[:, 0:JH * P], ALU.mult).then_inc(s_act, 1)

            squares_summed(NT - 2)
            y_plus_dx(NT - 1)
            mean_square(NT - 2)
            route(0)
            x1_stats(NT - 2)
            squares_summed(NT - 1)
            h2_rows(NT - 2)
            up_act(0)
            mean_square(NT - 1)
            x1_stats(NT - 1)
            h2_rows(NT - 1)
            slots(0)
            up_act(1)
            route(1)
            slots(1)
            for u in range(2, NSH):
                up_act(u)
            for e in range(NE + 1):
                if e < NE:
                    up_act(NSH + e)
                if e >= 1:
                    dve.wait_ge(p_dn, e)
                    vec.tensor_copy(oes[:, e - 1, :], bank[down_bank[(e - 1) % 2]][:, 0:D]).then_inc(s_oes, 1)
            def shared_added(t):
                dve.wait_ge(p_sd, t + 1)
                vec.tensor_tensor(res[:, t, :], xs[:, t, :], bank[sd_bank[t % 4]][:, 0:D], ALU.add).then_inc(s_pre, 1)

            for t in range(2):
                shared_added(t)
            dve.wait_ge(s_ex, 1)
            then_wait(vec.tensor_reduce(es[:, :], ex[:, :, :], AX.X, ALU.add))
            then_wait(vec.reciprocal(gate[:, :], es[:, :]))
            then_wait(vec.tensor_tensor(gate[:, :], gate[:, :], keep[:, :], ALU.mult))
            shared_added(2)
            for t in range(NT):
                dve.wait_ge(s_gath[t], 16)
                then_wait(vec.scalar_tensor_tensor(gath[:, t, :], gath[:, t, :], gate[:, t:t + 1],
                                                   mrow[:, t // TB, GB - GA, :], ALU.mult, ALU.mult))
                dve.wait_ge(s_pre, t + 1)
                vec.tensor_tensor(res[:, t, :], res[:, t, :], gath[:, t, :], ALU.add).then_inc(s_fin, 1)
                if t + 3 < NT:
                    shared_added(t + 3)

        @block.tensor
        def _(pe):
            mm = pe.matmul
            pe.wait_ge(s_sc, 1)

            def transposed_x(b):
                if b:
                    pe.wait_ge(s_hT, KD)
                for i in range(TB):
                    pe.wait_ge(s_xn, b * TB + i + 1)
                    for k in range(KD):
                        ins = pe.transpose(bank[k][:, i * P:(i + 1) * P], xn[:, b * TB + i, k * P:(k + 1) * P], ident[:, :])
                ins.then_inc(p_hT, 1)

            def wait_read(n):
                b, i = divmod(n, NPROJ)
                if PROJ[i] < MC:
                    pe.wait_ge(s_conv, b * MC + PROJ[i] + 1)
                else:
                    pe.wait_ge(s_zs, b * MD + PROJ[i] - MC + 1)

            def project(b, q):
                n = place(b, q)
                col = DI + q * P if q < MC else (q - MC) * P
                if n >= 4:
                    wait_read(n - 4)
                for k in range(KD):
                    ins = mm(bank[proj_bank[n % 4]], win[:, k, col:col + P], hT[:, k, seq(b)],
                             start=(k == 0), stop=(k == KD - 1))
                ins.then_inc(p_proj, 1)

            pe.wait_ge(s_wma, 16)
            for j in range(2 * KD):
                for k in range(KD):
                    ins = mm(mc_ps[:, j * NB:(j + 1) * NB], wm[:, k, j * P:(j + 1) * P], sc[:, k * NB:(k + 1) * NB],
                             start=(k == 0), stop=(k == KD - 1))
            ins.then_inc(p_mc, 1)
            pe.wait_ge(s_const, 1)
            transposed_x(0)
            pe.wait_ge(s_hT, KD)
            pe.wait_ge(s_winx, 16)
            project(0, PROJ[0])
            project(0, PROJ[1])
            transposed_x(1)
            pe.wait_ge(s_winz, 16)
            project(0, PROJ[2])
            project(0, PROJ[3])
            pe.wait_ge(s_hT, NB * KD)
            for t in range(NT):
                for k in range(KD):
                    ins = mm(dt_ps[:, t * NH:(t + 1) * NH], hT[:, k, tok(t)], win[:, k, DPROJ - NH:DPROJ],
                             start=(k == 0), stop=(k == KD - 1))
            ins.then_inc(p_dt, 1)
            pe.wait_ge(s_wmb, 16)
            for i in range(2):
                for k in range(KD):
                    ins = mm(bank[i][0:NB, :], sc[:, k * NB:(k + 1) * NB], wm[:, k, 2 * D + i * 2 * D:4 * D + i * 2 * D],
                             start=(k == 0), stop=(k == KD - 1))
            ins.then_inc(p_mt, 1)
            for b in range(NB):
                for q in PROJ[4 if b == 0 else 0:]:
                    project(b, q)

            def small(b):
                if b == 0:
                    pe.wait_ge(s_dt, 1)
                    pe.wait_ge(s_mraw, 2)
                else:
                    pe.wait_ge(s_ydx, TB - 2)
                n = TB * NH
                rhs = a[:, b * TB:(b + 1) * TB, :].rearrange("p t h -> p (t h)")
                for q, lhs in enumerate((le2[:, :], gt2[:, :], half[:, 0, :], half[:, 1, :])):
                    ins = mm(small_ps[:, q * n:(q + 1) * n], lhs, rhs, start=True, stop=True)
                ins.then_inc(p_small, 1)

            def prep(c):
                b = c // TB
                pe.wait_ge(s_xc, MC * (b + 1))
                if c == 0:
                    for n in range(NB * NPROJ - 4, NB * NPROJ - 2):
                        wait_read(n)
                if c >= 1:
                    pe.wait_ge(s_xdt, c)
                for m in range(MD):
                    ins = pe.transpose(bank[X][:, m * P:(m + 1) * P], xcT[:, m, tok(c)], ident[:, :])
                ins.then_inc(p_xtok, 1)
                if c >= 1:
                    pe.wait_ge(s_gm, c)
                if c >= 5:
                    pe.wait_ge(s_h2T, c - 4)
                pe.transpose(b_ps, xcT[:, MD, tok(c)], ident[:, :])
                for q in range(NQ):
                    cols = slice(c * P + q * Q, c * P + (q + 1) * Q)
                    ins = mm(g_ps[q * Q:(q + 1) * Q, :], xcT[:, MD, cols], xcT[:, MD + 1, cols], start=True, stop=True)
                ins.then_inc(p_bg, 1)
                pe.wait_ge(s_al, c + 1)
                if c >= 1:
                    pe.wait_ge(s_l, c)
                mm(bank[SEG], gt2[:, :], al[:, c % 2, :, :].rearrange("p h l -> p (h l)"),
                   start=True, stop=True).then_inc(p_seg, 1)

            def state_sum(c, q):
                pe.wait_ge(s_btok, c + 1)
                pe.wait_ge(s_xdd, c + 1)
                if c >= 1 or q:
                    pe.wait_ge(s_st, NQ * c + q)
                rows = slice(q * Q, (q + 1) * Q)
                mm(bank[ST], btok[rows, c % 2, :], xdd[rows, c % 2, :], start=True, stop=True).then_inc(p_st, 1)

            def off_diagonal(c):
                if c == 0:
                    for n in range(NB * NPROJ - 2, NB * NPROJ):
                        wait_read(n)
                else:
                    pe.wait_ge(s_yoffe, c)
                for q in range(NQ):
                    rows = slice(q * Q, (q + 1) * Q)
                    pe.wait_ge(s_st, NQ * c + q + 1)
                    ins = mm(bank[YOFF][rows, :], xcT[:, MD + 1, c * P + q * Q:c * P + (q + 1) * Q], st[:, c % 2, q, :],
                             start=True, stop=True)
                ins.then_inc(p_yoff, 1)

            def diagonal(c):
                pe.wait_ge(s_m, c + 1)
                if c >= 1:
                    pe.wait_ge(s_y, c)
                for q in range(NQ):
                    rows = slice(q * Q, (q + 1) * Q)
                    for h in range(NH):
                        ins = mm(bank[YD][rows, h * HD:(h + 1) * HD], lm[rows, c % 2, h, :],
                                 xdt[rows, c % 2, h * HD:(h + 1) * HD], start=True, stop=True)
                ins.then_inc(p_yd, 1)

            def y_transposed(c):
                pe.wait_ge(s_y, c + 1)
                if c >= 1:
                    pe.wait_ge(s_ydx, c)
                if c == TB - 2:
                    pe.wait_ge(s_dec, NB)
                for m in range(MD):
                    ins = pe.transpose(bank[YT][:, m * P:(m + 1) * P], y[:, c % 2, m * P:(m + 1) * P], ident[:, :])
                ins.then_inc(p_yT, 1)

            def out_project(c):
                b = c // TB
                pe.wait_ge(s_wog, MD * (b + 1))
                if c >= 1:
                    pe.wait_ge(s_x1, c)
                pe.wait_ge(s_yg, c + 1)
                for m in range(MD):
                    ins = mm(out_ps, yg[:, c % 2, m, :], wog[:, b, m, :], start=(m == 0), stop=(m == MD - 1))
                ins.then_inc(p_out, 1)

            def sum_squares(c):
                pe.wait_ge(s_sqs, c + 1)
                if c >= 1:
                    pe.wait_ge(s_x1, c)
                mm(ssq_ps[:, c:c + 1], sqs[:, c % 2, :], ones[:, 0:1], start=True, stop=True).then_inc(p_ssq, 1)

            def h2_transposed(t):
                pe.wait_ge(s_h2, t + 1)
                pe.wait_ge(s_gm, min(t + 5, NT))
                if t >= 1:
                    pe.wait_ge(s_h2T, t)
                if t > TB:
                    pe.wait_ge(s_sh, 1)
                for k in range(KD):
                    ins = pe.transpose(h2T_ps[:, k * P:(k + 1) * P], h2[:, t, k * P:(k + 1) * P], ident[:, :])
                ins.then_inc(p_h2T, 1)

            def logits(t):
                pe.wait_ge(s_h2T, t + 1)
                pe.wait_ge(s_gm, min(t + 6, NT))
                if t >= TB:
                    pe.wait_ge(s_sh, 1)
                for k in range(KD):
                    ins = mm(lg_ps[:, t * NE:(t + 1) * NE], h2T[:, k, tok(t)], pk[:, C_WG + k * NE:C_WG + (k + 1) * NE],
                             start=(k == 0), stop=(k == KD - 1))
                ins.then_inc(p_lg, 1)

            def positions(b):
                pe.wait_ge(s_oh, b + 1)
                pe.wait_ge(s_y, NT)
                if b == 1:
                    pe.wait_ge(s_dest, 1)
                n = TB * NE
                ps = pos_ps[:, b * n:(b + 1) * n]
                ts = slice(b * TB, (b + 1) * TB)
                mm(ps, le_b[:, :], oh[:, ts, :].rearrange("p t e -> p (t e)"), start=True, stop=False)
                mm(ps, ones_b[:, :], pre[:, ts, :].rearrange("p t e -> p (t e)"), start=False, stop=True).then_inc(p_pos, 1)

            def up_shared(u, q):
                _, b, j = UPS[u]
                if q == 0:
                    if u == 0:
                        pe.wait_ge(s_shw, 32)
                        pe.wait_ge(s_l, NT)
                        pe.wait_ge(s_st, NQ * NT)
                    if u == 1:
                        pe.wait_ge(s_yoffe, NT)
                        pe.wait_ge(s_ydx, NT)
                    if u >= 2:
                        pe.wait_ge(s_act, u - 1)
                    pe.wait_ge(s_h2T, TB * (b + 1))
                w = (shw1, shw3)[q]
                for k in range(KD):
                    ins = mm(bank[up_bank[u % 2][q]], w[:, k, HJ[j]:HJ[j] + P], h2T[:, k, seq(b)],
                             start=(k == 0), stop=(k == KD - 1))
                if q:
                    ins.then_inc(p_up, 1)

            def slots_transposed(e):
                pe.wait_ge(s_xg[e // 2], 16)
                if e == 1:
                    pe.wait_ge(s_dest, NB)
                if e >= 2:
                    pe.wait_ge(s_xdT, e - 1)
                for k in range(KD):
                    ins = pe.transpose(bank[xdT_bank[e % 2]][:, k * P:(k + 1) * P],
                                       xg[:, e, k * P:(k + 1) * P], ident[:, :])
                ins.then_inc(p_xdT, 1)

            def up_expert(e):
                u = NSH + e
                pe.wait_ge(s_ew[e], 64)
                pe.wait_ge(s_xdT, e + 1)
                pe.wait_ge(s_act, u - 1)
                for q, w in enumerate((ew1, ew3)):
                    for j in range(JH):
                        for k in range(KD):
                            ins = mm(bank[up_bank[u % 2][q]][:, j * P:(j + 1) * P], w[:, e % EB, k, HJ[j]:HJ[j] + P],
                                     xdT[:, e % 2, k, :], start=(k == 0), stop=(k == KD - 1))
                ins.then_inc(p_up, 1)

            def down_expert(e):
                pe.wait_ge(s_act, NSH + e + 1)
                pe.wait_ge(s_pad, 1)
                if e >= 2:
                    pe.wait_ge(s_oes, e - 1)
                for j in range(JH):
                    ins = mm(bank[down_bank[e % 2]][:, 0:D], eact[:, e % 2, j, :], ew2[:, e % EB, j, :],
                             start=(j == 0), stop=(j == JH - 1))
                ins.then_inc(p_dn, 1)

            def down_shared(t):
                pe.wait_ge(s_shg, NB)
                pe.wait_ge(s_act, len(UPS))
                if t >= 4:
                    pe.wait_ge(s_pre, t - 3)
                for j in range(JH):
                    ins = mm(bank[sd_bank[t % 4]][:, 0:D], shact[:, j, tok(t)], shw2g[:, t // TB, j, :],
                             start=(j == 0), stop=(j == JH - 1))
                ins.then_inc(p_sd, 1)

            small(0)
            prep(0)
            prep(1)
            state_sum(0, 0)
            for c in range(NT):
                state_sum(c, 1)
                if 0 < c < NT - 1:
                    prep(c + 1)
                if c >= 1:
                    y_transposed(c - 1)
                if c >= 2:
                    out_project(c - 2)
                    sum_squares(c - 2)
                if c >= 4:
                    logits(c - 4)
                if c >= 3:
                    h2_transposed(c - 3)
                off_diagonal(c)
                if c + 1 < NT:
                    state_sum(c + 1, 0)
                diagonal(c)
                if c + 2 == TB:
                    small(1)
            out_project(NT - 2)
            y_transposed(NT - 1)
            sum_squares(NT - 2)
            up_shared(0, 0)
            up_shared(0, 1)
            logits(NT - 4)
            h2_transposed(NT - 3)
            out_project(NT - 1)
            sum_squares(NT - 1)
            logits(NT - 3)
            h2_transposed(NT - 2)
            positions(0)
            up_shared(1, 0)
            up_shared(1, 1)
            logits(NT - 2)
            h2_transposed(NT - 1)
            up_shared(2, 0)
            logits(NT - 1)
            up_shared(2, 1)
            up_shared(3, 0)
            positions(1)
            up_shared(3, 1)
            for u in range(4, NSH):
                for q in range(2):
                    up_shared(u, q)
            slots_transposed(0)
            for e in range(NE + 1):
                if e + 1 < NE:
                    slots_transposed(e + 1)
                if e < NE:
                    up_expert(e)
                if e >= 1:
                    down_expert(e - 1)
            for t in range(NT):
                down_shared(t)


def kernel(L0_attn_x, L0_attn_in_proj_w, L0_attn_conv_w, L0_attn_conv_b, L0_attn_A_log, L0_attn_D,
           L0_attn_dt_bias, L0_attn_norm_w, L0_attn_out_proj_w, L0_ffn_Wg, L0_ffn_W1, L0_ffn_W3,
           L0_ffn_W2, L0_ffn_sw1, L0_ffn_sw3, L0_ffn_sw2, L0_c, L0_wmod):
    import numpy as np
    import concourse.bacc as bacc
    from concourse.bass_utils import run_bass_kernel_spmd

    def blocks(m):
        m = np.asarray(m)
        m = m.reshape(-1, P, int(np.prod(m.shape[1:])) if m.ndim > 1 else 1)
        return m.transpose(1, 0, 2).reshape(P, -1)

    pack = np.concatenate([
        blocks(L0_attn_conv_w), blocks(L0_attn_conv_b), blocks(L0_attn_norm_w),
        blocks(np.repeat(np.asarray(L0_attn_D), HD)),
        np.broadcast_to(np.asarray(L0_attn_A_log), (P, NH)), np.broadcast_to(np.asarray(L0_attn_dt_bias), (P, NH)),
        blocks(np.asarray(L0_c).T), blocks(L0_ffn_Wg)], axis=1)
    ins = {
        "x": L0_attn_x, "in_w": np.asarray(L0_attn_in_proj_w).T, "out_w": np.asarray(L0_attn_out_proj_w).T,
        "pack": pack, "wmod": L0_wmod, "w1": L0_ffn_W1, "w3": L0_ffn_W3, "w2": L0_ffn_W2,
        "sw1": L0_ffn_sw1, "sw3": L0_ffn_sw3, "sw2": L0_ffn_sw2,
    }
    nc = bacc.Bacc("TRN2", target_bir_lowering=False, num_devices=1)
    arrays, aps = {}, {}
    for name, value in ins.items():
        value = np.ascontiguousarray(value)
        arrays[f"in_{name}"] = value
        aps[name] = nc.dram_tensor(f"in_{name}", value.shape, mybir.dt.from_np(value.dtype), kind="ExternalInput").ap()
    aps["out"] = nc.dram_tensor("out_x", (NB, L, D), mybir.dt.float32, kind="ExternalOutput").ap()
    build(nc, **aps)
    return run_bass_kernel_spmd(nc, [arrays], core_ids=[0]).results[0]["out_x"]
```

```python
from contextlib import ExitStack

import concourse.bass as bass
from concourse import mybir

P = 128
D = 256
KD = D // P
NB = 2
L = 512
NT = NB * L // P
TB = L // P
DI = 512
MD = DI // P
NH = 8
HD = DI // NH
NS = 128
Q = 64
NQ = P // Q
TAPS = 4
MC = MD + 2
DPROJ = 2 * DI + 2 * NS + NH
NE = 8
EB = 4
DB = 3
CAP = NB * L // NE
HID = 352
JH = 3
HJ = [0, P, HID - P]
DUP = HJ[1] + P - HJ[2]
EPS = 1e-5

C_CW = 0
C_CB = C_CW + MC * TAPS
C_NW = C_CB + MC
C_D = C_NW + MD
C_AL = C_D + MD
C_DB = C_AL + NH
C_C = C_DB + NH
C_WG = C_C + KD * NB
NPACK = C_WG + KD * NE

SA, CA, GA, SB, CB, GB = range(6)


def build(nc, x, in_w, out_w, pack, wmod, w1, w3, w2, sw1, sw3, sw2, out):
    f32, f32r, bf16, i32 = mybir.dt.float32, mybir.dt.float32r, mybir.dt.bfloat16, mybir.dt.int32
    ALU, ACT, AX = mybir.AluOpType, mybir.ActivationFunctionType, mybir.AxisListType

    mod_rows = nc.dram_tensor("mod_rows", (NB, 4, D), f32, kind="Internal").ap()
    xd = nc.dram_tensor("xd", (NE * CAP + NB * L, D + 1), f32, kind="Internal").ap()
    oe = nc.dram_tensor("oe", (NB * L + NE * CAP, D), f32, kind="Internal").ap()

    with ExitStack() as ctx:
        def sb(name, shape, dt=f32):
            return ctx.enter_context(nc.sbuf_tensor(name, shape, dt))

        def sem(name):
            return ctx.enter_context(nc.semaphore(name))

        ident = sb("ident", [P, P])
        ones = sb("ones", [P, P])
        le = sb("le", [P, Q])
        le2 = sb("le2", [P, P])
        gt2 = sb("gt2", [P, P])
        half = sb("half", [P, NQ, P])
        le_b = sb("le_b", [P, P], bf16)
        ones_b = sb("ones_b", [P, P], bf16)
        neg_half = sb("neg_half", [P, NH])
        euler = sb("euler", [P, NT * NH])
        rank = sb("rank", [P, TB, NE])
        slot0 = sb("slot0", [P, TB, NE])
        spill = sb("spill", [P, NT])
        pk = sb("pk", [P, NPACK])
        xs = sb("xs", [P, NT, D])
        wm = sb("wm", [P, KD, 6 * D])
        shw1 = sb("shw1", [P, KD, HID])
        shw3 = sb("shw3", [P, KD, HID])
        shw2 = sb("shw2", [P, JH, D])
        ew1 = sb("ew1", [P, EB, KD, HID])
        ew3 = sb("ew3", [P, EB, KD, HID])
        empty = ew1[:, :, :, :].rearrange("p q k n -> p (q k n)")[:, 0:NE * (D + 1)].rearrange("p (e d) -> p e d", e=NE)
        ew2 = sb("ew2", [P, DB, JH, D])
        sc = sb("sc", [P, KD * NB])
        mcol = sb("mcol", [P, 2 * NB * KD])
        mrow = sb("mrow", [P, NB, 4, D])
        shw2g = sb("shw2g", [P, NB, JH, D])
        stats = sb("stats", [P, NT, 6])
        stats2 = sb("stats2", [P, 6])
        mv = sb("mv", [P, NT, 2])
        ve = sb("ve", [P, NT])
        rstd = sb("rstd", [P, NT])
        mv2 = sb("mv2", [P, NT, 2])
        ve2 = sb("ve2", [P, NT])
        rstd2 = sb("rstd2", [P, NT])
        xn_id = sb("xn_id", [P, NT, D + 1])
        xn = xn_id[:, :, 0:D]
        h2 = xn
        cent = sb("cent", [P, D])
        hT = sb("hT", [P, KD, NB * L])
        acc = sb("acc", [P, 3, L])
        xcT = sb("xcT", [P, MC, NB * L])
        zs = sb("zs", [P, MD, NB * L])
        NDT = NT * NH
        v = sb("v", [P, NDT])
        nabs = sb("nabs", [P, NDT])
        en = sb("en", [P, NDT])
        zz = sb("zz", [P, NDT])
        z2 = sb("z2", [P, NDT])
        pp = sb("pp", [P, NDT])
        dt = sb("dt", [P, NT, NH])
        expa = sb("expa", [P, NH])
        a = sb("a", [P, NT, NH])
        dec = sb("dec", [P, NB, 2 + NQ, TB, NH])
        wm_flat = wm[:, :, :].rearrange("p k n -> p (k n)")
        lm = wm_flat[:, 0:2 * NH * Q].rearrange("p (r h l) -> p r h l", r=2, h=NH)
        xdt = wm_flat[:, 2 * DI:4 * DI].rearrange("p (r n) -> p r n", r=2)
        stdec = wm_flat[:, 4 * DI:6 * DI].rearrange("p (q n) -> p q n", q=NQ)
        rv = sb("rv", [P, NT])
        rr = sb("rr", [P, NT])
        h2T = hT
        mx = sb("mx", [P, NT])
        sh = sb("sh", [P, NT, NE])
        cand = sb("cand", [P, NT, NE])
        best = sb("best", [P, NT])
        oh = sb("oh", [P, NT, NE], bf16)
        pre = sb("pre", [P, NT, NE], bf16)
        offs = sb("offs", [P, NT, NE])
        off = sb("off", [P, NT])
        cnts = sb("cnts", [P, NT, NE])
        cnt = sb("cnt", [P, NT])
        keep = sb("keep", [P, NT])
        flat = sb("flat", [P, NT])
        dlt = sb("dlt", [P, NT])
        dest = sb("dest", [P, NT], i32)
        slot_tok = sb("slot_tok", [P, NE], i32)
        ex = sb("ex", [P, NT, NE])
        es = sb("es", [P, NT])
        gate = sb("gate", [P, NT])
        sg = acc
        shact = wm_flat.rearrange("p (j n) -> p j n", j=JH)
        xg_id = zs[:, :, :].rearrange("p m n -> p (m n)")[:, 0:NE * (D + 1)].rearrange("p (e d) -> p e d", e=NE)
        xg = xg_id[:, :, 0:D]
        POOL_TILES = [2, 4, 6]
        DVE_TILES = [t for t in range(NT) if t not in POOL_TILES]
        at = NE * (D + 1)
        eact = zs[:, :, :].rearrange("p m n -> p (m n)")[:, at:at + 2 * HID].rearrange("p (r n) -> p r n", r=2)
        gated_gb = zs[:, 3, 0:len(POOL_TILES) * D].rearrange("p (i d) -> p i d", d=D)
        oes = xcT[:, 4:6, :].rearrange("p m (e d) -> p (m e) d", d=D)
        routed = xcT[:, 0:2, :].rearrange("p m (t d) -> p (m t) d", d=D)
        res = xcT[:, 2:4, :].rearrange("p m (t d) -> p (m t) d", d=D)
        with ExitStack() as mixer:
            def sb_mixer(name, shape, dt=f32):
                return mixer.enter_context(nc.sbuf_tensor(name, shape, dt))

            win = sb_mixer("win", [P, KD, DPROJ])
            wo = sb_mixer("wo", [P, MD, D])
            wog = sb_mixer("wog", [P, NB, MD, D])
            alh, alr = (sb_mixer(name, [P, 2, NH, Q], f32r) for name in ("alh", "alr"))
            gt2r = sb_mixer("gt2r", [P, P], f32r)
            a_high, a_rest = sb_mixer("a_high", [P, NT, NH], f32r), sb_mixer("a_rest", [P, NT, NH])
            btok = sb_mixer("btok", [P, 2, NS])
            gm = sb_mixer("gm", [P, 2, Q])
            st = sb_mixer("st", [P, 2, NQ, DI])
            ydx = sb_mixer("ydx", [P, 2, MD, P])
            yg = sb_mixer("yg", [P, 2, MD, P])
            sq = sb_mixer("sq", [P, 2, MD, P])
            sqs = sb_mixer("sqs", [P, 2, P])
            win_flat = win[:, :, :].rearrange("p k n -> p (k n)")
            xdd = win_flat[:, 0:2 * DI].rearrange("p (r n) -> p r n", r=2)
            y = win_flat[:, 2 * DI:4 * DI].rearrange("p (r n) -> p r n", r=2)
            yoff = win_flat[:, 4 * DI:5 * DI]
            mrow_sb = ydx[0:NB, :, :, :].rearrange("b r m n -> b (r m n)").rearrange("b (q d) -> b q d", d=D)
            gside, gtest = (m[0:NB, :, :, :].rearrange("b r m n -> b (r m n)")
                            .rearrange("b (u s d) -> b u s d", u=2, s=2) for m in (yg, sq))
        w1h, w1r = sb("w1h", [P, 3, KD, HID], f32r), sb("w1r", [P, 3, KD, HID], f32r)
        w3h, w3r = sb("w3h", [P, 3, KD, HID], f32r), sb("w3r", [P, 3, KD, HID], f32r)
        w2h, w2r = sb("w2h", [P, 3, JH, D], f32r), sb("w2r", [P, 3, JH, D], f32r)
        xdh, xdr = sb("xdh", [P, 2, KD, P], f32r), sb("xdr", [P, 2, KD, P], f32r)
        acth, actr = sb("acth", [P, 2, JH, P], f32r), sb("actr", [P, 2, JH, P], f32r)

        bank = [ctx.enter_context(nc.psum_tensor(f"bank{i}", [P, 512], f32))[:, :] for i in range(8)]
        SEG, ST, X, BG, YD, YOFF, YT, MISC = range(8)
        proj_bank = [2, 3, 4, 5]
        mc_ps = bank[6][:, 0:2 * NB * KD]
        dt_ps = bank[7][:, 0:NDT]
        out_ps = bank[MISC][:, 0:D]
        small_ps = bank[YT][:, 0:(2 + NQ) * TB * NH]
        ssq_ps = bank[MISC][:, 352:352 + NT]
        lg_ps = bank[BG][:, 4 * P - NT * NE:4 * P]
        pos_ps = bank[YD][:, 0:NT * NE]
        b_ps = bank[BG][:, 0:P]
        g_ps = bank[BG][:, P:P + Q]
        h2T_ps = bank[BG][:, P + Q:P + Q + D]
        up_bank = [(0, 1), (5, 6)]
        down_bank = [3, 4]
        xdT_ps = bank[MISC][:, 0:KD * P]
        actT_ps = [bank[MISC if e == NE - 1 else X][:, 0:JH * P] for e in range(NE)]
        EARLY = 1
        sd_bank = [3, 0, 1, 5, 6, 0, 1, 5]

        s_pack, s_x = sem("pack_in"), [sem(f"x{t}_in") for t in range(NT)]
        s_wma, s_wmb = sem("wmod_a_in"), sem("wmod_b_in")
        s_winx, s_winz = sem("winx_in"), sem("winz_in")
        s_wo, s_shw, s_sh2 = sem("wo_in"), sem("shared_up_in"), sem("shared_down_in")
        s_ewu = [sem(f"expert{e}_up_in") for e in range(NE)]
        s_ewd = [sem(f"expert{e}_down_in") for e in range(NE)]
        s_rowout, s_rowin = sem("mod_rows_out"), sem("mod_rows_in")
        s_zeroed, s_scat, s_xg = sem("emptied"), sem("scattered"), [sem(f"slots{q}_in") for q in range(NE // 2)]
        s_oeout, s_routed, s_out = sem("expert_rows_out"), [sem(f"routed{t}_in") for t in range(NT)], sem("stored")
        s_pc, s_const = sem("pool_chain"), sem("constants")
        s_mrow, s_rstd, s_expa, s_en = sem("mod_rows_sb"), sem("rstd"), sem("exp_a"), sem("exp_neg")
        s_alh, s_xdd, s_sdec, s_yg = sem("a_masked"), sem("x_decayed"), sem("state_decayed"), sem("y_gated")
        s_rr, s_rstd2, s_shg, s_pad = sem("rrms"), sem("rstd2"), sem("shared_gated"), sem("w2_pads")
        s_ggb, s_finp = sem("gates_by_rows"), sem("final_rows_pool")
        s_sc, s_hT, s_tap, s_xc, s_zs = sem("silu_c"), sem("hT"), sem("first_tap"), sem("conv_silu"), sem("z_silu")
        s_alr = sem("a_rest_masked")
        s_mraw, s_dec, s_l, s_btok = sem("mod_rows_raw"), sem("decays"), sem("decay_matrix"), sem("b_tokens")
        s_sq, s_h2T = sem("y_squared"), sem("h2T")
        s_sg, s_ex = sem("up_silu"), sem("gate_exp")
        s_xdh, s_wh, s_ah = sem("slots_high"), sem("up_weights_high"), sem("act_high")
        s_w2h = sem("down_weights_high")
        s_xdr, s_wr, s_w2, s_ar = sem("slots_rest"), sem("up_weights_rest"), sem("down_weights_split"), sem("act_rest")
        s_vc = sem("vector_chain")
        s_ve, s_xn, s_mcol, s_conv = sem("variance"), sem("x_normed"), sem("mod_cols"), sem("conv_done")
        s_nabs, s_dt, s_wog, s_split = sem("neg_abs"), sem("time_steps"), sem("wo_gated"), sem("a_split")
        s_m, s_xdt, s_gm = sem("m_matrix"), sem("x_dt"), sem("g_masked")
        s_yoffe, s_y, s_st = sem("yoff_scaled"), sem("y_sum"), sem("states")
        s_sqs, s_cent = sem("squares_summed"), sem("x_centred")
        s_ydx, s_rv, s_x1, s_ve2, s_h2 = sem("y_plus_dx"), sem("mean_square"), sem("x1"), sem("variance2"), sem("h2_rows")
        s_sh, s_oh, s_dest = sem("logits_shifted"), sem("one_hot"), sem("slots")
        s_pre, s_gated, s_gate = sem("shared_added"), sem("rows_gated"), sem("gates")
        s_act, s_oes, s_fin = sem("up_act"), sem("expert_rows"), sem("final_rows")
        p_mc, p_mt, p_hT, p_dt, p_proj = sem("p_mod_cols"), sem("p_mod_rows"), sem("p_hT"), sem("p_dt"), sem("p_proj")
        p_small, p_xtok, p_bg, p_seg = sem("p_small"), sem("p_x_tokens"), sem("p_b_g"), sem("p_seg")
        p_yd, p_yoff, p_st, p_yT, p_ssq, p_out = sem("p_y_diag"), sem("p_y_off"), sem("p_state"), sem("p_yT"), sem("p_sum_squares"), sem("p_out")
        p_h2T, p_lg, p_pos = sem("p_h2T"), sem("p_logits"), sem("p_positions")
        p_actT = sem("p_act_T")
        p_up, p_xdT, p_dn, p_sd = sem("p_up"), sem("p_slots_T"), sem("p_down"), sem("p_shared_down")

        block = ctx.enter_context(nc.Block())

        def tok(c):
            return slice(c * P, (c + 1) * P)

        def seq(b):
            return slice(b * L, (b + 1) * L)

        def decays_before(c, q):
            return NQ * c + q + 1 - (c // TB + 1)

        PROJ = [0, 1, MC, 2, 3, MC + 1, 4, 5, MC + 2, MC + 3]
        NPROJ = MC + MD

        def place(b, q):
            return b * NPROJ + PROJ.index(q)

        UPS = [("shared", b, j) for b in range(NB) for j in range(JH)] + [("expert", e, 0) for e in range(NE)]
        NSH = NB * JH

        @block.sync
        def _(sp):
            sp.dma_start(pk[:, :], pack).then_inc(s_pack, 16)
            xv = x.rearrange("b (t p) d -> p (b t) d", p=P)
            wmv = wmod.rearrange("(k p) n -> p k n", p=P)
            wiv = in_w.rearrange("(k p) n -> p k n", p=P)
            sp.dma_start(wm[:, :, 0:2 * D], wmv[:, :, 0:2 * D]).then_inc(s_wma, 16)
            for t in range(TB):
                sp.dma_start(xs[:, t, :], xv[:, t, :]).then_inc(s_x[t], 16)
            sp.dma_start(win[:, :, DI:DPROJ], wiv[:, :, DI:DPROJ]).then_inc(s_winx, 16)
            for t in range(TB, NT):
                sp.dma_start(xs[:, t, :], xv[:, t, :]).then_inc(s_x[t], 16)
            sp.dma_start(wm[:, :, 2 * D:6 * D], wmv[:, :, 2 * D:6 * D]).then_inc(s_wmb, 16)
            sp.dma_start(win[:, :, 0:DI], wiv[:, :, 0:DI]).then_inc(s_winz, 16)
            sp.dma_start(wo[:, :, :], out_w.rearrange("(m p) n -> p m n", p=P)).then_inc(s_wo, 16)
            sp.wait_ge(s_mrow, 1)
            sp.dma_start(mod_rows, mrow_sb[:, :, :]).then_inc(s_rowout, 16)
            sp.dma_start(shw1[:, :, :], sw1.rearrange("(k p) n -> p k n", p=P)).then_inc(s_shw, 16)
            sp.dma_start(shw3[:, :, :], sw3.rearrange("(k p) n -> p k n", p=P)).then_inc(s_shw, 16)
            sp.wait_ge(s_rowout, 16)
            sp.dma_start(mrow[:, :, :, :].rearrange("p b a d -> p (b a d)"),
                         mod_rows.rearrange("b q d -> (b q d)").partition_broadcast(P)).then_inc(s_rowin, 16)
            sp.dma_start(shw2[:, 0:2, :], sw2[0:2 * P, :].rearrange("(j p) n -> p j n", p=P)).then_inc(s_sh2, 16)
            sp.dma_start(shw2[DUP:P, 2, :], sw2[2 * P:HID, :]).then_inc(s_sh2, 16)
            sp.wait_ge(s_const, 1)
            sp.dma_start(xd[0:NE * CAP, :].rearrange("(e p) d -> p e d", p=P), empty[:, :, :]).then_inc(s_zeroed, 16)
            sp.dma_start(oe[0:NB * L, :].rearrange("(t p) d -> p t d", p=P), empty[:, :, 0:D]).then_inc(s_zeroed, 16)
            sp.wait_ge(s_pad, 1)

            def load_up(e):
                q = e % EB
                if e >= EB:
                    sp.wait_ge(s_wr, 2 * (e - EB + 1))
                sp.dma_start(ew1[:, q, :, :], w1[e].rearrange("(k p) n -> p k n", p=P)).then_inc(s_ewu[e], 16)
                sp.dma_start(ew3[:, q, :, :], w3[e].rearrange("(k p) n -> p k n", p=P)).then_inc(s_ewu[e], 16)

            def load_down(e):
                q = e % DB
                if e >= DB:
                    sp.wait_ge(s_w2, e - DB + 1)
                sp.dma_start(ew2[:, q, 0:2, :], w2[e, 0:2 * P, :].rearrange("(j p) n -> p j n", p=P)).then_inc(s_ewd[e], 16)
                sp.dma_start(ew2[DUP:P, q, 2, :], w2[e, 2 * P:HID, :]).then_inc(s_ewd[e], 16)

            sp.wait_ge(s_zeroed, 32)
            for e in range(EB):
                load_up(e)
                if e < DB:
                    load_down(e)
            sp.wait_ge(s_scat, 16 * NT)
            for q in range(NE // 2):
                sp.dma_start(xg_id[:, 2 * q:2 * q + 2, :],
                             xd[2 * q * CAP:(2 * q + 2) * CAP, :].rearrange("(e p) d -> p e d", p=P)).then_inc(s_xg[q], 16)
            load_down(EB - 1)
            load_up(EB)
            load_up(EB + 1)
            load_up(EB + 2)
            load_down(EB)
            load_down(EB + 1)
            load_up(EB + 3)
            load_down(EB + 2)
            load_down(EB + 3)
            sp.wait_ge(s_oeout, 16 * NE)
            for t in range(NT):
                sp.dma_start(routed[:, t, :], oe[t * P:(t + 1) * P, :]).then_inc(s_routed[t], 16)
            ov = out.rearrange("b (t p) d -> (b t) p d", p=P)
            for t in range(NT):
                if t in POOL_TILES:
                    sp.wait_ge(s_finp, POOL_TILES.index(t) + 1)
                else:
                    sp.wait_ge(s_fin, DVE_TILES.index(t) + 1)
                sp.dma_start(ov[t], res[:, t, :]).then_inc(s_out, 16)
            sp.wait_ge(s_out, 16 * NT)

        @block.gpsimd
        def _(pool):
            chained = [0]

            def then_wait(ins):
                chained[0] += 1
                ins.then_inc(s_pc, 1)
                pool.wait_ge(s_pc, chained[0])

            pool.memset(empty[:, :, 0:D], 0.0)
            pool.iota(empty[:, :, D], pattern=[[P, NE]], base=NB * L, channel_multiplier=1,
                      allow_small_or_imprecise_dtypes=True)
            pool.iota(xn_id[:, :, D], pattern=[[P, NT]], base=0, channel_multiplier=1,
                      allow_small_or_imprecise_dtypes=True)
            pool.memset(neg_half[:, :], -0.5)
            pool.memset(euler[:, :], 2.718281828459045)
            pool.memset(ones_b[:, :], 1.0)
            pool.memset(ones[:, :], 1.0)
            pool.memset(half[:, :, :], 1.0)
            then_wait(pool.memset(ident[:, :], 0.0))
            pool.affine_select(out=ident[:, :], in_=ident[:, :], compare_op=ALU.not_equal, fill=1.0,
                               base=0, pattern=[[-1, P]], channel_multiplier=1)
            pool.affine_select(out=le_b[:, :], in_=ones[:, :], compare_op=ALU.is_ge, fill=0.0,
                               base=0, pattern=[[1, P]], channel_multiplier=-1)
            le2v, gt2v = (m[:, :].rearrange("p (q l) -> p q l", q=NQ) for m in (le2, gt2))
            onev = ones[:, :].rearrange("p (q l) -> p q l", q=NQ)
            pool.affine_select(out=le2v, in_=onev, compare_op=ALU.is_ge, fill=0.0, base=0,
                               pattern=[[Q, NQ], [1, Q]], channel_multiplier=-1)
            pool.affine_select(out=gt2v, in_=onev, compare_op=ALU.is_gt, fill=0.0, base=0,
                               pattern=[[-Q, NQ], [-1, Q]], channel_multiplier=1)
            then_wait(pool.affine_select(out=half[:, :, :], in_=half[:, :, :], compare_op=ALU.is_ge, fill=0.0,
                                         base=0, pattern=[[-Q, NQ], [0, P]], channel_multiplier=1))
            pool.affine_select(out=gt2v, in_=gt2v, compare_op=ALU.is_ge, fill=0.0, base=Q - 1,
                               pattern=[[Q, NQ], [0, Q]], channel_multiplier=-1)
            pool.affine_select(out=half[:, :, :], in_=half[:, :, :], compare_op=ALU.is_ge, fill=0.0, base=Q - 1,
                               pattern=[[Q, NQ], [0, P]], channel_multiplier=-1)
            then_wait(pool.affine_select(out=le2v, in_=le2v, compare_op=ALU.is_ge, fill=0.0, base=0,
                                         pattern=[[-Q, NQ], [0, Q]], channel_multiplier=1))
            pool.tensor_tensor(le[:, :], le2[:, 0:Q], le2[:, Q:P], ALU.add)
            pool.iota(rank[:, :, :], pattern=[[0, TB], [-1, NE]], base=NE, channel_multiplier=0,
                      allow_small_or_imprecise_dtypes=True)
            pool.iota(slot0[:, :, :], pattern=[[0, TB], [CAP, NE]], base=-1, channel_multiplier=0,
                      allow_small_or_imprecise_dtypes=True)
            pool.iota(spill[:, :], pattern=[[P, NT]], base=NE * CAP, channel_multiplier=1,
                      allow_small_or_imprecise_dtypes=True).then_inc(s_const, 1)

            for b in range(NB):
                pool.wait_ge(s_ve, b + 1)
                bt = slice(b * TB, (b + 1) * TB)
                pool.tensor_tensor(rstd[:, bt], ve[:, bt], neg_half[:, 0:TB], ALU.pow).then_inc(s_rstd, 1)
            pool.wait_ge(s_pack, 16)
            pool.tensor_tensor(expa[:, :], euler[:, 0:NH], pk[:, C_AL:C_AL + NH], ALU.pow).then_inc(s_expa, 1)
            pool.wait_ge(s_nabs, 1)
            pool.tensor_tensor(en[:, :], euler[:, :], nabs[:, :], ALU.pow).then_inc(s_en, 1)
            pool.wait_ge(s_mraw, 2)
            gates = [mrow_sb[:, q - GA, :] for q in (GA, GB)]
            pool.tensor_scalar(mrow_sb[:, CB - GA, :], mrow_sb[:, CB - GA, :], 1.0, None, ALU.add)
            for u in range(2):
                pool.tensor_scalar(gside[:, u, 0, :], gates[u], 0.25, None, ALU.max)
                pool.tensor_scalar(gside[:, u, 1, :], gates[u], -0.25, None, ALU.min)
                pool.tensor_scalar(gtest[:, u, 0, :], gates[u], 0.0, None, ALU.is_ge)
                ins = pool.tensor_scalar(gtest[:, u, 1, :], gates[u], 0.0, None, ALU.is_lt)
            then_wait(ins)
            then_wait(pool.tensor_tensor(gside[:, :, :, :], gside[:, :, :, :], gtest[:, :, :, :], ALU.mult))
            for u in range(2):
                ins = pool.tensor_tensor(gates[u], gside[:, u, 0, :], gside[:, u, 1, :], ALU.add)
            ins.then_inc(s_mrow, 1)
            pool.memset(shw2[0:DUP, 2, :], 0.0)
            pool.memset(ew2[0:DUP, :, 2, :], 0.0).then_inc(s_pad, 1)

            def masked_a(c):
                if c >= 2:
                    pool.wait_ge(p_seg, c - 1)
                pool.tensor_tensor(alh[:, c % 2, :, :], le[:, :].unsqueeze(1).to_broadcast([P, NH, Q]),
                                   a_high[:, c, :].unsqueeze(2).to_broadcast([P, NH, Q]), ALU.mult).then_inc(s_alh, 1)

            def rest_decay(c):
                pool.wait_ge(s_xdt, c + 1)
                pool.wait_ge(s_dec, c // TB + 1)
                if c >= 2:
                    pool.wait_ge(p_st, NQ * (c - 1))
                pool.tensor_tensor(xdd[:, c % 2, :].rearrange("p (h d) -> p h d", h=NH),
                                   xdt[:, c % 2, :].rearrange("p (h d) -> p h d", h=NH),
                                   dec[:, c // TB, 1, c % TB, :].unsqueeze(2).to_broadcast([P, NH, HD]),
                                   ALU.mult).then_inc(s_xdd, 1)

            def decayed_state(c, q):
                if c % TB == 0 and q == 0:
                    return
                pool.wait_ge(s_st, NQ * c + q)
                before = st[:, c % 2, 0, :] if q else st[:, (c - 1) % 2, NQ - 1, :]
                pool.tensor_tensor(stdec[:, q, :].rearrange("p (h d) -> p h d", h=NH),
                                   before.rearrange("p (h d) -> p h d", h=NH),
                                   dec[:, c // TB, 2 + q, c % TB, :].unsqueeze(2).to_broadcast([P, NH, HD]),
                                   ALU.mult).then_inc(s_sdec, 1)

            def gated(c):
                pool.wait_ge(s_ydx, c + 1)
                pool.wait_ge(s_zs, MD * (c // TB + 1))
                if c >= 2:
                    pool.wait_ge(p_out, c - 1)
                pool.tensor_tensor(yg[:, c % 2, :, :], ydx[:, c % 2, :, :], zs[:, :, tok(c)], ALU.mult).then_inc(s_yg, 1)

            pool.wait_ge(s_split, 1)
            masked_a(0)
            masked_a(1)

            def gated_shared_weights(b):
                pool.wait_ge(s_rowin, 16)
                pool.wait_ge(s_sh2, 32)
                pool.wait_ge(s_pad, 1)
                pool.tensor_tensor(shw2g[:, b, :, :], shw2[:, :, :],
                                   mrow[:, b, GB - GA, :].unsqueeze(1).to_broadcast([P, JH, D]),
                                   ALU.mult).then_inc(s_shg, 1)

            def rrms(c):
                pool.wait_ge(s_rv, c + 1)
                pool.tensor_tensor(rr[:, c:c + 1], rv[:, c:c + 1], neg_half[:, 0:1], ALU.pow).then_inc(s_rr, 1)

            def norm2(c):
                pool.wait_ge(s_ve2, c + 1)
                pool.tensor_tensor(rstd2[:, c:c + 1], ve2[:, c:c + 1], neg_half[:, 0:1], ALU.pow).then_inc(s_rstd2, 1)

            def scatter(b):
                pool.wait_ge(s_dest, b + 1)
                pool.wait_ge(s_zeroed, 32)
                for t in range(b * TB, (b + 1) * TB):
                    pool.indirect_dma_start(out=xd, out_offset=bass.IndirectOffsetOnAxis(ap=dest[:, t:t + 1], axis=0),
                                            in_=xn_id[:, t, :], in_offset=None).then_inc(s_scat, 16)

            rest_decay(0)
            rest_decay(1)
            for c in range(NT):
                decayed_state(c, 1)
                if c + 1 < NT:
                    if c == 0:
                        decayed_state(1, 0)
                        masked_a(2)
                    else:
                        if c + 2 < NT:
                            masked_a(c + 2)
                        decayed_state(c + 1, 0)
                        rest_decay(c + 1)
                if c >= 2:
                    rrms(c - 2)
                if c >= 1:
                    gated(c - 1)
                if c >= 2:
                    norm2(c - 2)
                if 2 <= c < 2 + NB:
                    gated_shared_weights(c - 2)
            rrms(NT - 2)
            gated(NT - 1)
            norm2(NT - 2)
            rrms(NT - 1)
            norm2(NT - 1)

            def down_weights_rest(e):
                pool.wait_ge(s_w2h, e + 1)
                pool.tensor_tensor(w2r[:, e % 3, :, :], ew2[:, e % DB, :, :], w2h[:, e % 3, :, :],
                                   ALU.subtract).then_inc(s_w2, 1)

            scatter(0)
            scatter(1)
            down_weights_rest(0)
            down_weights_rest(1)
            pool.wait_ge(s_gate, 1)
            for i, t in enumerate(POOL_TILES):
                pool.tensor_tensor(gated_gb[:, i, :], mrow[:, t // TB, GB - GA, :],
                                   gate[:, t:t + 1].to_broadcast([P, D]), ALU.mult).then_inc(s_ggb, 1)
            for e in range(NE):
                if e + 2 < NE:
                    down_weights_rest(e + 2)
                pool.wait_ge(s_oes, e + 1)
                pool.indirect_dma_start(out=oe, out_offset=bass.IndirectOffsetOnAxis(ap=slot_tok[:, e:e + 1], axis=0),
                                        in_=oes[:, e, :], in_offset=None).then_inc(s_oeout, 16)
            for i, t in enumerate(POOL_TILES):
                pool.wait_ge(s_routed[t], 16)
                if i == 0:
                    pool.wait_ge(s_ggb, len(POOL_TILES))
                then_wait(pool.tensor_tensor(routed[:, t, :], routed[:, t, :], gated_gb[:, i, :], ALU.mult))
                pool.wait_ge(s_pre, t + 1)
                pool.tensor_tensor(res[:, t, :], res[:, t, :], routed[:, t, :], ALU.add).then_inc(s_finp, 1)

        @block.scalar
        def _(act):
            act.wait_ge(s_pack, 16)
            act.activation(sc[:, :], pk[:, C_C:C_C + KD * NB], ACT.Silu).then_inc(s_sc, 1)
            act.wait_ge(s_mcol, 1)

            def hT_out(b):
                for i in range(2):
                    act.wait_ge(p_hT, 2 * b + i + 1)
                    for k in range(KD):
                        act.activation(hT[:, k, (2 * b + i) * 2 * P:(2 * b + i + 1) * 2 * P],
                                       bank[i][:, k * 2 * P:(k + 1) * 2 * P], ACT.Identity,
                                       bias=mcol[:, (SA * NB + b) * KD + k:(SA * NB + b) * KD + k + 1],
                                       scale=mcol[:, (CA * NB + b) * KD + k:(CA * NB + b) * KD + k + 1]).then_inc(s_hT, 1)

            def first_tap(b, m):
                n, i = place(b, m), b * MC + m
                act.wait_ge(p_proj, n + 1)
                if i >= 3:
                    act.wait_ge(s_xc, i - 2)
                act.activation(acc[:, i % 3, :], bank[proj_bank[n % 4]], ACT.Identity,
                               bias=pk[:, C_CB + m:C_CB + m + 1],
                               scale=pk[:, C_CW + m * TAPS + TAPS - 1:C_CW + m * TAPS + TAPS]).then_inc(s_tap, 1)

            def conv_silu(i):
                b, m = divmod(i, MC)
                act.wait_ge(s_conv, i + 1)
                act.activation(xcT[:, m, seq(b)], acc[:, i % 3, :], ACT.Silu).then_inc(s_xc, 1)

            def z_silu(b, m):
                n = place(b, MC + m)
                act.wait_ge(p_proj, n + 1)
                act.activation(zs[:, m, seq(b)], bank[proj_bank[n % 4]], ACT.Silu).then_inc(s_zs, 1)

            def masked_rest(c):
                if c >= 2:
                    act.wait_ge(p_seg, c - 1)
                for h in range(NH):
                    ins = act.activation(alr[:, c % 2, h, :], le[:, :], ACT.Copy, scale=a_rest[:, c, h:h + 1])
                ins.then_inc(s_alr, 1)

            hT_out(0)
            for b in range(NB):
                for q in PROJ:
                    i = b * MC + q
                    if q >= MC:
                        z_silu(b, q - MC)
                        if b == NB - 1 and q == MC + MD - 2:
                            conv_silu(NB * MC - 2)
                        continue
                    if i >= 2:
                        conv_silu(i - 2)
                    first_tap(b, q)
                    if i == 1:
                        hT_out(1)
                    if i in (MC + 3, MC + 4):
                        act.wait_ge(s_split, 2)
                        masked_rest(i - MC - 3)
                    if i == 3:
                        act.wait_ge(p_mt, 1)
                        for k in range(2):
                            act.activation(mrow_sb[:, 2 * k:2 * k + 2, :].rearrange("b q d -> b (q d)"),
                                           bank[k][0:NB, :], ACT.Copy).then_inc(s_mraw, 1)
            conv_silu(NB * MC - 1)

            def decays(b):
                act.wait_ge(p_small, b + 1)
                act.activation(dec[:, b, :, :, :].rearrange("p q t h -> p (q t h)"), small_ps, ACT.Exp).then_inc(s_dec, 1)

            def decay_matrix(c):
                act.wait_ge(p_seg, c + 1)
                if c >= 2:
                    act.wait_ge(p_yd, c - 1)
                act.activation(lm[:, c % 2, :, :].rearrange("p h l -> p (h l)"),
                               bank[SEG], ACT.Exp).then_inc(s_l, 1)

            def b_tokens(c):
                act.wait_ge(p_bg, c + 1)
                if c >= 2:
                    act.wait_ge(p_st, NQ * (c - 1))
                act.activation(btok[:, c % 2, :], b_ps, ACT.Copy).then_inc(s_btok, 1)

            def heads_scaled(out, ps, scale):
                for h in range(NH):
                    cols = slice(h * HD, (h + 1) * HD)
                    ins = act.activation(out[:, cols], ps[:, cols], ACT.Copy, scale=scale[:, h:h + 1])
                return ins

            def y_off(c):
                act.wait_ge(p_yoff, c + 1)
                if c >= 1:
                    act.wait_ge(s_y, c)
                heads_scaled(yoff, bank[YOFF], dec[:, c // TB, 0, c % TB, :]).then_inc(s_yoffe, 1)

            def y_squared(c):
                act.wait_ge(s_yg, c + 1)
                if c >= 2:
                    act.wait_ge(s_sqs, c - 1)
                act.activation(sq[:, c % 2, :, :].rearrange("p m n -> p (m n)"),
                               yg[:, c % 2, :, :].rearrange("p m n -> p (m n)"), ACT.Square).then_inc(s_sq, 1)

            def h2T_out(t):
                act.wait_ge(p_h2T, t + 1)
                act.activation(h2T[:, :, tok(t)], h2T_ps.rearrange("p (k n) -> p k n", k=KD), ACT.Copy).then_inc(s_h2T, 1)

            def up_silu(u):
                kind, e, j = UPS[u]
                act.wait_ge(p_up, u + 1)
                if u >= 2:
                    act.wait_ge(s_act, u - 1)
                n = L if kind == "shared" else HID
                act.activation(sg[:, u % 2, 0:n], bank[up_bank[u % 2][0]][:, 0:n], ACT.Silu).then_inc(s_sg, 1)

            def up_weights_high(e):
                act.wait_ge(s_ewu[e], 32)
                if e == 0:
                    act.wait_ge(p_ssq, NT)
                if e >= 3:
                    act.wait_ge(p_up, NSH + e - 2)
                for high, w in ((w1h, ew1), (w3h, ew3)):
                    act.activation(high[:, e % 3, :, :].rearrange("p k n -> p (k n)"),
                                   w[:, e % EB, :, :].rearrange("p k n -> p (k n)"), ACT.Copy).then_inc(s_wh, 1)

            def down_weights_high(e):
                act.wait_ge(s_ewd[e], 32)
                act.wait_ge(s_pad, 1)
                if e >= 3:
                    act.wait_ge(p_dn, e - 2)
                act.activation(w2h[:, e % 3, :, :].rearrange("p j n -> p (j n)"),
                               ew2[:, e % DB, :, :].rearrange("p j n -> p (j n)"), ACT.Copy).then_inc(s_w2h, 1)

            def slots_high(e):
                act.wait_ge(p_xdT, e + 1)
                if e >= 2:
                    act.wait_ge(p_up, NSH + e - 1)
                act.activation(xdh[:, e % 2, :, :].rearrange("p k n -> p (k n)"), xdT_ps, ACT.Copy).then_inc(s_xdh, 1)

            def act_high(e):
                act.wait_ge(p_actT, e + 1)
                if e >= 2:
                    act.wait_ge(p_dn, e - 1)
                act.activation(acth[:, e % 2, :, :].rearrange("p j n -> p (j n)"), actT_ps[e], ACT.Copy).then_inc(s_ah, 1)

            decays(0)
            b_tokens(0)
            decay_matrix(0)
            for c in range(NT):
                if c + 1 == TB:
                    decays(1)
                if c + 1 < NT:
                    b_tokens(c + 1)
                    decay_matrix(c + 1)
                if c >= 3:
                    h2T_out(c - 3)
                y_off(c)
                if c + 2 < NT:
                    masked_rest(c + 2)
                if c >= 1:
                    y_squared(c - 1)
            y_squared(NT - 1)
            up_silu(0)
            h2T_out(NT - 3)
            h2T_out(NT - 2)
            up_silu(1)
            h2T_out(NT - 1)
            for u in range(2, NSH):
                up_silu(u)
                if u < 4:
                    up_weights_high(u - 2)
                    down_weights_high(u - 2)
                if u == 4:
                    act.wait_ge(s_sh, NB)
                    act.activation(ex[:, :, :].rearrange("p t e -> p (t e)"), sh[:, :, :].rearrange("p t e -> p (t e)"),
                                   ACT.Exp).then_inc(s_ex, 1)
            slots_high(0)
            up_weights_high(2)
            for e in range(NE):
                if e + 1 < NE:
                    slots_high(e + 1)
                up_silu(NSH + e)
                if e >= 1:
                    act_high(e - 1)
                if 1 <= e < NE - 2:
                    up_weights_high(e + 2)
                if 1 <= e < NE - 1:
                    down_weights_high(e + 1)
            act_high(NE - 1)

        @block.vector
        def _(dve):
            vec = nc.vector
            chained = [0]

            def then_wait(ins):
                chained[0] += 1
                ins.then_inc(s_vc, 1)
                dve.wait_ge(s_vc, chained[0])

            def norm1(b):
                for t in range(b * TB, (b + 1) * TB):
                    dve.wait_ge(s_x[t], 16)
                    ins = vec.bn_stats(stats[:, t, :], xs[:, t, :])
                then_wait(ins)
                for t in range(b * TB, (b + 1) * TB):
                    ins = vec.bn_aggr(mv[:, t, :], stats[:, t, :])
                then_wait(ins)
                bt = slice(b * TB, (b + 1) * TB)
                vec.tensor_scalar(ve[:, bt], mv[:, bt, 1], EPS, None, ALU.add).then_inc(s_ve, 1)
                dve.wait_ge(s_rstd, b + 1)
                for t in range(b * TB, (b + 1) * TB):
                    vec.tensor_scalar(xn[:, t, :], xs[:, t, :], mv[:, t, 0:1], rstd[:, t:t + 1],
                                      ALU.subtract, ALU.mult).then_inc(s_xn, 1)

            def conv(b, m):
                n, i = place(b, m), b * MC + m
                dve.wait_ge(s_tap, i + 1)
                ps = bank[proj_bank[n % 4]]
                for s in range(1, TAPS):
                    w = C_CW + m * TAPS + TAPS - 1 - s
                    ins = vec.scalar_tensor_tensor(acc[:, i % 3, s:L], ps[:, 0:L - s], pk[:, w:w + 1],
                                                   acc[:, i % 3, s:L], ALU.mult, ALU.add)
                    if s < TAPS - 1:
                        then_wait(ins)
                ins.then_inc(s_conv, 1)

            norm1(0)
            dve.wait_ge(p_mc, 1)
            then_wait(vec.tensor_copy(mcol[:, :].rearrange("p (q b k) -> p q b k", b=NB, k=KD),
                                      mc_ps.rearrange("p (q k b) -> p q b k", b=NB, k=KD)))
            vec.tensor_scalar(mcol[:, CA * 4:CA * 4 + 4], mcol[:, CA * 4:CA * 4 + 4], 1.0, None,
                              ALU.add).then_inc(s_mcol, 1)
            norm1(1)
            conv(0, 0)
            conv(0, 1)

            dve.wait_ge(p_dt, 1)
            then_wait(vec.tensor_tensor(v[:, :].rearrange("p (t h) -> p t h", h=NH),
                                        dt_ps.rearrange("p (t h) -> p t h", h=NH),
                                        pk[:, C_DB:C_DB + NH].unsqueeze(1).to_broadcast([P, NT, NH]), ALU.add))
            vec.scalar_tensor_tensor(nabs[:, :], v[:, :], -1.0, v[:, :], ALU.mult, ALU.min).then_inc(s_nabs, 1)
            conv(0, 2)
            conv(0, 3)
            conv(0, 4)
            dve.wait_ge(s_en, 1)
            then_wait(vec.tensor_scalar(zz[:, :], en[:, :], 2.0, None, ALU.add))
            then_wait(vec.reciprocal(zz[:, :], zz[:, :]))
            then_wait(vec.tensor_tensor(zz[:, :], zz[:, :], en[:, :], ALU.mult))
            then_wait(vec.tensor_tensor(z2[:, :], zz[:, :], zz[:, :], ALU.mult))
            then_wait(vec.tensor_scalar(pp[:, :], z2[:, :], 1.0 / 17, None, ALU.mult))
            conv(0, 5)
            for k in (15, 13, 11, 9, 7, 5, 3):
                then_wait(vec.scalar_tensor_tensor(pp[:, :], pp[:, :], 1.0 / k, z2[:, :], ALU.add, ALU.mult))
            then_wait(vec.scalar_tensor_tensor(pp[:, :], pp[:, :], 1.0, zz[:, :], ALU.add, ALU.mult))
            then_wait(vec.tensor_scalar(v[:, :], v[:, :], 0.0, None, ALU.max))
            dtf = dt[:, :, :].rearrange("p t h -> p (t h)")
            then_wait(vec.scalar_tensor_tensor(dtf, pp[:, :], 2.0, v[:, :], ALU.mult, ALU.add))
            dve.wait_ge(s_expa, 1)
            vec.scalar_tensor_tensor(a[:, :, :], dt[:, :, :], -1.0, expa[:, :].unsqueeze(1).to_broadcast([P, NT, NH]),
                                     ALU.mult, ALU.mult).then_inc(s_dt, 1)
            dve.wait_ge(s_dt, 1)
            vec.tensor_copy(a_high[:, :, :], a[:, :, :]).then_inc(s_split, 1)
            dve.wait_ge(s_split, 1)
            vec.tensor_tensor(a_rest[:, :, :], a[:, :, :], a_high[:, :, :], ALU.subtract).then_inc(s_split, 1)
            dve.wait_ge(s_const, 1)
            vec.tensor_copy(gt2r[:, :], gt2[:, :]).then_inc(s_split, 1)
            for m in range(MC):
                conv(1, m)

            def gated_out_weights(b):
                dve.wait_ge(s_rowin, 16)
                dve.wait_ge(s_wo, 16)
                for m in range(MD):
                    vec.scalar_tensor_tensor(wog[:, b, m, :], wo[:, m, :], pk[:, C_NW + m:C_NW + m + 1],
                                             mrow[:, b, 0, :], ALU.mult, ALU.mult).then_inc(s_wog, 1)

            def x_dt(c):
                dve.wait_ge(p_xtok, c + 1)
                if c >= 2:
                    dve.wait_ge(p_yd, c - 1)
                    dve.wait_ge(s_xdd, c - 1)
                vec.tensor_tensor(xdt[:, c % 2, :].rearrange("p (h d) -> p h d", h=NH),
                                  bank[X].rearrange("p (h d) -> p h d", h=NH),
                                  dt[:, c, :].unsqueeze(2).to_broadcast([P, NH, HD]), ALU.mult).then_inc(s_xdt, 1)

            def g_masked(c):
                dve.wait_ge(s_btok, c + 1)
                vec.tensor_tensor(gm[:, c % 2, :], g_ps, le[:, :], ALU.mult).then_inc(s_gm, 1)

            def m_matrix(c):
                dve.wait_ge(s_l, c + 1)
                dve.wait_ge(s_gm, c + 1)
                vec.tensor_tensor(lm[:, c % 2, :, :], lm[:, c % 2, :, :],
                                  gm[:, c % 2, :].unsqueeze(1).to_broadcast([P, NH, Q]), ALU.mult).then_inc(s_m, 1)

            def y_sum(c):
                dve.wait_ge(s_yoffe, c + 1)
                dve.wait_ge(p_yd, c + 1)
                if c >= 2:
                    dve.wait_ge(p_yT, c - 1)
                vec.tensor_tensor(y[:, c % 2, :], yoff, bank[YD], ALU.add).then_inc(s_y, 1)

            def state(c, q):
                dve.wait_ge(p_st, NQ * c + q + 1)
                if c >= 2:
                    dve.wait_ge(p_yoff, c - 1)
                if c % TB == 0 and q == 0:
                    vec.tensor_copy(st[:, c % 2, q, :], bank[ST]).then_inc(s_st, 1)
                    return
                dve.wait_ge(s_sdec, decays_before(c, q))
                vec.tensor_tensor(st[:, c % 2, q, :], stdec[:, q, :], bank[ST], ALU.add).then_inc(s_st, 1)

            def y_plus_dx(c):
                dve.wait_ge(p_yT, c + 1)
                if c >= 2:
                    dve.wait_ge(s_yg, c - 1)
                for m in range(MD):
                    ins = vec.scalar_tensor_tensor(ydx[:, c % 2, m, :], xcT[:, m, tok(c)], pk[:, C_D + m:C_D + m + 1],
                                                   bank[YT][:, m * P:(m + 1) * P], ALU.mult, ALU.add)
                ins.then_inc(s_ydx, 1)

            def squares_summed(t):
                dve.wait_ge(s_sq, t + 1)
                if t >= 2:
                    dve.wait_ge(p_ssq, t - 1)
                vec.tensor_reduce(sqs[:, t % 2, :], sq[:, t % 2, :, :].rearrange("p m n -> p n m"),
                                  AX.X, ALU.add).then_inc(s_sqs, 1)

            def mean_square(t):
                dve.wait_ge(p_ssq, t + 1)
                vec.tensor_scalar(rv[:, t:t + 1], ssq_ps[:, t:t + 1], 1.0 / DI, EPS, ALU.mult, ALU.add).then_inc(s_rv, 1)

            def x1_stats(t):
                dve.wait_ge(s_rr, t + 1)
                vec.scalar_tensor_tensor(xs[:, t, :], out_ps, rr[:, t:t + 1], xs[:, t, :],
                                         ALU.mult, ALU.add).then_inc(s_x1, 1)
                dve.wait_ge(s_x1, t + 1)
                then_wait(vec.bn_stats(stats2[:, :], xs[:, t, :]))
                then_wait(vec.bn_aggr(mv2[:, t, :], stats2[:, :]))
                vec.tensor_scalar(ve2[:, t:t + 1], mv2[:, t, 1:2], EPS, None, ALU.add).then_inc(s_ve2, 1)
                vec.scalar_tensor_tensor(cent[:, :], xs[:, t, :], mv2[:, t, 0:1], mrow[:, t // TB, CB - GA, :],
                                         ALU.subtract, ALU.mult).then_inc(s_cent, 1)

            def h2_rows(t):
                dve.wait_ge(s_cent, t + 1)
                dve.wait_ge(s_rstd2, t + 1)
                vec.scalar_tensor_tensor(h2[:, t, :], cent[:, :], rstd2[:, t:t + 1], mrow[:, t // TB, SB - GA, :],
                                         ALU.mult, ALU.add).then_inc(s_h2, 1)

            def route(b):
                ts, n = slice(b * TB, (b + 1) * TB), [P, TB, NE]
                lg = lg_ps.rearrange("p (t e) -> p t e", e=NE)[:, ts, :]
                dve.wait_ge(p_lg, (b + 1) * TB)
                if b == 0:
                    dve.wait_ge(s_h2T, TB + 1)
                then_wait(vec.tensor_reduce(mx[:, ts], lg, AX.X, ALU.max))
                ins = vec.tensor_tensor(sh[:, ts, :], lg, mx[:, ts].unsqueeze(2).to_broadcast(n), ALU.subtract)
                ins.then_inc(s_sh, 1)
                dve.wait_ge(s_sh, b + 1)
                then_wait(vec.scalar_tensor_tensor(cand[:, ts, :], sh[:, ts, :], 0.0, rank[:, :, :], ALU.is_ge, ALU.mult))
                then_wait(vec.tensor_reduce(best[:, ts], cand[:, ts, :], AX.X, ALU.max))
                then_wait(vec.tensor_tensor(oh[:, ts, :], cand[:, ts, :], best[:, ts].unsqueeze(2).to_broadcast(n), ALU.is_equal))
                for t in range(b * TB, (b + 1) * TB):
                    if t == 0:
                        ins = vec.memset(pre[:, 0, :], 0.0)
                    else:
                        ins = vec.tensor_tensor(pre[:, t, :], pre[:, t - 1, :], oh[:, t - 1, :], ALU.add)
                    if t % TB < TB - 1:
                        then_wait(ins)
                ins.then_inc(s_oh, 1)
                then_wait(vec.tensor_tensor(offs[:, ts, :], oh[:, ts, :], slot0[:, :, :], ALU.mult))
                then_wait(vec.tensor_reduce(off[:, ts], offs[:, ts, :], AX.X, ALU.add))

            def slots(b):
                ts = slice(b * TB, (b + 1) * TB)
                dve.wait_ge(p_pos, b + 1)
                then_wait(vec.tensor_tensor(cnts[:, ts, :], pos_ps.rearrange("p (t e) -> p t e", e=NE)[:, ts, :],
                                            oh[:, ts, :], ALU.mult))
                then_wait(vec.tensor_reduce(cnt[:, ts], cnts[:, ts, :], AX.X, ALU.add))
                vec.tensor_scalar(keep[:, ts], cnt[:, ts], float(CAP), None, ALU.is_le)
                then_wait(vec.tensor_tensor(flat[:, ts], cnt[:, ts], off[:, ts], ALU.add))
                then_wait(vec.tensor_tensor(dlt[:, ts], flat[:, ts], spill[:, ts], ALU.subtract))
                then_wait(vec.tensor_tensor(dlt[:, ts], dlt[:, ts], keep[:, ts], ALU.mult))
                vec.tensor_tensor(dest[:, ts], dlt[:, ts], spill[:, ts], ALU.add).then_inc(s_dest, 1)

            dve.wait_ge(s_const, 1)
            x_dt(0)
            g_masked(0)
            x_dt(1)
            g_masked(1)
            state(0, 0)
            for c in range(NT):
                m_matrix(c)
                if c >= 2:
                    squares_summed(c - 2)
                state(c, 1)
                if 0 < c < NT - 1:
                    x_dt(c + 1)
                    g_masked(c + 1)
                if c < NB:
                    gated_out_weights(c)
                if c >= 1:
                    y_plus_dx(c - 1)
                if c >= 2:
                    mean_square(c - 2)
                    x1_stats(c - 2)
                if c + 1 < NT:
                    state(c + 1, 0)
                if c >= 2:
                    h2_rows(c - 2)
                y_sum(c)

            def up_act(u):
                kind, e, j = UPS[u]
                dve.wait_ge(s_sg, u + 1)
                g, w = bank[up_bank[u % 2][1]], sg[:, u % 2, :]
                if kind == "shared":
                    vec.tensor_tensor(shact[:, j, seq(e)], w, g, ALU.mult).then_inc(s_act, 1)
                else:
                    if e >= 2:
                        dve.wait_ge(p_actT, e - 1)
                    vec.tensor_tensor(eact[:, e % 2, :], w[:, 0:HID], g[:, 0:HID], ALU.mult).then_inc(s_act, 1)

            squares_summed(NT - 2)
            y_plus_dx(NT - 1)
            mean_square(NT - 2)
            route(0)
            x1_stats(NT - 2)
            squares_summed(NT - 1)
            h2_rows(NT - 2)
            up_act(0)
            mean_square(NT - 1)
            x1_stats(NT - 1)
            h2_rows(NT - 1)
            slots(0)
            up_act(1)
            route(1)
            slots(1)

            def up_weights_rest(e):
                for i, (rest, high, w) in enumerate(((w1r, w1h, ew1), (w3r, w3h, ew3))):
                    dve.wait_ge(s_wh, 2 * e + i + 1)
                    vec.tensor_tensor(rest[:, e % 3, :, :], w[:, e % EB, :, :], high[:, e % 3, :, :],
                                      ALU.subtract).then_inc(s_wr, 1)

            def slots_rest(e):
                dve.wait_ge(s_xdh, e + 1)
                vec.tensor_tensor(xdr[:, e % 2, :, :].rearrange("p k n -> p (k n)"), xdT_ps,
                                  xdh[:, e % 2, :, :].rearrange("p k n -> p (k n)"), ALU.subtract).then_inc(s_xdr, 1)

            def act_rest(e):
                dve.wait_ge(s_ah, e + 1)
                vec.tensor_tensor(actr[:, e % 2, :, :].rearrange("p j n -> p (j n)"), actT_ps[e],
                                  acth[:, e % 2, :, :].rearrange("p j n -> p (j n)"), ALU.subtract).then_inc(s_ar, 1)

            def expert_rows(e):
                dve.wait_ge(p_dn, e + 1)
                vec.tensor_copy(oes[:, e, :], bank[down_bank[e % 2]][:, 0:D]).then_inc(s_oes, 1)

            def shared_added(t):
                dve.wait_ge(p_sd, t + 1)
                vec.tensor_tensor(res[:, t, :], xs[:, t, :], bank[sd_bank[t]][:, 0:D], ALU.add).then_inc(s_pre, 1)

            for u in range(2, NSH):
                up_act(u)
                if u < 4:
                    up_weights_rest(u - 2)
                if u == 4:
                    dve.wait_ge(s_ex, 1)
                    then_wait(vec.tensor_reduce(es[:, :], ex[:, :, :], AX.X, ALU.add))
                    then_wait(vec.reciprocal(gate[:, :], es[:, :]))
                    vec.tensor_tensor(gate[:, :], gate[:, :], keep[:, :], ALU.mult).then_inc(s_gate, 1)
            slots_rest(0)
            for t in range(EARLY):
                shared_added(t)
            up_weights_rest(2)
            for e in range(NE):
                if e + 1 < NE:
                    slots_rest(e + 1)
                up_act(NSH + e)
                if e >= 1:
                    act_rest(e - 1)
                if e == 1:
                    for q in range(NE // 2):
                        dve.wait_ge(s_xg[q], 16)
                    vec.tensor_copy(slot_tok[:, :], xg_id[:, :, D])
                if e >= 2:
                    expert_rows(e - 2)
                if 1 <= e < NE - 2:
                    up_weights_rest(e + 2)
            act_rest(NE - 1)
            expert_rows(NE - 2)
            expert_rows(NE - 1)

            for t in range(EARLY, NT - 2):
                shared_added(t)

            def gated_rows(t):
                dve.wait_ge(s_routed[t], 16)
                vec.scalar_tensor_tensor(routed[:, t, :], routed[:, t, :], gate[:, t:t + 1],
                                         mrow[:, t // TB, GB - GA, :], ALU.mult, ALU.mult).then_inc(s_gated, 1)

            dve.wait_ge(s_gate, 1)
            gated_rows(DVE_TILES[0])
            for i, t in enumerate(DVE_TILES):
                if i + 1 < len(DVE_TILES):
                    gated_rows(DVE_TILES[i + 1])
                dve.wait_ge(s_gated, i + 1)
                dve.wait_ge(s_pre, t + 1)
                vec.tensor_tensor(res[:, t, :], res[:, t, :], routed[:, t, :], ALU.add).then_inc(s_fin, 1)
                if i < 2:
                    shared_added(NT - 2 + i)

        @block.tensor
        def _(pe):
            mm = pe.matmul
            pe.wait_ge(s_sc, 1)

            def transposed_x(b):
                for i in range(TB):
                    if b and i % 2 == 0:
                        pe.wait_ge(s_hT, KD * (i // 2 + 1))
                    pe.wait_ge(s_xn, b * TB + i + 1)
                    for k in range(KD):
                        at = (k * 2 + i % 2) * P
                        ins = pe.transpose(bank[i // 2][:, at:at + P], xn[:, b * TB + i, k * P:(k + 1) * P], ident[:, :])
                    if i % 2:
                        ins.then_inc(p_hT, 1)

            def wait_read(n):
                b, i = divmod(n, NPROJ)
                if PROJ[i] < MC:
                    pe.wait_ge(s_conv, b * MC + PROJ[i] + 1)
                else:
                    pe.wait_ge(s_zs, b * MD + PROJ[i] - MC + 1)

            def project(b, q):
                n = place(b, q)
                col = DI + q * P if q < MC else (q - MC) * P
                if n >= 4:
                    wait_read(n - 4)
                for k in range(KD):
                    ins = mm(bank[proj_bank[n % 4]], win[:, k, col:col + P], hT[:, k, seq(b)],
                             start=(k == 0), stop=(k == KD - 1))
                ins.then_inc(p_proj, 1)

            pe.wait_ge(s_wma, 16)
            for j in range(2 * KD):
                for k in range(KD):
                    ins = mm(mc_ps[:, j * NB:(j + 1) * NB], wm[:, k, j * P:(j + 1) * P], sc[:, k * NB:(k + 1) * NB],
                             start=(k == 0), stop=(k == KD - 1))
            ins.then_inc(p_mc, 1)
            pe.wait_ge(s_const, 1)
            transposed_x(0)
            pe.wait_ge(s_hT, 2 * KD)
            pe.wait_ge(s_winx, 16)
            project(0, PROJ[0])
            project(0, PROJ[1])
            transposed_x(1)
            pe.wait_ge(s_winz, 16)
            project(0, PROJ[2])
            project(0, PROJ[3])
            pe.wait_ge(s_hT, NB * 2 * KD)
            for t in range(NT):
                for k in range(KD):
                    ins = mm(dt_ps[:, t * NH:(t + 1) * NH], hT[:, k, tok(t)], win[:, k, DPROJ - NH:DPROJ],
                             start=(k == 0), stop=(k == KD - 1))
            ins.then_inc(p_dt, 1)
            pe.wait_ge(s_wmb, 16)
            for i in range(2):
                for k in range(KD):
                    ins = mm(bank[i][0:NB, :], sc[:, k * NB:(k + 1) * NB], wm[:, k, 2 * D + i * 2 * D:4 * D + i * 2 * D],
                             start=(k == 0), stop=(k == KD - 1))
            ins.then_inc(p_mt, 1)
            for b in range(NB):
                for q in PROJ[4:] if b == 0 else PROJ[:-1]:
                    project(b, q)

            def small(b):
                if b == 0:
                    pe.wait_ge(s_dt, 1)
                    pe.wait_ge(s_mraw, 2)
                else:
                    pe.wait_ge(s_ydx, TB - 2)
                n = TB * NH
                rhs = a[:, b * TB:(b + 1) * TB, :].rearrange("p t h -> p (t h)")
                for q, lhs in enumerate((le2[:, :], gt2[:, :], half[:, 0, :], half[:, 1, :])):
                    ins = mm(small_ps[:, q * n:(q + 1) * n], lhs, rhs, start=True, stop=True)
                ins.then_inc(p_small, 1)

            def prep(c):
                b = c // TB
                pe.wait_ge(s_xc, MC * (b + 1))
                if c == 0:
                    for n in range(NB * NPROJ - 4, NB * NPROJ - 2):
                        wait_read(n)
                if c >= 1:
                    pe.wait_ge(s_xdt, c)
                for m in range(MD):
                    ins = pe.transpose(bank[X][:, m * P:(m + 1) * P], xcT[:, m, tok(c)], ident[:, :])
                ins.then_inc(p_xtok, 1)
                if c >= 1:
                    pe.wait_ge(s_gm, c)
                if c >= 5:
                    pe.wait_ge(s_h2T, c - 4)
                pe.transpose(b_ps, xcT[:, MD, tok(c)], ident[:, :])
                for q in range(NQ):
                    cols = slice(c * P + q * Q, c * P + (q + 1) * Q)
                    ins = mm(g_ps[q * Q:(q + 1) * Q, :], xcT[:, MD, cols], xcT[:, MD + 1, cols], start=True, stop=True)
                ins.then_inc(p_bg, 1)
                if c == 0:
                    pe.wait_ge(s_split, 3)
                pe.wait_ge(s_alh, c + 1)
                pe.wait_ge(s_alr, c + 1)
                if c >= 1:
                    pe.wait_ge(s_l, c)
                mm(bank[SEG], gt2r[:, :], alh[:, c % 2, :, :].rearrange("p h l -> p (h l)"), start=True, stop=False)
                mm(bank[SEG], gt2r[:, :], alr[:, c % 2, :, :].rearrange("p h l -> p (h l)"),
                   start=False, stop=True).then_inc(p_seg, 1)

            def state_sum(c, q):
                pe.wait_ge(s_btok, c + 1)
                pe.wait_ge(s_xdd, c + 1)
                if c >= 1 or q:
                    pe.wait_ge(s_st, NQ * c + q)
                rows = slice(q * Q, (q + 1) * Q)
                mm(bank[ST], btok[rows, c % 2, :], xdd[rows, c % 2, :], start=True, stop=True).then_inc(p_st, 1)

            def off_diagonal(c):
                if c == 0:
                    for n in range(NB * NPROJ - 2, NB * NPROJ):
                        wait_read(n)
                else:
                    pe.wait_ge(s_yoffe, c)
                for q in range(NQ):
                    rows = slice(q * Q, (q + 1) * Q)
                    pe.wait_ge(s_st, NQ * c + q + 1)
                    ins = mm(bank[YOFF][rows, :], xcT[:, MD + 1, c * P + q * Q:c * P + (q + 1) * Q], st[:, c % 2, q, :],
                             start=True, stop=True)
                ins.then_inc(p_yoff, 1)

            def diagonal(c):
                pe.wait_ge(s_m, c + 1)
                if c >= 1:
                    pe.wait_ge(s_y, c)
                for q in range(NQ):
                    rows = slice(q * Q, (q + 1) * Q)
                    for h in range(NH):
                        ins = mm(bank[YD][rows, h * HD:(h + 1) * HD], lm[rows, c % 2, h, :],
                                 xdt[rows, c % 2, h * HD:(h + 1) * HD], start=True, stop=True)
                ins.then_inc(p_yd, 1)

            def y_transposed(c):
                pe.wait_ge(s_y, c + 1)
                if c >= 1:
                    pe.wait_ge(s_ydx, c)
                if c == TB - 2:
                    pe.wait_ge(s_dec, NB)
                for m in range(MD):
                    ins = pe.transpose(bank[YT][:, m * P:(m + 1) * P], y[:, c % 2, m * P:(m + 1) * P], ident[:, :])
                ins.then_inc(p_yT, 1)

            def out_project(c):
                b = c // TB
                pe.wait_ge(s_wog, MD * (b + 1))
                if c >= 1:
                    pe.wait_ge(s_x1, c)
                pe.wait_ge(s_yg, c + 1)
                for m in range(MD):
                    ins = mm(out_ps, yg[:, c % 2, m, :], wog[:, b, m, :], start=(m == 0), stop=(m == MD - 1))
                ins.then_inc(p_out, 1)

            def sum_squares(c):
                pe.wait_ge(s_sqs, c + 1)
                if c >= 1:
                    pe.wait_ge(s_x1, c)
                mm(ssq_ps[:, c:c + 1], sqs[:, c % 2, :], ones[:, 0:1], start=True, stop=True).then_inc(p_ssq, 1)

            def h2_transposed(t):
                pe.wait_ge(s_h2, t + 1)
                pe.wait_ge(s_gm, min(t + 5, NT))
                if t >= 1:
                    pe.wait_ge(s_h2T, t)
                if t > TB:
                    pe.wait_ge(s_sh, 1)
                for k in range(KD):
                    ins = pe.transpose(h2T_ps[:, k * P:(k + 1) * P], h2[:, t, k * P:(k + 1) * P], ident[:, :])
                ins.then_inc(p_h2T, 1)

            def logits(t):
                pe.wait_ge(s_h2T, t + 1)
                pe.wait_ge(s_gm, min(t + 6, NT))
                if t >= TB:
                    pe.wait_ge(s_sh, 1)
                for k in range(KD):
                    ins = mm(lg_ps[:, t * NE:(t + 1) * NE], h2T[:, k, tok(t)], pk[:, C_WG + k * NE:C_WG + (k + 1) * NE],
                             start=(k == 0), stop=(k == KD - 1))
                ins.then_inc(p_lg, 1)

            def positions(b):
                pe.wait_ge(s_oh, b + 1)
                pe.wait_ge(s_y, NT)
                if b == 1:
                    pe.wait_ge(s_dest, 1)
                n = TB * NE
                ps = pos_ps[:, b * n:(b + 1) * n]
                ts = slice(b * TB, (b + 1) * TB)
                mm(ps, le_b[:, :], oh[:, ts, :].rearrange("p t e -> p (t e)"), start=True, stop=False)
                mm(ps, ones_b[:, :], pre[:, ts, :].rearrange("p t e -> p (t e)"), start=False, stop=True).then_inc(p_pos, 1)

            def up_shared(u, q):
                _, b, j = UPS[u]
                if q == 0:
                    if u == 0:
                        pe.wait_ge(s_shw, 32)
                        pe.wait_ge(s_l, NT)
                        pe.wait_ge(s_st, NQ * NT)
                    if u == 1:
                        pe.wait_ge(s_yoffe, NT)
                        pe.wait_ge(s_ydx, NT)
                    if u >= 2:
                        pe.wait_ge(s_act, u - 1)
                    pe.wait_ge(s_h2T, TB * (b + 1))
                w = (shw1, shw3)[q]
                for k in range(KD):
                    ins = mm(bank[up_bank[u % 2][q]], w[:, k, HJ[j]:HJ[j] + P], h2T[:, k, seq(b)],
                             start=(k == 0), stop=(k == KD - 1))
                if q:
                    ins.then_inc(p_up, 1)

            def slots_transposed(e):
                pe.wait_ge(s_xg[e // 2], 16)
                if e >= 1:
                    pe.wait_ge(s_xdr, e)
                for k in range(KD):
                    ins = pe.transpose(xdT_ps[:, k * P:(k + 1) * P], xg[:, e, k * P:(k + 1) * P], ident[:, :])
                ins.then_inc(p_xdT, 1)

            def up_expert(e, q):
                u, r = NSH + e, e % 2
                if q == 0:
                    pe.wait_ge(s_xdr, e + 1)
                    pe.wait_ge(s_act, u - 1)
                pe.wait_ge(s_wr, 2 * e + q + 1)
                high, rest = ((w1h, w1r), (w3h, w3r))[q]
                ps = bank[up_bank[u % 2][q]][:, 0:HID]
                for k in range(KD):
                    mm(ps, xdh[:, r, k, :], high[:, e % 3, k, :], start=(k == 0), stop=False)
                    mm(ps, xdh[:, r, k, :], rest[:, e % 3, k, :], start=False, stop=False)
                    ins = mm(ps, xdr[:, r, k, :], high[:, e % 3, k, :], start=False, stop=(k == KD - 1))
                if q:
                    ins.then_inc(p_up, 1)

            def act_transposed(e):
                pe.wait_ge(s_act, NSH + e + 1)
                if e == NE - 1:
                    pe.wait_ge(s_xdr, NE)
                elif e >= 1:
                    pe.wait_ge(s_ar, e)
                for j in range(JH):
                    ins = pe.transpose(actT_ps[e][:, j * P:(j + 1) * P], eact[:, e % 2, HJ[j]:HJ[j] + P], ident[:, :])
                ins.then_inc(p_actT, 1)

            def down_expert(e):
                r = e % 2
                pe.wait_ge(s_ar, e + 1)
                pe.wait_ge(s_w2, e + 1)
                if e < EARLY:
                    pe.wait_ge(s_pre, e + 1)
                if e >= 2:
                    pe.wait_ge(s_oes, e - 1)
                ps = bank[down_bank[e % 2]][:, 0:D]
                for j in range(JH):
                    mm(ps, acth[:, r, j, :], w2h[:, e % 3, j, :], start=(j == 0), stop=False)
                    mm(ps, acth[:, r, j, :], w2r[:, e % 3, j, :], start=False, stop=False)
                    ins = mm(ps, actr[:, r, j, :], w2h[:, e % 3, j, :], start=False, stop=(j == JH - 1))
                ins.then_inc(p_dn, 1)

            def down_shared(t):
                pe.wait_ge(s_shg, NB)
                if t < EARLY:
                    pe.wait_ge(s_h2T, NT)
                    pe.wait_ge(s_sh, NB)
                    pe.wait_ge(s_dest, NB)
                    pe.wait_ge(s_act, JH)
                else:
                    pe.wait_ge(s_act, len(UPS))
                if t >= EARLY + 4:
                    pe.wait_ge(s_pre, t - 3)
                for j in range(JH):
                    ins = mm(bank[sd_bank[t]][:, 0:D], shact[:, j, tok(t)], shw2g[:, t // TB, j, :],
                             start=(j == 0), stop=(j == JH - 1))
                ins.then_inc(p_sd, 1)

            small(0)
            project(NB - 1, PROJ[-1])
            prep(0)
            prep(1)
            state_sum(0, 0)
            for c in range(NT):
                state_sum(c, 1)
                if 0 < c < NT - 1:
                    prep(c + 1)
                if c >= 1:
                    y_transposed(c - 1)
                if c >= 2:
                    out_project(c - 2)
                    sum_squares(c - 2)
                if c >= 4:
                    logits(c - 4)
                if c >= 3:
                    h2_transposed(c - 3)
                off_diagonal(c)
                if c + 1 < NT:
                    state_sum(c + 1, 0)
                diagonal(c)
                if c + 2 == TB:
                    small(1)
            out_project(NT - 2)
            y_transposed(NT - 1)
            sum_squares(NT - 2)
            up_shared(0, 0)
            up_shared(0, 1)
            logits(NT - 4)
            h2_transposed(NT - 3)
            out_project(NT - 1)
            sum_squares(NT - 1)
            logits(NT - 3)
            h2_transposed(NT - 2)
            positions(0)
            up_shared(1, 0)
            up_shared(1, 1)
            logits(NT - 2)
            h2_transposed(NT - 1)
            up_shared(2, 0)
            logits(NT - 1)
            up_shared(2, 1)
            positions(1)
            up_shared(3, 0)
            up_shared(3, 1)
            for u in range(4, NSH):
                for q in range(2):
                    up_shared(u, q)
            slots_transposed(0)
            for t in range(EARLY):
                down_shared(t)
            for e in range(NE):
                up_expert(e, 0)
                if e + 1 < NE:
                    slots_transposed(e + 1)
                up_expert(e, 1)
                if e >= 1:
                    act_transposed(e - 1)
                if e >= 2:
                    down_expert(e - 2)
            act_transposed(NE - 1)
            down_expert(NE - 2)
            down_expert(NE - 1)
            for t in range(EARLY, NT):
                down_shared(t)


def kernel(L0_attn_x, L0_attn_in_proj_w, L0_attn_conv_w, L0_attn_conv_b, L0_attn_A_log, L0_attn_D,
           L0_attn_dt_bias, L0_attn_norm_w, L0_attn_out_proj_w, L0_ffn_Wg, L0_ffn_W1, L0_ffn_W3,
           L0_ffn_W2, L0_ffn_sw1, L0_ffn_sw3, L0_ffn_sw2, L0_c, L0_wmod):
    import numpy as np
    import concourse.bacc as bacc
    from concourse.bass_utils import run_bass_kernel_spmd

    def blocks(m):
        m = np.asarray(m)
        m = m.reshape(-1, P, int(np.prod(m.shape[1:])) if m.ndim > 1 else 1)
        return m.transpose(1, 0, 2).reshape(P, -1)

    pack = np.concatenate([
        blocks(L0_attn_conv_w), blocks(L0_attn_conv_b), blocks(L0_attn_norm_w),
        blocks(np.repeat(np.asarray(L0_attn_D), HD)),
        np.broadcast_to(np.asarray(L0_attn_A_log), (P, NH)), np.broadcast_to(np.asarray(L0_attn_dt_bias), (P, NH)),
        blocks(np.asarray(L0_c).T), blocks(L0_ffn_Wg)], axis=1)
    ins = {
        "x": L0_attn_x, "in_w": np.asarray(L0_attn_in_proj_w).T, "out_w": np.asarray(L0_attn_out_proj_w).T,
        "pack": pack, "wmod": L0_wmod, "w1": L0_ffn_W1, "w3": L0_ffn_W3, "w2": L0_ffn_W2,
        "sw1": L0_ffn_sw1, "sw3": L0_ffn_sw3, "sw2": L0_ffn_sw2,
    }
    nc = bacc.Bacc("TRN2", target_bir_lowering=False, num_devices=1)
    arrays, aps = {}, {}
    for name, value in ins.items():
        value = np.ascontiguousarray(value)
        arrays[f"in_{name}"] = value
        aps[name] = nc.dram_tensor(f"in_{name}", value.shape, mybir.dt.from_np(value.dtype), kind="ExternalInput").ap()
    aps["out"] = nc.dram_tensor("out_x", (NB, L, D), mybir.dt.float32, kind="ExternalOutput").ap()
    build(nc, **aps)
    return run_bass_kernel_spmd(nc, [arrays], core_ids=[0]).results[0]["out_x"]
```
